# Optimizing a Trainium2 kernel written in Bass

```python
import numpy as np
import jax
import jax.numpy as jnp

def _softmax(x, axis=-1):
    return jax.nn.softmax(x, axis=axis)

def _gelu(x):
    return jax.nn.gelu(x, approximate=True)

def _silu(x):
    return jax.nn.silu(x)

def _sigmoid(x):
    return jax.nn.sigmoid(x)

def _layernorm(x, axis=-1, eps=1e-05):
    m = jnp.mean(x, axis=axis, keepdims=True)
    v = jnp.var(x, axis=axis, keepdims=True)
    return (x - m) / jnp.sqrt(v + eps)

def _scatter_add(tgt, idx, src, axis=0):
    return tgt.at[idx].add(src)

def _segment_sum(src, seg, n):
    return jax.ops.segment_sum(src, seg, n)
kernel_name = 'mk_gnn_ffn_d2_gnn_r8_57eb0d'

def setup_inputs(seed: int=0):
    np.random.seed(seed)
    _w = jnp.asarray

    def _rec_inputs():
        import jax
        import jax.numpy as jnp
        _gk = jax.random.key(seed)
        x = -6.415e-05 + 1 * jax.random.normal(jax.random.fold_in(_gk, 1), (1250, 1024), jnp.float32)
        _s = jax.random.randint(jax.random.fold_in(_gk, 2), (20000,), 0, 1250, jnp.int32)
        _d = jax.random.randint(jax.random.fold_in(_gk, 3), (20000,), 0, 1250, jnp.int32)
        _loop = jnp.arange(1250, dtype=jnp.int32)
        src = jnp.concatenate([_s, _d, _loop])
        dst = jnp.concatenate([_d, _s, _loop])
        _o = jnp.argsort(dst, stable=True)
        src = src[_o]
        dst = dst[_o]
        return (x, src, dst)
    x, src, dst = _rec_inputs()

    def _L0_gnn_setup():
        import jax, jax.numpy as jnp
        import numpy as np
        NEG_SLOPE = 0.1
        EPS = 1e-05
        key = jax.random.key(seed)
        k1, k2, k3, k4, k5 = jax.random.split(key, 5)
        N, E, DIN, DOUT = (1250, 20000, 1024, 1024)
        x = jax.random.normal(k1, (N, DIN), dtype=jnp.float32)
        W = jax.random.normal(k2, (DIN, DOUT), dtype=jnp.float32) * 0.02
        a = jax.random.normal(k3, (1, 2 * DOUT), dtype=jnp.float32) * 0.02
        src = jax.random.randint(k4, (E,), 0, N, dtype=jnp.int64)
        dst = jax.random.randint(k5, (E,), 0, N, dtype=jnp.int64)
        return {'x': x, 'W': W, 'a': a, 'src': src, 'dst': dst}
    _L0_gnn_all = _L0_gnn_setup()
    _L0_gnn_in = {k: v for k, v in _L0_gnn_all.items() if k in ('W', 'a')}
    del _L0_gnn_all

    def _L0_ffn_setup():
        import jax, jax.numpy as jnp
        import numpy as np
        D_MODEL = 1024
        MLP_DIM = 512
        N_EXPERTS = 8
        B, T = (4, 1024)
        key = jax.random.key(seed)
        ks = jax.random.split(key, 7)
        scale_in = (1.0 / D_MODEL) ** 0.5
        scale_out = (1.0 / MLP_DIM) ** 0.5
        bound_g = (1.0 / D_MODEL) ** 0.5
        w_gate = jax.random.uniform(ks[0], (D_MODEL, N_EXPERTS), minval=-bound_g, maxval=bound_g, dtype=jnp.float32)
        b_gate = jax.random.uniform(ks[1], (N_EXPERTS,), minval=-bound_g, maxval=bound_g, dtype=jnp.float32)
        W1 = jax.random.uniform(ks[2], (N_EXPERTS, D_MODEL, MLP_DIM), minval=-scale_in, maxval=scale_in, dtype=jnp.float32)
        b1 = jnp.zeros((N_EXPERTS, MLP_DIM), dtype=jnp.float32)
        W2 = jax.random.uniform(ks[3], (N_EXPERTS, MLP_DIM, D_MODEL), minval=-scale_out, maxval=scale_out, dtype=jnp.float32)
        b2 = jnp.zeros((N_EXPERTS, D_MODEL), dtype=jnp.float32)
        x = jax.random.normal(ks[4], (B, T, D_MODEL), dtype=jnp.float32)
        return {'x': x, 'w_gate': w_gate, 'b_gate': b_gate, 'W1': W1, 'b1': b1, 'W2': W2, 'b2': b2}
    _L0_ffn_all = _L0_ffn_setup()
    _L0_ffn_in = {k: v for k, v in _L0_ffn_all.items() if k in ('w_gate', 'b_gate', 'W1', 'b1', 'W2', 'b2')}
    del _L0_ffn_all

    def _L1_gnn_setup():
        import jax, jax.numpy as jnp
        import numpy as np
        N_NODES = 3125
        N_EDGES = 50000
        D = 1024

        def _sage_layer(h, edge_src, edge_dst, deg_inv, W_self, W_neigh, b):
            msg = h[edge_src]
            agg = jax.ops.segment_sum(msg, edge_dst, num_segments=h.shape[0])
            mean = agg * deg_inv[:, None]
            return h @ W_self + mean @ W_neigh + b
        key = jax.random.key(seed)
        ks = jax.random.split(key, 8)
        s = 1.0 / np.sqrt(D)
        return {'x': jax.random.normal(ks[0], (N_NODES, D), dtype=jnp.float32), 'edge_src': jax.random.randint(ks[1], (N_EDGES,), 0, N_NODES, dtype=jnp.int32), 'edge_dst': jax.random.randint(ks[2], (N_EDGES,), 0, N_NODES, dtype=jnp.int32), 'W_self0': jax.random.normal(ks[3], (D, D), dtype=jnp.float32) * s, 'W_neigh0': jax.random.normal(ks[4], (D, D), dtype=jnp.float32) * s, 'b0': jnp.zeros((D,), dtype=jnp.float32), 'W_self1': jax.random.normal(ks[5], (D, D), dtype=jnp.float32) * s, 'W_neigh1': jax.random.normal(ks[6], (D, D), dtype=jnp.float32) * s, 'b1': jnp.zeros((D,), dtype=jnp.float32)}
    _L1_gnn_all = _L1_gnn_setup()
    _L1_gnn_in = {k: v for k, v in _L1_gnn_all.items() if k in ('W_self0', 'W_neigh0', 'b0', 'W_self1', 'W_neigh1', 'b1')}
    del _L1_gnn_all

    def _L1_ffn_setup():
        import jax, jax.numpy as jnp
        import numpy as np
        BLOCK = 32
        W_BITS = 4
        ACT_BITS = 16

        def act_qdq(x):
            qmax = 2.0 ** (ACT_BITS - 1) - 1.0
            scale = jnp.maximum(jnp.max(jnp.abs(x)) / qmax, 1e-12)
            return jnp.clip(jnp.round(x / scale), -qmax - 1.0, qmax) * scale

        def fixed_qdq_u16(x):
            scale = 1.0 / 65536.0
            return jnp.clip(jnp.round(x / scale), 0.0, 65535.0) * scale

        def lpbq_dequant(w):
            O, I = w.shape
            qmax = 2.0 ** (W_BITS - 1) - 1.0
            wb = w.reshape(O, I // BLOCK, BLOCK)
            s = jnp.maximum(jnp.max(jnp.abs(wb), axis=-1, keepdims=True) / qmax, 1e-12)
            wq = jnp.clip(jnp.round(wb / s), -qmax - 1.0, qmax) * s
            return wq.reshape(O, I)
        key = jax.random.key(seed)
        k1, k2, k3, k4 = jax.random.split(key, 4)
        B, S, H, I = (2, 512, 1024, 384)
        x = jax.random.normal(k1, (B, S, H), jnp.float32)
        w_gate = jax.random.normal(k2, (I, H), jnp.float32) * 0.02
        w_up = jax.random.normal(k3, (I, H), jnp.float32) * 0.02
        w_down = jax.random.normal(k4, (H, I), jnp.float32) * 0.02
        return {'x': x, 'w_gate': w_gate, 'w_up': w_up, 'w_down': w_down}
    _L1_ffn_all = _L1_ffn_setup()
    _L1_ffn_in = {k: v for k, v in _L1_ffn_all.items() if k in ('w_gate', 'w_up', 'w_down')}
    del _L1_ffn_all
    return {'x': x, 'src': src, 'dst': dst, 'L0_gnn_W': _L0_gnn_in['W'], 'L0_gnn_a': _L0_gnn_in['a'], 'L0_ffn_w_gate': _L0_ffn_in['w_gate'], 'L0_ffn_b_gate': _L0_ffn_in['b_gate'], 'L0_ffn_W1': _L0_ffn_in['W1'], 'L0_ffn_b1': _L0_ffn_in['b1'], 'L0_ffn_W2': _L0_ffn_in['W2'], 'L0_ffn_b2': _L0_ffn_in['b2'], 'L1_gnn_W_self0': _L1_gnn_in['W_self0'], 'L1_gnn_W_neigh0': _L1_gnn_in['W_neigh0'], 'L1_gnn_b0': _L1_gnn_in['b0'], 'L1_gnn_W_self1': _L1_gnn_in['W_self1'], 'L1_gnn_W_neigh1': _L1_gnn_in['W_neigh1'], 'L1_gnn_b1': _L1_gnn_in['b1'], 'L1_ffn_w_gate': _L1_ffn_in['w_gate'], 'L1_ffn_w_up': _L1_ffn_in['w_up'], 'L1_ffn_w_down': _L1_ffn_in['w_down']}

def reference(x, src, dst, L0_gnn_W, L0_gnn_a, L0_ffn_w_gate, L0_ffn_b_gate, L0_ffn_W1, L0_ffn_b1, L0_ffn_W2, L0_ffn_b2, L1_gnn_W_self0, L1_gnn_W_neigh0, L1_gnn_b0, L1_gnn_W_self1, L1_gnn_W_neigh1, L1_gnn_b1, L1_ffn_w_gate, L1_ffn_w_up, L1_ffn_w_down):
    import jax
    import jax.numpy as jnp

    def _L0_gnn_ref(x, W, a, src, dst):
        import jax, jax.numpy as jnp
        import numpy as np
        NEG_SLOPE = 0.1
        EPS = 1e-05
        N = x.shape[0]
        d = W.shape[1]
        h = x @ W
        a_l, a_r = (a[0, :d], a[0, d:])
        al = h @ a_l
        ar = h @ a_r
        e = jnp.exp(-jax.nn.leaky_relu(al[src] + ar[dst], negative_slope=NEG_SLOPE))
        rowsum = jax.ops.segment_sum(e, src, num_segments=N)
        h_prime = jax.ops.segment_sum(e[:, None] * h[dst], src, num_segments=N)
        h_prime = h_prime / (rowsum[:, None] + EPS)
        return jax.nn.elu(h_prime)

    def _L0_ffn_ref(x, w_gate, b_gate, W1, b1, W2, b2):
        import jax, jax.numpy as jnp
        import numpy as np
        D_MODEL = 1024
        MLP_DIM = 512
        N_EXPERTS = 8
        B, T = (4, 1024)
        b, t, d = x.shape
        x_flat = x.reshape(b * t, d)
        logits = x_flat @ w_gate + b_gate
        probs = jax.nn.softmax(logits, axis=-1)
        route_p = jnp.max(probs, axis=-1)
        route_idx = jnp.argmax(probs, axis=-1)
        h = jnp.einsum('nd,edm->enm', x_flat, W1) + b1[:, None, :]
        h = jax.nn.relu(h)
        y = jnp.einsum('enm,emd->end', h, W2) + b2[:, None, :]
        n = b * t
        out = y[route_idx, jnp.arange(n)] * route_p[:, None]
        return out.reshape(b, t, d)

    def _L1_gnn_ref(x, edge_src, edge_dst, W_self0, W_neigh0, b0, W_self1, W_neigh1, b1):
        import jax, jax.numpy as jnp
        import numpy as np
        N_NODES = 3125
        N_EDGES = 50000
        D = 1024

        def _sage_layer(h, edge_src, edge_dst, deg_inv, W_self, W_neigh, b):
            msg = h[edge_src]
            agg = jax.ops.segment_sum(msg, edge_dst, num_segments=h.shape[0])
            mean = agg * deg_inv[:, None]
            return h @ W_self + mean @ W_neigh + b
        N = x.shape[0]
        deg = jax.ops.segment_sum(jnp.ones_like(edge_dst, dtype=x.dtype), edge_dst, num_segments=N)
        deg_inv = 1.0 / jnp.maximum(deg, 1.0)
        h = jax.nn.relu(_sage_layer(x, edge_src, edge_dst, deg_inv, W_self0, W_neigh0, b0))
        out = _sage_layer(h, edge_src, edge_dst, deg_inv, W_self1, W_neigh1, b1)
        return out

    def _L1_ffn_ref(x, w_gate, w_up, w_down):
        import jax, jax.numpy as jnp
        import numpy as np
        BLOCK = 32
        W_BITS = 4
        ACT_BITS = 16

        def act_qdq(x):
            qmax = 2.0 ** (ACT_BITS - 1) - 1.0
            scale = jnp.maximum(jnp.max(jnp.abs(x)) / qmax, 1e-12)
            return jnp.clip(jnp.round(x / scale), -qmax - 1.0, qmax) * scale

        def fixed_qdq_u16(x):
            scale = 1.0 / 65536.0
            return jnp.clip(jnp.round(x / scale), 0.0, 65535.0) * scale

        def lpbq_dequant(w):
            O, I = w.shape
            qmax = 2.0 ** (W_BITS - 1) - 1.0
            wb = w.reshape(O, I // BLOCK, BLOCK)
            s = jnp.maximum(jnp.max(jnp.abs(wb), axis=-1, keepdims=True) / qmax, 1e-12)
            wq = jnp.clip(jnp.round(wb / s), -qmax - 1.0, qmax) * s
            return wq.reshape(O, I)
        x = act_qdq(x)
        up = act_qdq(x @ lpbq_dequant(w_up).T)
        gate = act_qdq(x @ lpbq_dequant(w_gate).T)
        sig = fixed_qdq_u16(jax.nn.sigmoid(gate))
        gate = act_qdq(gate * sig)
        o = act_qdq(gate * up)
        return o @ lpbq_dequant(w_down).T
    x = x + _L0_gnn_ref(_layernorm(x, axis=-1), L0_gnn_W, L0_gnn_a, src, dst)
    x = x + _L0_ffn_ref(_layernorm(x, axis=-1)[None], L0_ffn_w_gate, L0_ffn_b_gate, L0_ffn_W1, L0_ffn_b1, L0_ffn_W2, L0_ffn_b2)[0]
    x = x + _L1_gnn_ref(_layernorm(x, axis=-1), src, dst, L1_gnn_W_self0, L1_gnn_W_neigh0, L1_gnn_b0, L1_gnn_W_self1, L1_gnn_W_neigh1, L1_gnn_b1)
    x = x + _L1_ffn_ref(_layernorm(x, axis=-1)[None], L1_ffn_w_gate, L1_ffn_w_up, L1_ffn_w_down)[0]
    return x

_drawn_inputs = setup_inputs


def setup_inputs(seed=0):
    import zlib

    import numpy as np

    out = dict(_drawn_inputs(seed))
    spreads = {'L0_ffn_b1': (0.0, 0.791),
     'L0_ffn_b2': (0.0, 0.315),
     'L1_gnn_b0': (0.0, 0.1),
     'L1_gnn_b1': (0.0, 0.1)}
    factors = {'L0_ffn_b_gate': 6.734}
    for name, (base, spread) in spreads.items():
        noise = np.random.default_rng([zlib.crc32(name.encode()), seed]).standard_normal(out[name].shape)
        drawn = base * np.exp(spread * noise) if base else spread * noise
        out[name] = jnp.asarray(drawn.astype(out[name].dtype))
    for name, factor in factors.items():
        out[name] = (out[name] * factor).astype(out[name].dtype)
    return out
```

```python
from contextlib import ExitStack

import concourse.bass as bass
from concourse import mybir

ALU = mybir.AluOpType
ACT = mybir.ActivationFunctionType
AX = mybir.AxisListType.X
F32 = mybir.dt.float32
F16 = mybir.dt.float16
I32 = mybir.dt.int32
ds = bass.ds

P = 128
HALF = 512
CHUNKS = 4
UNIT = CHUNKS * P
ROUND = 12582912.0
LN_EPS = 1e-5
GAT_EPS = 1e-5
NEG_SLOPE = 0.1
W_BLOCK = 32


def flat(ap):
    return ap.rearrange("p a d -> p (a d)")


def tiles(n):
    return -(-n // P)


def makers(ctx, nc, phase):
    def sb(name, shape, dt=F32):
        return ctx.enter_context(nc.sbuf_tensor(f"{phase}_{name}", shape, dt))

    def ps(name, shape):
        return ctx.enter_context(nc.psum_tensor(f"{phase}_{name}", shape, F32))

    def sem(name):
        return ctx.enter_context(nc.semaphore(f"{phase}_{name}"))
    return sb, ps, sem


def layer_stats(dve, g, link, halves, stats, mean_var):
    link(dve.bn_stats(stats[:, 0:6], halves[0]), g.always)
    link(dve.bn_stats(stats[:, 6:12], halves[1]), g.always)
    link(dve.bn_aggr(mean_var, stats))


def wait_apart(eng, always, sem, value):
    if isinstance(value, int):
        eng.wait_ge(always, 1)
        eng.wait_ge(sem, value)
        return
    with eng.register() as reg:
        eng.reg_mov(reg, value)
        eng.wait_ge(always, 1)
        eng.wait_ge(sem, reg)


def chain(eng, sem, t, per, start=0):
    k = [0]

    def link(ins, always=None):
        k[0] += 1
        assert k[0] <= per
        ins.then_inc(sem, 1)
        if always is None:
            eng.wait_ge(sem, t * per + k[0] + start)
        else:
            wait_apart(eng, always, sem, t * per + k[0] + start)
    return link


def pipeline(eng, count, stages):
    deepest = max(lag for _, lag in stages)
    first, end = deepest + deepest % 2, count - count % 2

    def step(s):
        for stage, lag in stages:
            t = s - lag
            if 0 <= t < count:
                stage(t, t % 2, t // 2)

    if first >= end:
        for s in range(count + deepest):
            step(s)
        return
    for s in range(first):
        step(s)
    with eng.Fori(first // 2, end // 2) as i:
        for r in (0, 1):
            for stage, lag in stages:
                stage(2 * i + (r - lag), (r - lag) % 2, i + (r - lag) // 2)
    for s in range(end, count + deepest):
        step(s)


class Shared:
    pass


def graph_phase(nc, g, src, dst, x, w_gnn, x_arrived, w_arrived):
    T, N, NP, E = g.T, g.N, g.NP, g.E
    full, rest = E // UNIT, E % UNIT
    units = full + (rest > 0)
    with ExitStack() as ctx:
        sb, ps, sem = makers(ctx, nc, "graph")

        src_i = sb("src_i", [P, UNIT], I32)
        dst_i = sb("dst_i", [P, UNIT], I32)
        tile_i = sb("tile_i", [P, UNIT], I32)
        src_f = sb("src_f", [P, UNIT], F32)
        dst_f = sb("dst_f", [P, UNIT], F32)
        tile_f = sb("tile_f", [P, UNIT], F32)
        hit = sb("hit", [P, UNIT], F32)
        present = sb("present", [P, T], F32)
        from_start = sb("from_start", [T, units], F32)
        from_end = sb("from_end", [T, units], F32)
        edge_of = sb("edge_of", [T, 2], F32)
        bounds = sb("bounds", [T, 2], F32)
        bounds_i = sb("bounds_i", [1, 2 * T], I32)
        col_i = sb("col_i", [P, NP], I32)
        row_i = sb("row_i", [P, 1], I32)
        node_i = sb("node_i", [P, T], I32)
        src_t = sb("src_t", [P, CHUNKS, units], F32)
        dst_t = sb("dst_t", [P, CHUNKS, units], F32)
        zeros16 = sb("zeros16", [P, P], F16)
        iota16 = sb("iota16", [P, NP], F16)
        dst_hot = sb("dst_hot", [P, CHUNKS, P], F16)
        src_hot = sb("src_hot", [P, CHUNKS, N], F16)
        counts = sb("counts", [P, 2, NP], F32)
        turned = sb("turned", [P, 2, T, P], F32)
        deg_t = sb("deg_t", [P, 2], F32)
        acc = ps("acc", [P, 2, 3 * HALF])
        ps_turn = ps("ps_turn", [P, 2, HALF])

        s_iota = sem("s_iota")
        s_fill = sem("s_fill")
        s_src = sem("s_src")
        s_dst = sem("s_dst")
        s_rest = sem("s_rest")
        s_const = sem("s_const")
        s_prep = sem("s_prep")
        s_present = sem("s_present")
        s_present_t = sem("s_present_t")
        s_edges_t = sem("s_edges_t")
        s_edges_kept = sem("s_edges_kept")
        s_bounds = sem("s_bounds")
        s_bounds_t = sem("s_bounds_t")
        s_ready = sem("s_ready")
        s_hot = sem("s_hot")
        s_hot_free = sem("s_hot_free")
        s_acc = sem("s_acc")
        s_counts = sem("s_counts")
        s_turn = sem("s_turn")
        s_turn_free = sem("s_turn_free")
        s_counts_out = [sem("s_counts_out0"), sem("s_counts_out1")]
        s_turned_out = [sem("s_turned_out0"), sem("s_turned_out1")]
        block = ctx.enter_context(nc.Block())

        @block.gpsimd
        def _(pool):
            pool.iota(col_i[:], [[1, NP]], base=0, channel_multiplier=0).then_inc(s_iota, 1)
            pool.iota(row_i[:], [[1, 1]], base=0, channel_multiplier=1).then_inc(s_iota, 1)
            pool.iota(node_i[:], [[P, T]], base=0, channel_multiplier=1).then_inc(s_iota, 1)
            pool.iota(g.token_id[:], [[P, T]], base=0, channel_multiplier=1).then_inc(s_iota, 1)

        @block.sync
        def _(sp):
            sp.wait_ge(s_fill, 2)
            sp.dma_start(dst_i[0:full, :], dst[0:full * UNIT].rearrange("(a b) -> a b", b=UNIT)).then_inc(s_dst, 16)
            sp.dma_start(src_i[0:full, :], src[0:full * UNIT].rearrange("(a b) -> a b", b=UNIT)).then_inc(s_src, 16)
            if rest:
                sp.dma_start(dst_i[full:full + 1, 0:rest], dst[full * UNIT:E].rearrange("(a b) -> a b", a=1)).then_inc(s_rest, 16)
                sp.dma_start(src_i[full:full + 1, 0:rest], src[full * UNIT:E].rearrange("(a b) -> a b", a=1)).then_inc(s_rest, 16)
            whole = N // P
            sp.dma_start(g.big1[:, 0:whole, :], x[0:whole * P, :].rearrange("(t p) d -> p t d", p=P)).then_inc(x_arrived, 16)
            sp.wait_ge(s_fill, 3)
            sp.dma_start(g.big1[0:N - whole * P, whole, :], x[whole * P:N, :]).then_inc(x_arrived, 16)
            sp.dma_start(g.w_gnn[:], w_gnn.rearrange("(k p) n -> p k n", p=P)).then_inc(w_arrived, 16)

            def store(t, p, m):
                sp.wait_ge(s_counts, t + 3)
                sp.dma_start(g.counts_dram[ds(t, 1)].rearrange("a p n -> (a p) n"), counts[:, p, :]).then_inc(s_counts_out[p], 16)
                sp.wait_ge(s_turn_free, 3 * t + 5)
                sp.dma_start(g.turned_dram[ds(t, 1)].rearrange("a p n -> (a p) n"),
                             turned[:, p].rearrange("p j c -> p (j c)")).then_inc(s_turned_out[p], 16)
            pipeline(sp, T, [(store, 0)])
            for p in (0, 1):
                sp.wait_ge(s_counts_out[p], 16 * (T // 2) + 16)
                sp.wait_ge(s_turned_out[p], 16 * (T // 2) + 16)

        @block.vector
        def _(dve):
            dve.sem_inc(g.always, 1)
            dve.memset(src_i[:], -1).then_inc(s_fill, 1)
            dve.memset(dst_i[:], -1).then_inc(s_fill, 1)
            dve.memset(g.big1[:, T - 1, :], 0.0).then_inc(s_fill, 1)
            dve.memset(zeros16[:], 0.0).then_inc(s_const, 1)
            dve.memset(g.ones[:], 1.0).then_inc(s_const, 1)
            dve.memset(g.eps[:], LN_EPS).then_inc(s_const, 1)
            dve.memset(counts[:, :, N:NP], 0.0).then_inc(s_const, 1)
            dve.wait_ge(s_iota, 4)
            dve.tensor_copy(g.col_id[:], col_i[:, 0:P]).then_inc(s_const, 1)
            dve.tensor_copy(iota16[:], col_i[:]).then_inc(s_const, 1)
            dve.tensor_copy(g.row_id[:], row_i[:]).then_inc(s_const, 1)
            dve.tensor_copy(g.node_id[:], node_i[:]).then_inc(s_const, 1)
            dve.wait_ge(s_const, 8)
            dve.tensor_scalar(g.ident[:], g.col_id[:], g.row_id[:, 0:1], None, ALU.is_equal).then_inc(s_const, 1)
            dve.tensor_scalar(g.before[:], g.col_id[:], g.row_id[:, 0:1], None, ALU.is_gt).then_inc(s_const, 1)
            dve.tensor_scalar(g.exists[:], g.node_id[:], float(N), None, ALU.is_lt).then_inc(s_const, 1)
            dve.wait_ge(s_dst, 16)
            dve.wait_ge(s_src, 16)
            if rest:
                dve.wait_ge(s_rest, 32)
            link = chain(dve, s_prep, 0, 5 + 2 * T)
            link(dve.tensor_copy(src_f[:], src_i[:]))
            link(dve.tensor_copy(dst_f[:], dst_i[:]))
            link(dve.tensor_scalar(tile_i[:], dst_i[:], 7, None, ALU.arith_shift_right))
            link(dve.tensor_copy(tile_f[:], tile_i[:]))
            for t in range(T):
                link(dve.tensor_scalar(hit[:], tile_f[:], float(t), None, ALU.is_equal))
                link(dve.tensor_reduce(present[:, t:t + 1], hit[:], AX, ALU.max))
            dve.sem_inc(s_present, 1)
            dve.wait_ge(s_edges_t, 2)
            dve.tensor_copy(src_t[:], acc[:, 0, 0:CHUNKS * P].rearrange("p (c u) -> p c u", c=CHUNKS)[:, :, 0:units]).then_inc(s_edges_kept, 1)
            dve.tensor_copy(dst_t[:], acc[:, 0, HALF:HALF + CHUNKS * P].rearrange("p (c u) -> p c u", c=CHUNKS)[:, :, 0:units]).then_inc(s_edges_kept, 1)
            dve.wait_ge(s_present_t, 1)
            link = chain(dve, s_bounds, 0, 9)
            here = ps_turn[0:T, 0, 0:units]
            link(dve.tensor_scalar(from_start[:], g.col_id[0:T, 0:units], 1.0, None, ALU.add))
            link(dve.tensor_scalar(from_end[:], g.col_id[0:T, 0:units], -1.0, float(units), ALU.mult, ALU.add))
            link(dve.tensor_tensor(from_start[:], from_start[:], here, ALU.mult))
            link(dve.tensor_tensor(from_end[:], from_end[:], here, ALU.mult))
            link(dve.tensor_reduce(edge_of[:, 0:1], from_end[:], AX, ALU.max))
            link(dve.tensor_reduce(edge_of[:, 1:2], from_start[:], AX, ALU.max))
            link(dve.tensor_scalar(bounds[:, 0:1], edge_of[:, 0:1], -1.0, float(units), ALU.mult, ALU.add))
            link(dve.tensor_scalar(bounds[:, 0:1], bounds[:, 0:1], float(units - 1), None, ALU.min))
            link(dve.tensor_scalar(bounds[:, 1:2], edge_of[:, 1:2], -1.0, bounds[:, 0:1], ALU.add, ALU.max))
            dve.wait_ge(s_bounds_t, 1)
            dve.tensor_copy(bounds_i[0:1, 0:T], ps_turn[0:1, 1, 0:T]).then_inc(s_ready, 1)
            dve.tensor_scalar(bounds_i[0:1, T:2 * T], ps_turn[0:1, 1, T:2 * T], 1.0, None, ALU.add).then_inc(s_ready, 1)
            dve.wait_ge(s_ready, 2)
            dve.wait_ge(s_edges_kept, 2)
            made = dve.alloc_register("hot_made")
            dve.reg_mov(made, 0)

            def hot(t, p, m):
                lo = dve.value_load(bounds_i[0:1, ds(t, 1)], min_val=0, max_val=units - 1)
                hi = dve.value_load(bounds_i[0:1, ds(t + T, 1)], min_val=1, max_val=units)
                with dve.Fori(lo, hi) as u:
                    for c in range(CHUNKS):
                        dve.reg_add(made, made, 1)
                        dve.wait_ge(s_hot_free, made)
                        dve.tensor_scalar(dst_hot[:, c, :], iota16[:, ds(t * P, P)], dst_t[:, c, ds(u, 1)], None, ALU.is_equal)
                        dve.tensor_scalar(src_hot[:, c, :], iota16[:, 0:N], src_t[:, c, ds(u, 1)], None, ALU.is_equal).then_inc(s_hot, 1)
            pipeline(dve, T, [(hot, 0)])
            dve.free_register(made)

        @block.tensor
        def _(pe):
            pe.sem_inc(s_hot_free, CHUNKS)
            pe.wait_ge(s_const, 11)
            pe.wait_ge(s_present, 1)
            pe.wait_ge(s_prep, 4 + 2 * T)
            for c in range(CHUNKS):
                last = pe.transpose(acc[:, 0, c * P:(c + 1) * P], src_f[:, c * P:(c + 1) * P], g.ident[:])
            last.then_inc(s_edges_t, 1)
            for c in range(CHUNKS):
                last = pe.transpose(acc[:, 0, HALF + c * P:HALF + (c + 1) * P], dst_f[:, c * P:(c + 1) * P], g.ident[:])
            last.then_inc(s_edges_t, 1)
            pe.transpose(ps_turn[0:T, 0, 0:P], present[:], g.ident[:]).then_inc(s_present_t, 1)
            pe.wait_ge(s_bounds, 9)
            pe.transpose(ps_turn[0:1, 1, 0:T], bounds[:, 0:1], g.ident[0:T, 0:T])
            pe.transpose(ps_turn[0:1, 1, T:2 * T], bounds[:, 1:2], g.ident[0:T, 0:T]).then_inc(s_bounds_t, 1)
            pe.wait_ge(s_ready, 2)
            pe.wait_ge(s_edges_kept, 2)
            done = pe.alloc_register("hot_done")
            pe.reg_mov(done, 0)
            spans = [(a, min(a + HALF, N)) for a in range(0, N, HALF)]

            def count(t, p, m):
                lo = pe.value_load(bounds_i[0:1, ds(t, 1)], min_val=0, max_val=units - 1)
                hi = pe.value_load(bounds_i[0:1, ds(t + T, 1)], min_val=1, max_val=units)
                pe.wait_ge(s_counts, t + 1)
                for a, b in spans:
                    pe.matmul(acc[:, p, a:b], zeros16[:], iota16[:, 0:b - a], start=True, stop=False, skip_group_check=True)
                with pe.Fori(lo, hi) as u:
                    for c in range(CHUNKS):
                        pe.reg_add(done, done, 1)
                        pe.wait_ge(s_hot, done)
                        for a, b in spans:
                            last = pe.matmul(acc[:, p, a:b], dst_hot[:, c, :], src_hot[:, c, a:b], start=False, stop=False, skip_group_check=True)
                        last.then_inc(s_hot_free, 1)
                for a, b in spans:
                    last = pe.matmul(acc[:, p, a:a + 2], zeros16[:], iota16[:, 0:2], start=False, stop=True, skip_group_check=True)
                last.then_inc(s_acc, 1)

            def turn(t, p, m):
                pe.wait_ge(s_counts, t + 3)
                for r in range(3):
                    pe.wait_ge(s_turn_free, t * 3 + r + 1)
                    for j in range(4 * r, min(4 * r + 4, T)):
                        last = pe.transpose(ps_turn[:, (p + r) % 2, (j % 4) * P:(j % 4 + 1) * P], counts[:, p, j * P:(j + 1) * P], g.ident[:])
                    last.then_inc(s_turn, 1)
            pipeline(pe, T, [(count, 0), (turn, 1)])
            pe.free_register(done)

        @block.scalar
        def _(act):
            act.sem_inc(s_counts, 2)
            act.sem_inc(s_turn_free, 2)
            for p in (0, 1):
                act.sem_inc(s_counts_out[p], 16)
                act.sem_inc(s_turned_out[p], 16)
            act.wait_ge(s_const, 11)

            def take(t, p, m):
                act.wait_ge(s_acc, t + 1)
                act.wait_ge(s_counts_out[p], m * 16 + 16)
                act.activation(counts[:, p, 0:N], acc[:, p, 0:N], ACT.Copy, accum_out=deg_t[:, p:p + 1]).then_inc(s_counts, 1)
                act.wait_ge(s_counts, t + 3)
                act.activation(g.deg[:, ds(t, 1)], deg_t[:, p:p + 1], ACT.Copy)

            def take_turned(t, p, m):
                act.wait_ge(s_turned_out[p], m * 16 + 16)
                for r in range(3):
                    act.wait_ge(s_turn, t * 3 + r + 1)
                    n = min(4, T - 4 * r)
                    ins = act.activation(turned[:, p, 4 * r:4 * r + n, :], ps_turn[:, (p + r) % 2, 0:n * P].rearrange("p (j c) -> p j c", c=P), ACT.Copy)
                    ins.then_inc(s_turn_free, 1)
            pipeline(act, T, [(take, 0), (take_turned, 1)])


def hidden_phase(nc, g, a, x_arrived, w_arrived):
    T, K, D = g.T, g.K, g.D
    with ExitStack() as ctx:
        sb, ps, sem = makers(ctx, nc, "hidden")

        a_rows = sb("a_rows", [P, 2 * D])
        stats = sb("stats", [P, 2, 12])
        mean_var = sb("mean_var", [P, 2, 2])
        std = sb("std", [P, 2])
        rstd = sb("rstd", [P, 2])
        normed = sb("normed", [P, 2, D])
        normed_t = sb("normed_t", [P, 2, K, P])
        product = sb("product", [P, D])
        side = sb("side", [P, 2, 2])
        ps_turn = ps("ps_turn", [P, D])
        ps_h = ps("ps_h", [P, 2, D])

        s_a = sem("s_a")
        s_stats = sem("s_stats")
        s_std = sem("s_std")
        s_normed = sem("s_normed")
        s_turn = sem("s_turn")
        s_turned = sem("s_turned")
        s_h = sem("s_h")
        s_h_taken = sem("s_h_taken")
        s_sides = sem("s_sides")
        s_half_free = sem("s_half_free")
        block = ctx.enter_context(nc.Block())

        @block.sync
        def _(sp):
            sp.dma_start(a_rows[:], a.broadcast_to([P, 2 * D])).then_inc(s_a, 16)

        @block.vector
        def _(dve):
            dve.sem_inc(s_normed, 2)
            dve.wait_ge(x_arrived, 32)

            def norm(t, p, m):
                link = chain(dve, s_stats, t, 3)
                layer_stats(dve, g, link, [flat(g.big1[:, ds(t, 1), a:a + HALF]) for a in (0, HALF)], stats[:, p, :], mean_var[:, p, :])
                dve.wait_ge(s_std, 2 * t + 1)
                dve.reciprocal(rstd[:, p:p + 1], std[:, p:p + 1]).then_inc(s_std, 1)
                dve.wait_ge(s_std, 2 * t + 2)
                dve.tensor_scalar(normed[:, p, :], g.big1[:, ds(t, 1), :].rearrange("p a d -> p (a d)"), mean_var[:, p, 0:1],
                                  rstd[:, p:p + 1], ALU.subtract, ALU.mult).then_inc(s_normed, 1)

            def sides(t, p, m):
                dve.wait_ge(s_h_taken, t + 1)
                link = chain(dve, s_sides, t, 3)
                for k in (0, 1):
                    link(dve.tensor_tensor_reduce(product[:], ps_h[:, p, :], a_rows[:, k * D:(k + 1) * D], 1.0, 0.0,
                                                  ALU.mult, ALU.add, side[:, p, k:k + 1]))
                dve.sem_inc(s_half_free, 1)
                link(dve.tensor_copy(flat(g.sides[:, ds(t, 1), :]), side[:, p, :]), g.always)
            dve.wait_ge(s_a, 16)
            pipeline(dve, T, [(norm, 0), (sides, 2)])

        @block.scalar
        def _(act):
            def root(t, p, m):
                act.wait_ge(s_stats, t * 3 + 3)
                act.activation(std[:, p:p + 1], mean_var[:, p, 1:2], ACT.Sqrt, bias=g.eps[:, 0:1]).then_inc(s_std, 1)

            def take_turned(t, p, m):
                act.wait_ge(s_turn, t + 1)
                act.activation(normed_t[:, p].rearrange("p k c -> p (k c)"), ps_turn[:], ACT.Copy).then_inc(s_turned, 1)

            def take_h(t, p, m):
                act.wait_ge(s_h, t + 1)
                act.activation(g.big2[:, ds(t, 1), :].rearrange("p a d -> p (a d)"), ps_h[:, p, :], ACT.Copy).then_inc(s_h_taken, 1)
            pipeline(act, T, [(root, 0), (take_turned, 1), (take_h, 2)])

        @block.tensor
        def _(pe):
            pe.sem_inc(s_turned, 1)
            pe.sem_inc(s_half_free, 2)
            pe.wait_ge(w_arrived, 16)

            def turn(t, p, m):
                pe.wait_ge(s_normed, t + 3)
                pe.wait_ge(s_turned, t + 1)
                for k in range(K):
                    last = pe.transpose(ps_turn[:, k * P:(k + 1) * P], normed[:, p, k * P:(k + 1) * P], g.ident[:])
                last.then_inc(s_turn, 1)

            def multiply(t, p, m):
                pe.wait_ge(s_turned, t + 2)
                pe.wait_ge(s_half_free, t + 1)
                for a in range(0, D, HALF):
                    for k in range(K):
                        last = pe.matmul(ps_h[:, p, a:a + HALF], normed_t[:, p, k, :], g.w_gnn[:, k, a:a + HALF], start=(k == 0), stop=(k == K - 1))
                last.then_inc(s_h, 1)
            pipeline(pe, T, [(turn, 0), (multiply, 1)])


def attention_phase(nc, g, w_gate, b_gate):
    T, K, D, X = g.T, g.K, g.D, g.X
    with ExitStack() as ctx:
        sb, ps, sem = makers(ctx, nc, "attend")
        gate_w = sb("gate_w", [P, K, X])
        gate_b = sb("gate_b", [P, X])
        order = sb("order", [P, X])
        counts = sb("counts", [P, 2, T, P])
        diag = sb("diag", [P, 2, P])
        sums = sb("sums", [P, T, P])
        leaky = sb("leaky", [P, 2, T, P])
        weights = sb("weights", [P, 2, T, P])
        rowsum = sb("rowsum", [P, 2])
        inv = sb("inv", [P, 2])
        below = sb("below", [P, D])
        above = sb("above", [P, D])
        elu = sb("elu", [P, D])
        stats = sb("stats", [P, 12])
        mean_var = sb("mean_var", [P, 2])
        std = sb("std", [P, 1])
        rstd = sb("rstd", [P, 1])
        normed = sb("normed", [P, 2, D])
        normed_t = sb("normed_t", [P, K, P])
        logits = sb("logits", [P, X])
        neg_max = sb("neg_max", [P, 1])
        exps = sb("exps", [P, X])
        exp_sum = sb("exp_sum", [P, 1])
        exp_max = sb("exp_max", [P, 1])
        ranked = sb("ranked", [P, X])
        best = sb("best", [P, 1])
        ps_h = ps("ps_h", [P, 2, D])
        ps_turn = ps("ps_turn", [P, D])
        ps_left = ps("ps_left", [P, P])
        ps_rowsum = ps("ps_rowsum", [P, 2])

        s_gate = sem("s_gate")
        s_order = sem("s_order")
        s_counts = [sem("s_counts0"), sem("s_counts1")]
        s_diag = sem("s_diag")
        s_left = sem("s_left")
        s_sums = sem("s_sums")
        s_exp = sem("s_exp")
        s_weights = sem("s_weights")
        s_attended = sem("s_attended")
        s_inv = sem("s_inv")
        s_below = sem("s_below")
        s_elu_parts = sem("s_elu_parts")
        s_x1 = sem("s_x1")
        s_stats = sem("s_stats")
        s_std = sem("s_std")
        s_normed = sem("s_normed")
        s_stored = [sem("s_stored0"), sem("s_stored1")]
        s_turn = sem("s_turn")
        s_turned = sem("s_turned")
        s_logits = sem("s_logits")
        s_logits_read = sem("s_logits_read")
        s_exps = sem("s_exps")
        s_route = sem("s_route")
        block = ctx.enter_context(nc.Block())

        @block.sync
        def _(sp):
            sp.dma_start(gate_w[:], w_gate.rearrange("(k p) e -> p k e", p=P)).then_inc(s_gate, 16)
            sp.dma_start(gate_b[:], b_gate.rearrange("(a e) -> a e", a=1).broadcast_to([P, X])).then_inc(s_gate, 16)

            def load(t, p, m):
                sp.wait_ge(s_weights, t + 1)
                sp.dma_start(counts[:, p], g.counts_dram.rearrange("j p n -> p j n")[:, :, ds(t * P, P)]).then_inc(s_counts[p], 16)

            def store(t, p, m):
                sp.wait_ge(s_normed, t + 1)
                sp.dma_start(g.normed_dram[ds(t * P, P), :], normed[:, p, :]).then_inc(s_stored[p], 16)
            pipeline(sp, T, [(load, 0), (store, 3)])
            for p in (0, 1):
                sp.wait_ge(s_stored[p], 16 * (T // 2) + 16)

        @block.vector
        def _(dve):
            dve.sem_inc(s_weights, 2)
            dve.sem_inc(s_inv, 2)
            dve.sem_inc(s_sums, 2)
            dve.sem_inc(s_logits_read, 2)
            dve.wait_ge(s_gate, 32)
            dve.tensor_scalar(order[:], g.col_id[:, 0:X], -1.0, float(X), ALU.mult, ALU.add).then_inc(s_order, 1)
            dve.wait_ge(s_order, 1)

            def weigh(t, p, m):
                dve.wait_ge(s_exp, t + 1)
                dve.wait_ge(s_counts[p], m * 16 + 16)
                dve.tensor_tensor(weights[:, p], leaky[:, p], counts[:, p], ALU.mult).then_inc(s_weights, 1)

            def add_sides(t, p, m):
                dve.wait_ge(s_left, t + 1)
                left = ps_left[:].unsqueeze(1).broadcast_to([P, T, P])
                right = g.sides[:, :, 1:2].broadcast_to([P, T, P])
                link = chain(dve, s_sums, t, 2, 2)
                link(dve.tensor_tensor(sums[:], left, right, ALU.add))
                link(dve.scalar_tensor_tensor(leaky[:, p], sums[:], NEG_SLOPE, sums[:], ALU.mult, ALU.max))

            def diagonal(t, p, m):
                dve.tensor_scalar(diag[:, p, :], g.ident[:], g.sides[:, ds(t, 1), 0:1].rearrange("p a b -> p (a b)"), None, ALU.mult).then_inc(s_diag, 1)

            def finish(t, p, m):
                dve.wait_ge(s_attended, t + 1)
                link = chain(dve, s_inv, t, 2, 2)
                link(dve.tensor_scalar(rowsum[:, p:p + 1], ps_rowsum[:, 0:1], GAT_EPS, None, ALU.add))
                link(dve.reciprocal(inv[:, p:p + 1], rowsum[:, p:p + 1]))
                dve.tensor_scalar(below[:], ps_h[:, p, :], inv[:, p:p + 1], 0.0, ALU.mult, ALU.min).then_inc(s_below, 1)
                dve.wait_ge(s_elu_parts, 2 * t + 2)
                link = chain(dve, s_x1, t, 2)
                x1 = flat(g.big1[:, ds(t, 1), :])
                link(dve.scalar_tensor_tensor(elu[:], below[:], -1.0, above[:], ALU.add, ALU.add))
                link(dve.tensor_tensor(x1, x1, elu[:], ALU.add), g.always)
                link = chain(dve, s_stats, t, 3)
                layer_stats(dve, g, link, [flat(g.big1[:, ds(t, 1), a:a + HALF]) for a in (0, HALF)], stats[:], mean_var[:])
                dve.wait_ge(s_std, 2 * t + 1)
                dve.reciprocal(rstd[:], std[:]).then_inc(s_std, 1)
                dve.wait_ge(s_std, 2 * t + 2)
                dve.wait_ge(s_stored[p], m * 16 + 16)
                dve.wait_ge(s_turn, t + 1)
                dve.tensor_scalar(normed[:, p, :], x1, mean_var[:, 0:1], rstd[:, 0:1], ALU.subtract, ALU.mult).then_inc(s_normed, 1)

            def route(t, p, m):
                dve.wait_ge(s_logits, t + 1)
                link = chain(dve, s_logits_read, t, 2, 2)
                link(dve.tensor_tensor(logits[:], ps_turn[:, 0:X], gate_b[:], ALU.add))
                link(dve.tensor_reduce(neg_max[:], logits[:], AX, ALU.max, negate=True))
                dve.wait_ge(s_exps, t + 1)
                link = chain(dve, s_route, t, 5)
                link(dve.reciprocal(g.route_p[:, ds(t, 1)], exp_sum[:]))
                link(dve.tensor_reduce(exp_max[:], exps[:], AX, ALU.max))
                link(dve.scalar_tensor_tensor(ranked[:], exps[:], exp_max[:, 0:1], order[:], ALU.is_ge, ALU.mult))
                link(dve.tensor_reduce(best[:], ranked[:], AX, ALU.max))
                link(dve.tensor_scalar(flat(g.chosen[:, ds(t, 1), :]), ranked[:], best[:, 0:1], None, ALU.is_equal))
            pipeline(dve, T, [(weigh, 2), (add_sides, 1), (diagonal, 0), (route, 4), (finish, 3)])

        @block.scalar
        def _(act):
            for p in (0, 1):
                act.sem_inc(s_stored[p], 16)

            def exponent(t, p, m):
                act.wait_ge(s_sums, 2 * t + 4)
                act.activation(leaky[:, p], leaky[:, p], ACT.Exp, scale=-1.0).then_inc(s_exp, 1)

            def elu_parts(t, p, m):
                act.wait_ge(s_below, t + 1)
                act.activation(above[:], ps_h[:, p, :], ACT.Relu, scale=inv[:, p:p + 1]).then_inc(s_elu_parts, 1)
                act.activation(below[:], below[:], ACT.Exp).then_inc(s_elu_parts, 1)

            def root(t, p, m):
                act.wait_ge(s_stats, 3 * t + 3)
                act.activation(std[:], mean_var[:, 1:2], ACT.Sqrt, bias=g.eps[:, 0:1]).then_inc(s_std, 1)

            def take_turned(t, p, m):
                act.wait_ge(s_turn, t + 3)
                act.activation(normed_t[:].rearrange("p k c -> p (k c)"), ps_turn[:], ACT.Copy).then_inc(s_turned, 1)

            def exps_of(t, p, m):
                act.wait_ge(s_logits_read, 2 * t + 4)
                act.activation(exps[:], logits[:], ACT.Exp, bias=neg_max[:, 0:1], accum_out=exp_sum[:]).then_inc(s_exps, 1)
            pipeline(act, T, [(exponent, 1), (exps_of, 4), (elu_parts, 3), (root, 3), (take_turned, 3)])

        @block.tensor
        def _(pe):
            pe.sem_inc(s_turn, 2)
            pe.wait_ge(s_gate, 32)

            def attend(t, p, m):
                pe.wait_ge(s_weights, t + 3)
                for j in range(T):
                    for a in range(0, D, HALF):
                        pe.matmul(ps_h[:, p, a:a + HALF], weights[:, p, j, :], g.big2[:, j, a:a + HALF], start=(j == 0), stop=(j == T - 1))
                pe.wait_ge(s_inv, 2 * t + 2)
                for j in range(T):
                    last = pe.matmul(ps_rowsum[:, 0:1], weights[:, p, j, :], g.ones[:, 0:1], start=(j == 0), stop=(j == T - 1))
                last.then_inc(s_attended, 1)

            def left(t, p, m):
                pe.wait_ge(s_diag, t + 1)
                pe.wait_ge(s_sums, 2 * t + 2)
                pe.matmul(ps_left[:], g.ones[:], diag[:, p, :], start=True, stop=True).then_inc(s_left, 1)

            def turn(t, p, m):
                pe.wait_ge(s_normed, t + 1)
                pe.wait_ge(s_logits_read, 2 * t + 2)
                for k in range(K):
                    last = pe.transpose(ps_turn[:, k * P:(k + 1) * P], normed[:, p, k * P:(k + 1) * P], g.ident[:])
                last.then_inc(s_turn, 1)

            def gate(t, p, m):
                pe.wait_ge(s_turned, t + 1)
                for k in range(K):
                    last = pe.matmul(ps_turn[:, 0:X], normed_t[:, k, :], gate_w[:, k, :], start=(k == 0), stop=(k == K - 1))
                last.then_inc(s_logits, 1)
            pipeline(pe, T, [(gate, 4), (attend, 2), (left, 0), (turn, 3)])


def expert_phase(nc, g, w1, b1, w2, b2):
    T, K, D, X, NP, S = g.T, g.K, g.D, g.X, g.NP, g.slot_tiles
    M = w1.shape[2]
    KM = M // P
    with ExitStack() as ctx:
        sb, ps, sem = makers(ctx, nc, "expert")
        rank = sb("rank", [P, T, X])
        total = sb("total", [P, T, X])
        base = sb("base", [P, T + 1, X])
        tiles_i = sb("tiles_i", [P, X], I32)
        n_tiles = sb("n_tiles", [P, X])
        ends = sb("ends", [P, X])
        first_slot = sb("first_slot", [P, X])
        place = sb("place", [P, T, X])
        slot_f = sb("slot_f", [P, T])
        passed = sb("passed", [1, S, X])
        expert_f = sb("expert_f", [1, S])
        expert_i = sb("expert_i", [1, S], I32)
        no_token = sb("no_token", [S, P], I32)
        tokens = sb("tokens", [P, S], I32)
        token_col = sb("token_col", [P, 2], I32)
        w1_t = sb("w1_t", [P, 2, K, M])
        w2_t = sb("w2_t", [P, 2, KM, D])
        b1_t = sb("b1_t", [1, 2, M])
        b2_t = sb("b2_t", [1, 2, D])
        rows = sb("rows", [P, 2, D])
        rows_t = sb("rows_t", [P, 2, K, P])
        hidden = sb("hidden", [P, 2, M])
        hidden_t = sb("hidden_t", [P, KM, P])
        y = sb("y", [P, 2, D])
        ps_turn = ps("ps_turn", [P, D])
        ps_hidden = ps("ps_hidden", [P, M])
        ps_hidden_t = ps("ps_hidden_t", [P, M])
        ps_y = ps("ps_y", [P, 2, D])

        s_sums = sem("s_sums")
        s_place = sem("s_place")
        s_clear = sem("s_clear")
        s_cleared = sem("s_cleared")
        s_scatter = sem("s_scatter")
        s_tokens = sem("s_tokens")
        s_token_col = sem("s_token_col")
        s_rows = [sem("s_rows0"), sem("s_rows1")]
        s_w1 = [sem("s_w1_0"), sem("s_w1_1")]
        s_w2 = [sem("s_w2_0"), sem("s_w2_1")]
        s_turn = sem("s_turn")
        s_turned = sem("s_turned")
        s_hidden = sem("s_hidden")
        s_relu = sem("s_relu")
        s_hidden_t = sem("s_hidden_t")
        s_hidden_taken = sem("s_hidden_taken")
        s_y = sem("s_y")
        s_y_taken = sem("s_y_taken")
        s_y_out = [sem("s_y_out0"), sem("s_y_out1")]
        block = ctx.enter_context(nc.Block())
        PLACE = 16 + T + X

        @block.sync
        def _(sp):
            sp.wait_ge(s_clear, 1)
            sp.dma_start(g.slot_token_dram.rearrange("(s p) a -> s (p a)", p=P), no_token[:]).then_inc(s_cleared, 16)
            sp.wait_ge(s_scatter, 16 * T)
            sp.dma_start(tokens[:], g.slot_token_dram.rearrange("(s p) a -> p (s a)", p=P), allow_slow_non_contiguous=True).then_inc(s_tokens, 16)
            sp.sem_inc(s_hidden, 2)
            sp.sem_inc(s_y, 2)

            def load(t, p, m):
                expert = sp.value_load(expert_i[0:1, ds(t, 1)], min_val=0, max_val=X - 1)
                sp.wait_ge(s_hidden, t + 1)
                sp.dma_start(w1_t[:, p], w1[ds(expert, 1)].rearrange("a (k p) m -> p (a k) m", p=P)).then_inc(s_w1[p], 16)
                sp.dma_start(b1_t[0:1, p, :], b1[ds(expert, 1), :]).then_inc(s_w1[p], 16)
                sp.wait_ge(s_y, t + 1)
                sp.dma_start(w2_t[:, p], w2[ds(expert, 1)].rearrange("a (k p) d -> p (a k) d", p=P)).then_inc(s_w2[p], 16)
                sp.dma_start(b2_t[0:1, p, :], b2[ds(expert, 1), :]).then_inc(s_w2[p], 16)
            pipeline(sp, S, [(load, 0)])

        @block.gpsimd
        def _(pool):
            pool.memset(no_token[:], 0).then_inc(s_clear, 1)
            pool.wait_ge(s_place, PLACE)
            pool.wait_ge(s_cleared, 16)
            for t in range(T):
                pool.indirect_dma_start(g.slot_token_dram, bass.IndirectOffsetOnAxis(g.slot[:, t:t + 1], 0),
                                        g.token_id[:, t:t + 1], None).then_inc(s_scatter, 16)
            pool.wait_ge(s_tokens, 16)

            def gather(t, p, m):
                pool.wait_ge(s_turn, t + 1)
                pool.tensor_copy(token_col[:, p:p + 1], tokens[:, ds(t, 1)]).then_inc(s_token_col, 1)
                wait_apart(pool, g.always, s_token_col, t + 1)
                pool.indirect_dma_start(rows[:, p, :], None, g.normed_dram, bass.IndirectOffsetOnAxis(token_col[:, p:p + 1], 0)).then_inc(s_rows[p], 16)
            pipeline(pool, S, [(gather, 0)])

        @block.vector
        def _(dve):
            dve.wait_ge(s_sums, 1)
            link = chain(dve, s_place, 0, PLACE)
            chosen = g.chosen[:].rearrange("p t e -> p (t e)")
            link(dve.tensor_copy(rank[:].rearrange("p t e -> p (t e)"), ps_turn[:, 0:T * X]))
            link(dve.tensor_copy(total[:].rearrange("p t e -> p (t e)"), ps_turn[:, HALF:HALF + T * X]))
            link(dve.memset(base[:, 0, :], 0.0))
            for t in range(T):
                link(dve.tensor_tensor(base[:, t + 1, :], base[:, t, :], total[:, t, :], ALU.add))
            link(dve.tensor_scalar(tiles_i[:], base[:, T, :], float(P - 1), None, ALU.add))
            link(dve.tensor_scalar(tiles_i[:], tiles_i[:], 7, None, ALU.arith_shift_right))
            link(dve.tensor_copy(n_tiles[:], tiles_i[:]))
            link(dve.tensor_copy(ends[:, 0:1], n_tiles[:, 0:1]))
            for e in range(1, X):
                link(dve.tensor_tensor(ends[:, e:e + 1], ends[:, e - 1:e], n_tiles[:, e:e + 1], ALU.add))
            link(dve.tensor_tensor(first_slot[:], ends[:], n_tiles[:], ALU.subtract))
            link(dve.tensor_scalar(first_slot[:], first_slot[:], float(P), None, ALU.mult))
            link(dve.tensor_tensor(place[:], rank[:], base[:, 0:T, :], ALU.add))
            link(dve.tensor_tensor(place[:], place[:], first_slot[:].unsqueeze(1).broadcast_to([P, T, X]), ALU.add))
            link(dve.tensor_tensor(place[:], place[:], g.chosen[:], ALU.mult))
            link(dve.tensor_reduce(slot_f[:], place[:], AX, ALU.add))
            link(dve.tensor_copy(g.slot[:], slot_f[:]))
            link(dve.tensor_tensor(passed[:], ends[0:1, :].unsqueeze(1).broadcast_to([1, S, X]),
                                   g.col_id[0:1, 0:S].unsqueeze(2).broadcast_to([1, S, X]), ALU.is_le))
            link(dve.tensor_reduce(expert_f[:], passed[:], AX, ALU.add))
            link(dve.tensor_scalar(expert_i[:], expert_f[:], float(X - 1), None, ALU.min))

            def take_hidden_t(t, p, m):
                dve.wait_ge(s_hidden_t, t + 1)
                dve.tensor_copy(hidden_t[:].rearrange("p k c -> p (k c)"), ps_hidden_t[:]).then_inc(s_hidden_taken, 1)

            def take_y(t, p, m):
                dve.wait_ge(s_y, t + 3)
                dve.wait_ge(s_y_out[p], m * 16 + 16)
                dve.tensor_copy(y[:, p, :], ps_y[:, p, :]).then_inc(s_y_taken, 1)
            pipeline(dve, S, [(take_hidden_t, 0), (take_y, 1)])

        @block.scalar
        def _(act):
            for p in (0, 1):
                act.sem_inc(s_y_out[p], 16)

            def take_turned(t, p, m):
                act.wait_ge(s_turn, t + 3)
                act.wait_ge(s_hidden, t + 1)
                act.activation(rows_t[:, p].rearrange("p k c -> p (k c)"), ps_turn[:], ACT.Copy).then_inc(s_turned, 1)

            def relu(t, p, m):
                act.wait_ge(s_hidden, t + 3)
                act.activation(hidden[:, p, :], ps_hidden[:], ACT.Relu).then_inc(s_relu, 1)

            def store(t, p, m):
                act.wait_ge(s_y_taken, t + 3)
                act.dma_start(g.y_dram[ds(t * P, P), :], y[:, p, :]).then_inc(s_y_out[p], 16)
            pipeline(act, S, [(take_turned, 0), (relu, 1), (store, 3)])
            act.wait_ge(s_y_out[0], 16 * ((S + 1) // 2) + 16)
            act.wait_ge(s_y_out[1], 16 * (S // 2) + 16)

        @block.tensor
        def _(pe):
            chosen = g.chosen[:].rearrange("p t e -> p (t e)")
            pe.matmul(ps_turn[:, 0:T * X], g.before[:], chosen, start=True, stop=True)
            pe.matmul(ps_turn[:, HALF:HALF + T * X], g.ones[:], chosen, start=True, stop=True).then_inc(s_sums, 1)
            pe.wait_ge(s_place, 2)
            pe.sem_inc(s_turn, 2)
            pe.sem_inc(s_turned, 1)

            def turn(t, p, m):
                pe.wait_ge(s_rows[p], m * 16 + 16)
                pe.wait_ge(s_turned, t + 1)
                for k in range(K):
                    last = pe.transpose(ps_turn[:, k * P:(k + 1) * P], rows[:, p, k * P:(k + 1) * P], g.ident[:])
                last.then_inc(s_turn, 1)

            def first(t, p, m):
                pe.wait_ge(s_w1[p], m * 32 + 32)
                pe.wait_ge(s_turned, t + 2)
                pe.wait_ge(s_relu, t + 1)
                pe.matmul(ps_hidden[:], g.ones[0:1, :], b1_t[0:1, p, :], start=True, stop=False)
                for k in range(K):
                    last = pe.matmul(ps_hidden[:], rows_t[:, p, k, :], w1_t[:, p, k, :], start=False, stop=(k == K - 1))
                last.then_inc(s_hidden, 1)

            def turn_hidden(t, p, m):
                pe.wait_ge(s_relu, t + 2)
                pe.wait_ge(s_hidden_taken, t + 1)
                for k in range(KM):
                    last = pe.transpose(ps_hidden_t[:, k * P:(k + 1) * P], hidden[:, p, k * P:(k + 1) * P], g.ident[:])
                last.then_inc(s_hidden_t, 1)

            def second(t, p, m):
                pe.wait_ge(s_w2[p], m * 32 + 32)
                pe.wait_ge(s_hidden_taken, t + 2)
                pe.wait_ge(s_y_taken, t + 1)
                for a in range(0, D, HALF):
                    pe.matmul(ps_y[:, p, a:a + HALF], g.ones[0:1, :], b2_t[0:1, p, a:a + HALF], start=True, stop=False)
                    for k in range(KM):
                        last = pe.matmul(ps_y[:, p, a:a + HALF], hidden_t[:, k, :], w2_t[:, p, k, a:a + HALF], start=False, stop=(k == KM - 1))
                last.then_inc(s_y, 1)
            pe.sem_inc(s_relu, 1)
            pe.sem_inc(s_hidden_taken, 1)
            pe.sem_inc(s_y_taken, 2)
            pipeline(pe, S, [(turn_hidden, 2), (turn, 0), (first, 1), (second, 2)])


def combine_phase(nc, g):
    T, D = g.T, g.D
    with ExitStack() as ctx:
        sb, ps, sem = makers(ctx, nc, "combine")
        slot_col = sb("slot_col", [P, 2], I32)
        y = sb("y", [P, 2, D])
        stats = sb("stats", [P, 12])
        mean_var = sb("mean_var", [P, 2])
        std = sb("std", [P, 1])
        rstd = sb("rstd", [P, 1])
        s_col = sem("s_col")
        s_y = [sem("s_y0"), sem("s_y1")]
        s_added = sem("s_added")
        s_stats = sem("s_stats")
        s_std = sem("s_std")
        s_normed = sem("s_normed")
        s_out = sem("s_out")
        block = ctx.enter_context(nc.Block())

        @block.gpsimd
        def _(pool):
            def gather(t, p, m):
                pool.wait_ge(s_added, t + 1)
                pool.tensor_copy(slot_col[:, p:p + 1], g.slot[:, ds(t, 1)]).then_inc(s_col, 1)
                wait_apart(pool, g.always, s_col, t + 1)
                pool.indirect_dma_start(y[:, p, :], None, g.y_dram, bass.IndirectOffsetOnAxis(slot_col[:, p:p + 1], 0)).then_inc(s_y[p], 16)
            pipeline(pool, T, [(gather, 0)])

        @block.vector
        def _(dve):
            dve.sem_inc(s_added, 2)

            def add(t, p, m):
                x2 = flat(g.big1[:, ds(t, 1), :])
                dve.wait_ge(s_y[p], m * 16 + 16)
                dve.scalar_tensor_tensor(x2, y[:, p, :], g.route_p[:, ds(t, 1)], x2, ALU.mult, ALU.add).then_inc(s_added, 1)
                wait_apart(dve, g.always, s_added, t + 3)
                link = chain(dve, s_stats, t, 3)
                layer_stats(dve, g, link, [flat(g.big1[:, ds(t, 1), a:a + HALF]) for a in (0, HALF)], stats[:], mean_var[:])
                dve.wait_ge(s_std, 2 * t + 1)
                dve.reciprocal(rstd[:], std[:]).then_inc(s_std, 1)
                dve.wait_ge(s_std, 2 * t + 2)
                dve.tensor_scalar(flat(g.big2[:, ds(t, 1), :]), x2, mean_var[:, 0:1], rstd[:, 0:1], ALU.subtract, ALU.mult).then_inc(s_normed, 1)
                dve.wait_ge(s_normed, t + 1)
            pipeline(dve, T, [(add, 0)])
            link = chain(dve, s_normed, 0, 2, T)
            link(dve.tensor_scalar(g.deg[:], g.deg[:], 1.0, None, ALU.max))
            link(dve.reciprocal(g.deg[:], g.deg[:]))

        @block.scalar
        def _(act):
            def root(t, p, m):
                act.wait_ge(s_stats, 3 * t + 3)
                act.activation(std[:], mean_var[:, 1:2], ACT.Sqrt, bias=g.eps[:, 0:1]).then_inc(s_std, 1)
            pipeline(act, T, [(root, 0)])

        @block.sync
        def _(sp):
            sp.wait_ge(s_added, T + 2)
            sp.dma_start(g.x_dram.rearrange("t p d -> p t d"), g.big1[:]).then_inc(s_out, 16)
            sp.wait_ge(s_out, 16)


def sage_phase(nc, g, phase, nodes, out, w_self, w_neigh, bias, last):
    T, K, D = g.T, g.K, g.D
    with ExitStack() as ctx:
        sb, ps, sem = makers(ctx, nc, phase)
        w = sb("w", [P, 2, K, D])
        bias_rows = sb("bias_rows", [P, D])
        counts = sb("counts", [P, 2, T, P])
        own = sb("own", [P, D])
        mean = sb("mean", [P, D])
        own_t = sb("own_t", [P, 2, K, P])
        mean_t = sb("mean_t", [P, 2, K, P])
        biased = sb("biased", [P, D])
        x2 = sb("x2", [P, 2, D]) if last else None
        stats = sb("stats", [P, 12])
        std = sb("std", [P, 1])
        rstd = sb("rstd", [P, 1])
        ps_sum = ps("ps_sum", [P, D])
        ps_own = ps("ps_own", [P, D])
        ps_mean = ps("ps_mean", [P, D])
        ps_out = ps("ps_out", [P, D])

        s_w = sem("s_w")
        s_bias = sem("s_bias")
        s_counts = [sem("s_counts0"), sem("s_counts1")]
        s_x2 = [sem("s_x2_0"), sem("s_x2_1")]
        s_own = sem("s_own")
        s_summed = sem("s_summed")
        s_mean = sem("s_mean")
        s_own_turn = sem("s_own_turn")
        s_own_t = sem("s_own_t")
        s_mean_turn = sem("s_mean_turn")
        s_mean_t = sem("s_mean_t")
        s_out = sem("s_out")
        s_biased = sem("s_biased")
        s_x3 = sem("s_x3")
        s_relu = sem("s_relu")
        s_std = sem("s_std")
        s_largest = sem("s_largest")
        block = ctx.enter_context(nc.Block())

        @block.sync
        def _(sp):
            sp.sem_inc(s_summed, 2)
            sp.sem_inc(s_x3, 2)
            sp.dma_start(bias_rows[:], bias.rearrange("(a d) -> a d", a=1).broadcast_to([P, D])).then_inc(s_bias, 16)

            def load(t, p, m):
                sp.wait_ge(s_summed, t + 1)
                sp.dma_start(counts[:, p].rearrange("p j c -> p (j c)"), g.turned_dram[ds(t, 1)].rearrange("a p n -> (a p) n")).then_inc(s_counts[p], 16)
                if last:
                    sp.wait_ge(s_x3, t + 1)
                    sp.dma_start(x2[:, p, :], g.x_dram[ds(t, 1)].rearrange("a p d -> (a p) d")).then_inc(s_x2[p], 16)
            load(0, 0, 0)
            sp.dma_start(w[:, 0], w_self.rearrange("(k p) n -> p k n", p=P)).then_inc(s_w, 16)
            load(1, 1, 0)
            sp.dma_start(w[:, 1], w_neigh.rearrange("(k p) n -> p k n", p=P)).then_inc(s_w, 16)
            with sp.Fori(1, T // 2) as i:
                for p in (0, 1):
                    load(2 * i + p, p, i)

        @block.vector
        def _(dve):
            dve.wait_ge(s_bias, 16)

            def copy_own(t, p, m):
                dve.wait_ge(s_own_turn, t + 1)
                dve.tensor_copy(own[:], flat(nodes[:, ds(t, 1), :])).then_inc(s_own, 1)

            def take_sum(t, p, m):
                dve.wait_ge(s_summed, t + 3)
                dve.wait_ge(s_mean_turn, t + 1)
                dve.tensor_scalar(mean[:], ps_sum[:], g.deg[:, ds(t, 1)], None, ALU.mult).then_inc(s_mean, 1)

            def take_mean(t, p, m):
                dve.wait_ge(s_mean_turn, t + 2)
                dve.tensor_copy(mean_t[:, p].rearrange("p k c -> p (k c)"), ps_mean[:]).then_inc(s_mean_t, 1)

            def finish(t, p, m):
                dve.wait_ge(s_out, t + 1)
                if not last:
                    dve.wait_ge(s_relu, t + 1)
                dve.tensor_tensor(biased[:], ps_out[:], bias_rows[:], ALU.add).then_inc(s_biased, 1)
                if last:
                    x3 = flat(out[:, ds(t, 1), :])
                    dve.wait_ge(s_biased, t + 2)
                    dve.wait_ge(s_x2[p], 16 * m + 16)
                    dve.tensor_tensor(x3, biased[:], x2[:, p, :], ALU.add).then_inc(s_x3, 1)
                    wait_apart(dve, g.always, s_x3, t + 3)
                    link = chain(dve, s_largest, t, 8)
                    layer_stats(dve, g, link, [flat(out[:, ds(t, 1), a:a + HALF]) for a in (0, HALF)], stats[:], g.mean_var[:])
                    dve.wait_ge(s_std, t + 1)
                    link(dve.reciprocal(rstd[:], std[:]))
                    link(dve.tensor_copy(g.means[:, ds(t, 1)], g.mean_var[:, 0:1]))
                    link(dve.tensor_copy(g.rstds[:, ds(t, 1)], rstd[:]))
                    link(dve.tensor_scalar(biased[:], x3, g.mean_var[:, 0:1], rstd[:, 0:1], ALU.subtract, ALU.mult))
                    link(dve.tensor_reduce(g.largest[:, ds(t, 1)], biased[:], AX, ALU.max, apply_absolute_value=True))
            pipeline(dve, T, [(copy_own, 0), (take_sum, 0), (take_mean, 1), (finish, 2)])

        @block.scalar
        def _(act):
            def take_own(t, p, m):
                act.wait_ge(s_own_turn, t + 2)
                act.activation(own_t[:, p].rearrange("p k c -> p (k c)"), ps_own[:], ACT.Copy).then_inc(s_own_t, 1)

            def relu(t, p, m):
                act.wait_ge(s_biased, t + 2)
                act.activation(flat(out[:, ds(t, 1), :]), biased[:], ACT.Relu).then_inc(s_relu, 1)

            def root(t, p, m):
                act.wait_ge(s_largest, 8 * t + 3)
                act.activation(std[:], g.mean_var[:, 1:2], ACT.Sqrt, bias=g.eps[:, 0:1]).then_inc(s_std, 1)
            pipeline(act, T, [(take_own, 1), (root if last else relu, 2)])

        @block.tensor
        def _(pe):
            pe.sem_inc(s_own_turn, 1)
            pe.sem_inc(s_mean_turn, 1)
            pe.sem_inc(s_biased, 1)
            pe.sem_inc(s_relu, 1)
            pe.sem_inc(s_mean, 1)
            pe.sem_inc(s_own_t, 1)
            pe.sem_inc(s_mean_t, 1)

            def add_up(t, p, m):
                pe.wait_ge(s_counts[p], 16 * m + 16)
                pe.wait_ge(s_mean, t + 1)
                for j in range(T):
                    for a in range(0, D, HALF):
                        last_mm = pe.matmul(ps_sum[:, a:a + HALF], counts[:, p, j, :], nodes[:, j, a:a + HALF], start=(j == 0), stop=(j == T - 1))
                last_mm.then_inc(s_summed, 1)

            def turn(t, p, m):
                pe.wait_ge(s_own, t + 1)
                pe.wait_ge(s_own_t, t + 1)
                for k in range(K):
                    last_mm = pe.transpose(ps_own[:, k * P:(k + 1) * P], own[:, k * P:(k + 1) * P], g.ident[:])
                last_mm.then_inc(s_own_turn, 1)
                pe.wait_ge(s_mean, t + 2)
                pe.wait_ge(s_mean_t, t + 1)
                for k in range(K):
                    last_mm = pe.transpose(ps_mean[:, k * P:(k + 1) * P], mean[:, k * P:(k + 1) * P], g.ident[:])
                last_mm.then_inc(s_mean_turn, 1)

            def linear(t, p, m):
                pe.wait_ge(s_own_t, t + 2)
                pe.wait_ge(s_mean_t, t + 2)
                pe.wait_ge(s_biased, t + 1)
                for a in range(0, D, HALF):
                    for side, turned in ((0, own_t), (1, mean_t)):
                        for k in range(K):
                            last_mm = pe.matmul(ps_out[:, a:a + HALF], turned[:, p, k, :], w[:, side, k, a:a + HALF],
                                                start=(side == 0 and k == 0), stop=(side == 1 and k == K - 1))
                last_mm.then_inc(s_out, 1)
            pe.wait_ge(s_w, 32)
            pipeline(pe, T, [(add_up, 0), (turn, 1), (linear, 2)])


def quantised(dve, link, out, value, inv_scale, scale, low, high):
    link(dve.tensor_scalar(out, value, inv_scale, ROUND, ALU.mult, ALU.add))
    link(dve.tensor_scalar(out, out, ROUND, high, ALU.subtract, ALU.min))
    link(dve.tensor_scalar(out, out, low, scale, ALU.max, ALU.mult))


def feed_forward_phase(nc, g, w_gate, w_up, w_down, out):
    T, K, D, N = g.T, g.K, g.D, g.N
    I = w_gate.shape[0]
    KI = I // P
    A_MAX, W_MAX, S_MAX = 32767.0, 7.0, 65535.0
    with ExitStack() as ctx:
        sb, ps, sem = makers(ctx, nc, "ffn")
        gate_rows = sb("gate_rows", [P, 2 * KI, D])
        down_rows = sb("down_rows", [P, D // P, I])
        gate_up_t = sb("gate_up_t", [P, K, 2 * I])
        down_t = sb("down_t", [P, KI, D])
        w_scale = sb("w_scale", [P, D // W_BLOCK])
        w_inv = sb("w_inv", [P, D // W_BLOCK])
        gate_up = g.big1[:].rearrange("p t d -> p (t d)")[:, 0:T * 2 * I].rearrange("p (t s i) -> p s t i", t=T, s=2)
        normed = sb("normed", [P, D])
        normed_t = sb("normed_t", [P, K, P])
        largest = sb("largest", [P, 3, T])
        widest = sb("widest", [P, 1])
        top = sb("top", [1, 1])
        scales = sb("scales", [P, 5, 2])
        sig = sb("sig", [P, T, I])
        o_t = sb("o_t", [P, KI, P])
        result = sb("result", [P, 2, D])
        ps_turn = ps("ps_turn", [P, D])
        ps_gate_up = ps("ps_gate_up", [P, 2, HALF])
        ps_scale = ps("ps_scale", [P, HALF])
        ps_down = ps("ps_down", [P, D])

        s_rows = sem("s_rows")
        s_down_rows = sem("s_down_rows")
        s_w = sem("s_w")
        s_w_turn = sem("s_w_turn")
        s_w_taken = sem("s_w_taken")
        s_widest = sem("s_widest")
        s_level = sem("s_level")
        s_scaled = sem("s_scaled")
        s_quant = sem("s_quant")
        s_normed = sem("s_normed")
        s_turn = sem("s_turn")
        s_turned = sem("s_turned")
        s_gate_up = sem("s_gate_up")
        s_gate_up_kept = sem("s_gate_up_kept")
        s_largest = sem("s_largest")
        s_all = sem("s_all")
        s_sig = sem("s_sig")
        s_o = sem("s_o")
        s_o_turn = sem("s_o_turn")
        s_o_t = sem("s_o_t")
        s_down = sem("s_down")
        s_result = sem("s_result")
        s_out = [sem("s_out0"), sem("s_out1")]
        block = ctx.enter_context(nc.Block())
        ROWS = [(gate_rows, i, D, gate_up_t, K, i * P) for i in range(2 * KI)]
        ROWS += [(down_rows, i, I, down_t, KI, i * P) for i in range(D // P)]
        W_STEPS = 8

        @block.sync
        def _(sp):
            sp.dma_start(gate_rows[:, 0:KI], w_gate.rearrange("(o p) i -> p o i", p=P)).then_inc(s_rows, 16)
            sp.dma_start(gate_rows[:, KI:2 * KI], w_up.rearrange("(o p) i -> p o i", p=P)).then_inc(s_rows, 16)
            sp.dma_start(down_rows[:], w_down.rearrange("(o p) i -> p o i", p=P)).then_inc(s_down_rows, 16)

            for p in (0, 1):
                sp.sem_inc(s_out[p], 16)

            def store(t, p, m):
                sp.wait_ge(s_result, t + 2)
                if isinstance(t, int) and (t + 1) * P > N:
                    sp.dma_start(out[t * P:N, :], result[0:N - t * P, p, :]).then_inc(s_out[p], 16)
                else:
                    sp.dma_start(out[ds(t * P, P), :], result[:, p, :]).then_inc(s_out[p], 16)
            with sp.Fori(0, T // 2 - 1) as i:
                for p in (0, 1):
                    store(2 * i + p, p, i)
            store(T - 2, 0, T // 2 - 1)
            store(T - 1, 1, T // 2 - 1)
            for p in (0, 1):
                sp.wait_ge(s_out[p], 16 * (T // 2) + 16)

        @block.vector
        def _(dve):
            dve.wait_ge(s_rows, 32)
            for n, (rows, i, width, _, _, _) in enumerate(ROWS):
                if n == 2 * KI:
                    dve.wait_ge(s_down_rows, 16)
                link = chain(dve, s_w, n, W_STEPS)
                blocks = width // W_BLOCK
                value = rows[:, i, :].rearrange("p (b c) -> p b c", c=W_BLOCK)
                scale, inv = w_scale[:, 0:blocks], w_inv[:, 0:blocks]
                wide = [P, blocks, W_BLOCK]
                link(dve.tensor_reduce(scale, value, AX, ALU.max, apply_absolute_value=True))
                link(dve.tensor_scalar(scale, scale, 1.0 / W_MAX, 1e-12, ALU.mult, ALU.max))
                link(dve.reciprocal(inv, scale))
                link(dve.tensor_tensor(value, value, inv.unsqueeze(2).broadcast_to(wide), ALU.mult))
                link(dve.tensor_scalar(value, value, ROUND, ROUND, ALU.add, ALU.subtract))
                link(dve.tensor_scalar(value, value, -W_MAX - 1.0, W_MAX, ALU.max, ALU.min))
                link(dve.tensor_tensor(value, value, scale.unsqueeze(2).broadcast_to(wide), ALU.mult))
                dve.sem_inc(s_w, 1)

            def scale_of(n, values):
                link = chain(dve, s_widest, n, 2)
                link(dve.tensor_tensor(values, values, g.exists[:], ALU.mult))
                link(dve.tensor_reduce(widest[:], values, AX, ALU.max))
                dve.wait_ge(s_level, 2 * n + 1)
                dve.tensor_reduce(top[:], ps_scale[0:1, 0:P], AX, ALU.max).then_inc(s_level, 1)
                dve.wait_ge(s_scaled, 3 * n + 1)
                dve.tensor_scalar(scales[:, n, 0:1], ps_scale[:, 0:1], 1.0 / A_MAX, 1e-12, ALU.mult, ALU.max).then_inc(s_scaled, 1)
                dve.wait_ge(s_scaled, 3 * n + 2)
                dve.reciprocal(scales[:, n, 1:2], scales[:, n, 0:1]).then_inc(s_scaled, 1)
                dve.wait_ge(s_scaled, 3 * n + 3)
                return scales[:, n, 0:1], scales[:, n, 1:2]

            scale, inv = scale_of(0, g.largest[:])

            def norm(t, p, m):
                dve.wait_ge(s_turn, t + 1)
                link = chain(dve, s_normed, t, 4)
                link(dve.tensor_scalar(normed[:], flat(g.big2[:, ds(t, 1), :]), g.means[:, ds(t, 1)], g.rstds[:, ds(t, 1)], ALU.subtract, ALU.mult))
                quantised(dve, link, normed[:], normed[:], inv, scale, -A_MAX - 1.0, A_MAX)

            def measure(t, p, m):
                dve.wait_ge(s_gate_up_kept, t + 1)
                for side in (0, 1):
                    ins = dve.tensor_reduce(largest[:, side, ds(t, 1)], ps_gate_up[:, side, 0:I], AX, ALU.max, apply_absolute_value=True)
                    ins.then_inc(s_largest, 1)
            pipeline(dve, T, [(norm, 0), (measure, 1)])
            dve.wait_ge(s_largest, 2 * T + 2)
            gate, up = gate_up[:, 0], gate_up[:, 1]
            link = chain(dve, s_quant, 0, 14)
            scale, inv = scale_of(1, largest[:, 0, :])
            quantised(dve, link, gate, gate, inv, scale, -A_MAX - 1.0, A_MAX)
            scale, inv = scale_of(2, largest[:, 1, :])
            quantised(dve, link, up, up, inv, scale, -A_MAX - 1.0, A_MAX)
            dve.wait_ge(s_sig, 1)
            quantised(dve, link, sig[:], sig[:], 65536.0, 1.0 / 65536.0, 0.0, S_MAX)
            link(dve.tensor_tensor(gate, gate, sig[:], ALU.mult))
            link(dve.tensor_reduce(largest[:, 0, :], gate, AX, ALU.max, apply_absolute_value=True))
            scale, inv = scale_of(3, largest[:, 0, :])
            quantised(dve, link, gate, gate, inv, scale, -A_MAX - 1.0, A_MAX)
            link2 = chain(dve, s_all, 0, 2)
            link2(dve.tensor_tensor(gate, gate, up, ALU.mult))
            link2(dve.tensor_reduce(largest[:, 0, :], gate, AX, ALU.max, apply_absolute_value=True))
            scale, inv = scale_of(4, largest[:, 0, :])

            def quantise_o(t, p, m):
                dve.wait_ge(s_o_turn, t + 1)
                link = chain(dve, s_o, t, 3)
                value = flat(gate[:, ds(t, 1), :])
                quantised(dve, link, normed[:, p * I:(p + 1) * I], value, inv, scale, -A_MAX - 1.0, A_MAX)

            def finish(t, p, m):
                dve.wait_ge(s_out[p], 16 * m + 16)
                dve.wait_ge(s_down, t + 2)
                dve.tensor_tensor(result[:, p, :], ps_down[:], flat(g.big2[:, ds(t, 1), :]), ALU.add).then_inc(s_result, 1)
            pipeline(dve, T, [(quantise_o, 0), (finish, 1)])

        @block.scalar
        def _(act):
            for n, (_, _, _, turned, blocks, at) in enumerate(ROWS):
                act.wait_ge(s_w_turn, n + 1)
                act.activation(turned[:, :, at:at + P], ps_turn[:, 0:blocks * P].rearrange("p (k c) -> p k c", c=P), ACT.Copy).then_inc(s_w_taken, 1)

            def take_turned(t, p, m):
                act.wait_ge(s_turn, t + 2)
                act.wait_ge(s_gate_up, t + 1)
                act.activation(normed_t[:].rearrange("p k c -> p (k c)"), ps_turn[:], ACT.Copy).then_inc(s_turned, 1)

            def keep(t, p, m):
                act.wait_ge(s_gate_up, t + 2)
                act.activation(gate_up[:, :, ds(t, 1), :].rearrange("p s a i -> p s (a i)"), ps_gate_up[:, :, 0:I], ACT.Copy).then_inc(s_gate_up_kept, 1)
            pipeline(act, T, [(keep, 1), (take_turned, 0)])
            act.wait_ge(s_quant, 3)
            act.activation(sig[:], gate_up[:, 0], ACT.Sigmoid).then_inc(s_sig, 1)

            def take_o(t, p, m):
                act.wait_ge(s_o_turn, t + 3)
                act.wait_ge(s_down, t + 1)
                act.activation(o_t[:].rearrange("p k c -> p (k c)"), ps_turn[:, 0:KI * P], ACT.Copy).then_inc(s_o_t, 1)
            pipeline(act, T, [(take_o, 0)])

        @block.tensor
        def _(pe):
            for n, (rows, i, _, _, blocks, _) in enumerate(ROWS):
                pe.wait_ge(s_w, (n + 1) * W_STEPS)
                if n:
                    pe.wait_ge(s_w_taken, n)
                for k in range(blocks):
                    last = pe.transpose(ps_turn[:, k * P:(k + 1) * P], rows[:, i, k * P:(k + 1) * P], g.ident[:])
                last.then_inc(s_w_turn, 1)

            def level(n):
                pe.wait_ge(s_widest, 2 * n + 2)
                pe.transpose(ps_scale[0:1, 0:P], widest[:, 0:1], g.ident[:]).then_inc(s_level, 1)
                pe.wait_ge(s_level, 2 * n + 2)
                pe.matmul(ps_scale[:, 0:1], g.ones[0:1, :], top[0:1, 0:1], start=True, stop=True).then_inc(s_scaled, 1)
            level(0)
            pe.sem_inc(s_turn, 1)
            pe.sem_inc(s_turned, 1)
            pe.sem_inc(s_gate_up, 1)
            pe.sem_inc(s_largest, 2)
            pe.wait_ge(s_w_taken, len(ROWS))

            def turn(t, p, m):
                pe.wait_ge(s_normed, 4 * t + 4)
                pe.wait_ge(s_turned, t + 1)
                for k in range(K):
                    last = pe.transpose(ps_turn[:, k * P:(k + 1) * P], normed[:, k * P:(k + 1) * P], g.ident[:])
                last.then_inc(s_turn, 1)

            def products(t, p, m):
                pe.wait_ge(s_turned, t + 2)
                pe.wait_ge(s_largest, 2 * t + 2)
                for side in (0, 1):
                    for k in range(K):
                        last = pe.matmul(ps_gate_up[:, side, 0:I], normed_t[:, k, :], gate_up_t[:, k, side * I:(side + 1) * I], start=(k == 0), stop=(k == K - 1))
                last.then_inc(s_gate_up, 1)
            pipeline(pe, T, [(turn, 0), (products, 0)])
            for n in range(1, 5):
                level(n)
            pe.sem_inc(s_o_t, 1)
            pe.sem_inc(s_result, 1)
            pe.sem_inc(s_o_turn, 2)
            pe.sem_inc(s_down, 1)

            def turn_o(t, p, m):
                pe.wait_ge(s_o, 3 * t + 3)
                pe.wait_ge(s_o_t, t + 1)
                for k in range(KI):
                    last = pe.transpose(ps_turn[:, k * P:(k + 1) * P], normed[:, p * I + k * P:p * I + (k + 1) * P], g.ident[:])
                last.then_inc(s_o_turn, 1)

            def down(t, p, m):
                pe.wait_ge(s_o_t, t + 2)
                pe.wait_ge(s_result, t + 1)
                for a in range(0, D, HALF):
                    for k in range(KI):
                        last = pe.matmul(ps_down[:, a:a + HALF], o_t[:, k, :], down_t[:, k, a:a + HALF], start=(k == 0), stop=(k == KI - 1))
                last.then_inc(s_down, 1)
            pipeline(pe, T, [(turn_o, 0), (down, 0)])


def build(nc, ins, out, until=99):
    x, src, dst, w_gnn = ins["x"], ins["src"], ins["dst"], ins["L0_gnn_W"]
    g = Shared()
    g.N, g.D = x.shape
    g.E = src.shape[0]
    g.T, g.K = tiles(g.N), g.D // P
    g.NP = g.T * P
    T, K, NP, D = g.T, g.K, g.NP, g.D
    g.X = ins["L0_ffn_w_gate"].shape[1]
    g.slot_tiles = (NP + g.X * (P - 1)) // P
    with ExitStack() as ctx:
        def sb(name, shape, dt):
            return ctx.enter_context(nc.sbuf_tensor(name, shape, dt))

        def sem(name):
            return ctx.enter_context(nc.semaphore(name))

        g.counts_dram = nc.dram_tensor("counts_dram", (T, P, NP), F32).ap()
        g.turned_dram = nc.dram_tensor("turned_dram", (T, P, NP), F32).ap()
        g.normed_dram = nc.dram_tensor("normed_dram", (NP, D), F32).ap()
        g.slot_token_dram = nc.dram_tensor("slot_token_dram", (g.slot_tiles * P, 1), I32).ap()
        g.y_dram = nc.dram_tensor("y_dram", (g.slot_tiles * P, D), F32).ap()
        g.x_dram = nc.dram_tensor("x_dram", (T, P, D), F32).ap()
        g.big1 = sb("big1", [P, T, D], F32)
        g.big2 = sb("big2", [P, T, D], F32)
        g.col_id = sb("col_id", [P, P], F32)
        g.row_id = sb("row_id", [P, 1], F32)
        g.node_id = sb("node_id", [P, T], F32)
        g.token_id = sb("token_id", [P, T], I32)
        g.exists = sb("exists", [P, T], F32)
        g.ident = sb("ident", [P, P], F32)
        g.before = sb("before", [P, P], F32)
        g.ones = sb("ones", [P, P], F32)
        g.eps = sb("eps", [P, 1], F32)
        g.deg = sb("deg", [P, T], F32)
        g.route_p = sb("route_p", [P, T], F32)
        g.chosen = sb("chosen", [P, T, g.X], F32)
        g.slot = sb("slot", [P, T], I32)
        g.mean_var = sb("mean_var", [P, 2], F32)
        g.means = sb("means", [P, T], F32)
        g.rstds = sb("rstds", [P, T], F32)
        g.largest = sb("largest", [P, T], F32)
        g.sides = sb("sides", [P, T, 2], F32)
        g.always = sem("always")
        x_arrived = sem("x_arrived")
        w_arrived = sem("w_arrived")
        with ExitStack() as early:
            g.w_gnn = early.enter_context(nc.sbuf_tensor("w_gnn", [P, K, D], F32))
            graph_phase(nc, g, src, dst, x, w_gnn, x_arrived, w_arrived)
            if until < 1:
                with nc.Block() as block:
                    @block.sync
                    def _(sp):
                        sp.wait_ge(x_arrived, 32)
                        sp.wait_ge(w_arrived, 16)
                return
            hidden_phase(nc, g, ins["L0_gnn_a"], x_arrived, w_arrived)
            if until < 2:
                return
        attention_phase(nc, g, ins["L0_ffn_w_gate"], ins["L0_ffn_b_gate"])
        if until < 3:
            return
        expert_phase(nc, g, ins["L0_ffn_W1"], ins["L0_ffn_b1"], ins["L0_ffn_W2"], ins["L0_ffn_b2"])
        combine_phase(nc, g)
        if until < 4:
            return
        sage_phase(nc, g, "sage0", g.big2, g.big1, ins["L1_gnn_W_self0"], ins["L1_gnn_W_neigh0"], ins["L1_gnn_b0"], False)
        if until < 5:
            return
        sage_phase(nc, g, "sage1", g.big1, g.big2, ins["L1_gnn_W_self1"], ins["L1_gnn_W_neigh1"], ins["L1_gnn_b1"], True)
        if until < 6:
            return
        feed_forward_phase(nc, g, ins["L1_ffn_w_gate"], ins["L1_ffn_w_up"], ins["L1_ffn_w_down"], out)


_INS = ["x", "src", "dst", "L0_gnn_W", "L0_gnn_a", "L0_ffn_w_gate", "L0_ffn_b_gate", "L0_ffn_W1", "L0_ffn_b1",
        "L0_ffn_W2", "L0_ffn_b2", "L1_gnn_W_self0", "L1_gnn_W_neigh0", "L1_gnn_b0", "L1_gnn_W_self1",
        "L1_gnn_W_neigh1", "L1_gnn_b1", "L1_ffn_w_gate", "L1_ffn_w_up", "L1_ffn_w_down"]


def kernel(**inputs):
    import numpy as np
    import concourse.bacc as bacc
    from concourse.bass_utils import run_bass_kernel_spmd

    nc = bacc.Bacc("TRN2", target_bir_lowering=False, num_devices=1)
    arrays, ins = {}, {}
    for name in _INS:
        a = np.ascontiguousarray(inputs[name])
        arrays[f"in_{name}"] = a
        ins[name] = nc.dram_tensor(f"in_{name}", a.shape, mybir.dt.from_np(a.dtype), kind="ExternalInput").ap()
    out = nc.dram_tensor("out", inputs["x"].shape, F32, kind="ExternalOutput").ap()
    build(nc, ins, out)
    r = run_bass_kernel_spmd(nc, [arrays], core_ids=[0])
    return r.results[0]["out"]
```

```python
from contextlib import ExitStack

import concourse.bass as bass
from concourse import mybir

ALU = mybir.AluOpType
ACT = mybir.ActivationFunctionType
AX = mybir.AxisListType.X
F32 = mybir.dt.float32
F32R = mybir.dt.float32r
F16 = mybir.dt.float16
I32 = mybir.dt.int32
ds = bass.ds

P = 128
HALF = 512
CHUNKS = 4
UNIT = CHUNKS * P
ROUND = 12582912.0
LN_EPS = 1e-5
GAT_EPS = 1e-5
NEG_SLOPE = 0.1
W_BLOCK = 32
W_MAX = 7.0
A_MAX = 32767.0
S_MAX = 65535.0


def flat(ap):
    return ap.rearrange("p a d -> p (a d)")


def tiles(n):
    return -(-n // P)


def makers(ctx, nc, phase):
    def sb(name, shape, dt=F32):
        return ctx.enter_context(nc.sbuf_tensor(f"{phase}_{name}", shape, dt))

    def ps(name, shape):
        return ctx.enter_context(nc.psum_tensor(f"{phase}_{name}", shape, F32))

    def sem(name):
        return nc.alloc_semaphore(f"{phase}_{name}")
    return sb, ps, sem


def layer_stats(dve, g, link, halves, stats, mean_var):
    link(dve.bn_stats(stats[:, 0:6], halves[0]), g.always)
    link(dve.bn_stats(stats[:, 6:12], halves[1]), g.always)
    link(dve.bn_aggr(mean_var, stats))


def wait_apart(eng, always, sem, value):
    if isinstance(value, int):
        eng.wait_ge(always, 1)
        eng.wait_ge(sem, value)
        return
    with eng.register() as reg:
        eng.reg_mov(reg, value)
        eng.wait_ge(always, 1)
        eng.wait_ge(sem, reg)


def chain(eng, sem, t, per, start=0):
    k = [0]

    def link(ins, always=None):
        k[0] += 1
        assert k[0] <= per
        ins.then_inc(sem, 1)
        if always is None:
            eng.wait_ge(sem, t * per + k[0] + start)
        else:
            wait_apart(eng, always, sem, t * per + k[0] + start)
    return link


def pipeline(eng, count, stages, pairs=None, last_apart=False):
    deepest = max(lag for _, lag in stages)
    first = deepest + deepest % 2
    end = count - count % 2 - (2 if last_apart else 0)

    def step(s):
        for stage, lag in stages:
            t = s - lag
            if 0 <= t and (pairs is not None or t < count):
                stage(t, t % 2, t // 2)

    if pairs is None and first >= end:
        for s in range(count + deepest):
            step(s)
        return
    for s in range(first):
        step(s)
    with eng.Fori(first // 2, end // 2 if pairs is None else pairs) as i:
        for r in (0, 1):
            for stage, lag in stages:
                stage(2 * i + (r - lag), (r - lag) % 2, i + (r - lag) // 2)
    if pairs is None:
        for s in range(end, count + deepest):
            step(s)
        return
    for r in range(deepest):
        for stage, lag in stages:
            if lag > r:
                stage(2 * pairs + (r - lag), (r - lag) % 2, pairs + (r - lag) // 2)


class Split:

    def __init__(self, makers, name, raw, both):
        _, _, sem = makers
        self.raw, self.both, self.K = raw, both, both.shape[2]
        self.s_raw = [sem(f"s_{name}_raw0"), sem(f"s_{name}_raw1")]
        self.s_high = sem(f"s_{name}_high")
        self.s_low = sem(f"s_{name}_low")

    def load(self, sp, source):
        rows = source.rearrange("(k p) n -> k p n", p=P)
        sp.sem_inc(self.s_low, 2)

        def load(k, p, m):
            sp.wait_ge(self.s_low, k + 1)
            sp.dma_start(self.raw[:, p, :], rows[ds(k, 1)].rearrange("a p n -> (a p) n")).then_inc(self.s_raw[p], 16)
        pipeline(sp, self.K, [(load, 0)])

    def high(self, act):
        def high(k, p, m):
            act.wait_ge(self.s_raw[p], 16 * m + 16)
            act.activation(flat(self.both[:, 0, ds(k, 1), :]), self.raw[:, p, :], ACT.Copy).then_inc(self.s_high, 1)
        pipeline(act, self.K, [(high, 0)])

    def low(self, dve):
        def low(k, p, m):
            dve.wait_ge(self.s_high, k + 1)
            dve.tensor_tensor(flat(self.both[:, 1, ds(k, 1), :]), self.raw[:, p, :],
                              flat(self.both[:, 0, ds(k, 1), :]).bitcast(F32), ALU.subtract).then_inc(self.s_low, 1)
        pipeline(dve, self.K, [(low, 0)])

    def ready(self, pe, k=None):
        pe.wait_ge(self.s_low, (self.K if k is None else k + 1) + 2)


TERMS = ((0, 0), (0, 1), (1, 0))


def products(pe, out, left, right, k, start, stop):
    for n, (l, r) in enumerate(TERMS):
        for a in range(0, out.shape[1], HALF):
            b = min(a + HALF, out.shape[1])
            last = pe.matmul(out[:, a:b], left(l, k), right(r, k)[:, a:b], start=start and n == 0, stop=stop and n == 2)
    return last


class Shared:
    pass


def graph_phase(nc, g, src, dst):
    T, N, NP, E = g.T, g.N, g.NP, g.E
    full, rest = E // UNIT, E % UNIT
    units = full + (rest > 0)
    with ExitStack() as ctx:
        sb, ps, sem = makers(ctx, nc, "graph")

        src_i = sb("src_i", [P, UNIT], I32)
        dst_i = sb("dst_i", [P, UNIT], I32)
        src_f = sb("src_f", [P, UNIT], F32)
        dst_f = sb("dst_f", [P, UNIT], F32)
        least = sb("least", [P, 1])
        most = sb("most", [P, 1])
        starts = sb("starts", [P, T])
        ends = sb("ends", [P, T])
        present = sb("present", [P, T], F32)
        from_start = sb("from_start", [T, units], F32)
        from_end = sb("from_end", [T, units], F32)
        edge_of = sb("edge_of", [T, 2], F32)
        bounds = sb("bounds", [T, 2], F32)
        bounds_i = sb("bounds_i", [1, 2 * T], I32)
        col_i = sb("col_i", [P, NP], I32)
        row_i = sb("row_i", [P, 1], I32)
        node_i = sb("node_i", [P, T], I32)
        src_t = sb("src_t", [P, CHUNKS, units], F32)
        dst_t = sb("dst_t", [P, CHUNKS, units], F16)
        zeros16 = sb("zeros16", [P, P], F16)
        iota16 = sb("iota16", [P, NP], F16)
        dst_hot = sb("dst_hot", [P, CHUNKS, P], F16)
        src_hot = sb("src_hot", [P, CHUNKS, N], F16)
        counts = sb("counts", [P, 2, NP], F32)
        turned = sb("turned", [P, 2, T, P], F32)
        deg_t = sb("deg_t", [P, 2], F32)
        acc = ps("acc", [P, 2, 3 * HALF])
        ps_turn = ps("ps_turn", [P, 2, HALF])

        s_iota = sem("s_iota")
        s_fill = sem("s_fill")
        s_src = sem("s_src")
        s_dst = sem("s_dst")
        s_rest = sem("s_rest")
        s_const = sem("s_const")
        s_prep = sem("s_prep")
        s_present_t = sem("s_present_t")
        s_edges_t = sem("s_edges_t")
        s_edges_kept = sem("s_edges_kept")
        s_bounds = sem("s_bounds")
        s_bounds_t = sem("s_bounds_t")
        s_ready = sem("s_ready")
        s_hot = sem("s_hot")
        s_hot_free = sem("s_hot_free")
        s_acc = sem("s_acc")
        s_counts = sem("s_counts")
        s_turn = sem("s_turn")
        s_turn_free = sem("s_turn_free")
        s_counts_out = [sem("s_counts_out0"), sem("s_counts_out1")]
        s_turned_out = [sem("s_turned_out0"), sem("s_turned_out1")]
        block = ctx.enter_context(nc.Block())

        @block.gpsimd
        def _(pool):
            pool.iota(col_i[:], [[1, NP]], base=0, channel_multiplier=0).then_inc(s_iota, 1)
            pool.iota(row_i[:], [[1, 1]], base=0, channel_multiplier=1).then_inc(s_iota, 1)
            pool.iota(node_i[:], [[P, T]], base=0, channel_multiplier=1).then_inc(s_iota, 1)
            pool.iota(g.token_id[:], [[P, T]], base=0, channel_multiplier=1).then_inc(s_iota, 1)

        @block.sync
        def _(sp):
            sp.wait_ge(s_fill, 2)
            sp.dma_start(dst_i[0:full, :], dst[0:full * UNIT].rearrange("(a b) -> a b", b=UNIT)).then_inc(s_dst, 16)
            sp.dma_start(src_i[0:full, :], src[0:full * UNIT].rearrange("(a b) -> a b", b=UNIT)).then_inc(s_src, 16)
            if rest:
                sp.dma_start(dst_i[full:full + 1, 0:rest], dst[full * UNIT:E].rearrange("(a b) -> a b", a=1)).then_inc(s_rest, 16)
                sp.dma_start(src_i[full:full + 1, 0:rest], src[full * UNIT:E].rearrange("(a b) -> a b", a=1)).then_inc(s_rest, 16)
            def store(t, p, m):
                sp.wait_ge(s_counts, t + 3)
                sp.dma_start(g.counts_dram[ds(t, 1)].rearrange("a p n -> (a p) n"), counts[:, p, :]).then_inc(s_counts_out[p], 16)
                sp.wait_ge(s_turn_free, 3 * t + 5)
                sp.dma_start(g.turned_dram[ds(t, 1)].rearrange("a p n -> (a p) n"),
                             turned[:, p].rearrange("p j c -> p (j c)")).then_inc(s_turned_out[p], 16)
            pipeline(sp, T, [(store, 0)])
            for p in (0, 1):
                sp.wait_ge(s_counts_out[p], 16 * (T // 2) + 16)
                sp.wait_ge(s_turned_out[p], 16 * (T // 2) + 16)

        @block.vector
        def _(dve):
            dve.sem_inc(g.always, 1)
            dve.memset(src_i[:], -1).then_inc(s_fill, 1)
            dve.memset(dst_i[:], N - 1).then_inc(s_fill, 1)
            dve.memset(zeros16[:], 0.0).then_inc(s_const, 1)
            dve.memset(g.ones[:], 1.0).then_inc(s_const, 1)
            dve.memset(g.eps[:], LN_EPS).then_inc(s_const, 1)
            dve.memset(counts[:, :, N:NP], 0.0).then_inc(s_const, 1)
            dve.wait_ge(s_iota, 4)
            dve.tensor_copy(g.col_id[:], col_i[:, 0:P]).then_inc(s_const, 1)
            dve.tensor_copy(iota16[:], col_i[:]).then_inc(s_const, 1)
            dve.tensor_copy(g.row_id[:], row_i[:]).then_inc(s_const, 1)
            dve.tensor_copy(g.node_id[:], node_i[:]).then_inc(s_const, 1)
            dve.wait_ge(s_const, 8)
            dve.tensor_scalar(g.ident[:], g.col_id[:], g.row_id[:, 0:1], None, ALU.is_equal).then_inc(s_const, 1)
            dve.tensor_scalar(g.before[:], g.col_id[:], g.row_id[:, 0:1], None, ALU.is_gt).then_inc(s_const, 1)
            dve.tensor_copy(g.ones_r[:], g.ones[:]).then_inc(s_const, 1)
            dve.tensor_scalar(g.exists[:], g.node_id[:], float(N), None, ALU.is_lt).then_inc(s_const, 1)
            dve.wait_ge(s_dst, 16)
            dve.wait_ge(s_src, 16)
            if rest:
                dve.wait_ge(s_rest, 32)
            link = chain(dve, s_prep, 0, 8)
            link(dve.tensor_copy(src_f[:], src_i[:]))
            link(dve.tensor_copy(dst_f[:], dst_i[:]))
            link(dve.tensor_reduce(least[:], dst_f[:], AX, ALU.min))
            link(dve.tensor_reduce(most[:], dst_f[:], AX, ALU.max))
            link(dve.tensor_scalar(starts[:], g.col_id[:, 0:T], float(P), None, ALU.mult))
            link(dve.tensor_scalar(ends[:], starts[:], float(P), None, ALU.add))
            link(dve.tensor_scalar(ends[:], ends[:], least[:, 0:1], None, ALU.is_gt))
            link(dve.scalar_tensor_tensor(present[:], starts[:], most[:, 0:1], ends[:], ALU.is_le, ALU.mult))
            dve.wait_ge(s_edges_t, 2)
            dve.tensor_copy(src_t[:], acc[:, 0, 0:CHUNKS * P].rearrange("p (c u) -> p c u", c=CHUNKS)[:, :, 0:units]).then_inc(s_edges_kept, 1)
            dve.tensor_copy(dst_t[:], acc[:, 0, HALF:HALF + CHUNKS * P].rearrange("p (c u) -> p c u", c=CHUNKS)[:, :, 0:units]).then_inc(s_edges_kept, 1)
            dve.wait_ge(s_present_t, 1)
            link = chain(dve, s_bounds, 0, 9)
            here = ps_turn[0:T, 0, 0:units]
            link(dve.tensor_scalar(from_start[:], g.col_id[0:T, 0:units], 1.0, None, ALU.add))
            link(dve.tensor_scalar(from_end[:], g.col_id[0:T, 0:units], -1.0, float(units), ALU.mult, ALU.add))
            link(dve.tensor_tensor(from_start[:], from_start[:], here, ALU.mult))
            link(dve.tensor_tensor(from_end[:], from_end[:], here, ALU.mult))
            link(dve.tensor_reduce(edge_of[:, 0:1], from_end[:], AX, ALU.max))
            link(dve.tensor_reduce(edge_of[:, 1:2], from_start[:], AX, ALU.max))
            link(dve.tensor_scalar(bounds[:, 0:1], edge_of[:, 0:1], -1.0, float(units), ALU.mult, ALU.add))
            link(dve.tensor_scalar(bounds[:, 0:1], bounds[:, 0:1], float(units - 1), None, ALU.min))
            link(dve.tensor_scalar(bounds[:, 1:2], edge_of[:, 1:2], -1.0, bounds[:, 0:1], ALU.add, ALU.max))
            dve.wait_ge(s_bounds_t, 1)
            dve.tensor_copy(bounds_i[0:1, 0:T], ps_turn[0:1, 1, 0:T]).then_inc(s_ready, 1)
            dve.tensor_scalar(bounds_i[0:1, T:2 * T], ps_turn[0:1, 1, T:2 * T], 1.0, None, ALU.add).then_inc(s_ready, 1)
            dve.wait_ge(s_ready, 2)
            dve.wait_ge(s_edges_kept, 2)
            made = dve.alloc_register("hot_made")
            dve.reg_mov(made, 0)

            def hot(t, p, m):
                lo = dve.value_load(bounds_i[0:1, ds(t, 1)], min_val=0, max_val=units - 1)
                hi = dve.value_load(bounds_i[0:1, ds(t + T, 1)], min_val=1, max_val=units)
                with dve.Fori(lo, hi) as u:
                    for c in range(0, CHUNKS, 2):
                        dve.reg_add(made, made, 1)
                        dve.wait_ge(s_hot_free, made)
                        here = [P, 2, P]
                        dve.tensor_tensor(dst_hot[:, c:c + 2, :], iota16[:, ds(t * P, P)].unsqueeze(1).broadcast_to(here),
                                          dst_t[:, c:c + 2, ds(u, 1)].broadcast_to(here), ALU.is_equal)
                        for d in (c, c + 1):
                            dve.tensor_scalar(src_hot[:, d, :], iota16[:, 0:N], src_t[:, d, ds(u, 1)], None, ALU.is_equal).then_inc(s_hot, 1)
            pipeline(dve, T, [(hot, 0)])
            dve.free_register(made)

        @block.tensor
        def _(pe):
            pe.sem_inc(s_hot_free, CHUNKS // 2)
            pe.wait_ge(s_const, 12)
            pe.wait_ge(s_prep, 8)
            for c in range(CHUNKS):
                last = pe.transpose(acc[:, 0, c * P:(c + 1) * P], src_f[:, c * P:(c + 1) * P], g.ident[:])
            last.then_inc(s_edges_t, 1)
            for c in range(CHUNKS):
                last = pe.transpose(acc[:, 0, HALF + c * P:HALF + (c + 1) * P], dst_f[:, c * P:(c + 1) * P], g.ident[:])
            last.then_inc(s_edges_t, 1)
            pe.transpose(ps_turn[0:T, 0, 0:P], present[:], g.ident[:]).then_inc(s_present_t, 1)
            pe.wait_ge(s_bounds, 9)
            pe.transpose(ps_turn[0:1, 1, 0:T], bounds[:, 0:1], g.ident[0:T, 0:T])
            pe.transpose(ps_turn[0:1, 1, T:2 * T], bounds[:, 1:2], g.ident[0:T, 0:T]).then_inc(s_bounds_t, 1)
            pe.wait_ge(s_ready, 2)
            pe.wait_ge(s_edges_kept, 2)
            done = pe.alloc_register("hot_done")
            pe.reg_mov(done, 0)
            spans = [(a, min(a + HALF, N)) for a in range(0, N, HALF)]

            def count(t, p, m):
                lo = pe.value_load(bounds_i[0:1, ds(t, 1)], min_val=0, max_val=units - 1)
                hi = pe.value_load(bounds_i[0:1, ds(t + T, 1)], min_val=1, max_val=units)
                pe.wait_ge(s_counts, t + 1)
                for a, b in spans:
                    pe.matmul(acc[:, p, a:b], zeros16[:], iota16[:, 0:b - a], start=True, stop=False, skip_group_check=True)
                with pe.Fori(lo, hi) as u:
                    for c in range(CHUNKS):
                        pe.reg_add(done, done, 1)
                        pe.wait_ge(s_hot, done)
                        for a, b in spans:
                            last = pe.matmul(acc[:, p, a:b], dst_hot[:, c, :], src_hot[:, c, a:b], start=False, stop=False, skip_group_check=True)
                        if c % 2:
                            last.then_inc(s_hot_free, 1)
                for a, b in spans:
                    last = pe.matmul(acc[:, p, a:a + 2], zeros16[:], iota16[:, 0:2], start=False, stop=True, skip_group_check=True)
                last.then_inc(s_acc, 1)

            def turn(t, p, m):
                pe.wait_ge(s_counts, t + 3)
                for r in range(3):
                    pe.wait_ge(s_turn_free, t * 3 + r + 1)
                    for j in range(4 * r, min(4 * r + 4, T)):
                        last = pe.transpose(ps_turn[:, (p + r) % 2, (j % 4) * P:(j % 4 + 1) * P], counts[:, p, j * P:(j + 1) * P], g.ident[:])
                    last.then_inc(s_turn, 1)
            pipeline(pe, T, [(count, 0), (turn, 1)])
            pe.free_register(done)

        @block.scalar
        def _(act):
            act.sem_inc(s_counts, 2)
            act.sem_inc(s_turn_free, 2)
            for p in (0, 1):
                act.sem_inc(s_counts_out[p], 16)
                act.sem_inc(s_turned_out[p], 16)
            act.wait_ge(s_const, 12)
            def take(t, p, m):
                act.wait_ge(s_acc, t + 1)
                act.wait_ge(s_counts_out[p], m * 16 + 16)
                act.activation(counts[:, p, 0:N], acc[:, p, 0:N], ACT.Copy, accum_out=deg_t[:, p:p + 1]).then_inc(s_counts, 1)
                act.wait_ge(s_counts, t + 3)
                act.activation(g.deg[:, ds(t, 1)], deg_t[:, p:p + 1], ACT.Copy)

            def take_turned(t, p, m):
                act.wait_ge(s_turned_out[p], m * 16 + 16)
                for r in range(3):
                    act.wait_ge(s_turn, t * 3 + r + 1)
                    n = min(4, T - 4 * r)
                    ins = act.activation(turned[:, p, 4 * r:4 * r + n, :], ps_turn[:, (p + r) % 2, 0:n * P].rearrange("p (j c) -> p j c", c=P), ACT.Copy)
                    ins.then_inc(s_turn_free, 1)
            pipeline(act, T, [(take, 0), (take_turned, 1)])


def hidden_phase(nc, g, x, w_source, a, w, nodes):
    T, K, D, N = g.T, g.K, g.D, g.N
    with ExitStack() as ctx:
        sb, ps, sem = makers(ctx, nc, "hidden")

        a_rows = sb("a_rows", [P, 2 * D])
        x_t = sb("x_t", [P, 2, D])
        stats = sb("stats", [P, 2, 12])
        mean_var = sb("mean_var", [P, 2, 2])
        std = sb("std", [P, 2])
        rstd = sb("rstd", [P, 2])
        normed = sb("normed", [P, 2, D])
        normed_t = sb("normed_t", [P, 2, 2, K, P], F32R)
        split = Split((sb, ps, sem), "w", sb("w_raw", [P, 2, D]), w)
        product = sb("product", [P, D])
        side = sb("side", [P, 2, 2])
        ps_turn = ps("ps_turn", [P, D])
        ps_h = ps("ps_h", [P, 2, D])

        s_a = sem("s_a")
        s_x = [sem("s_x0"), sem("s_x1")]
        s_x_pad = sem("s_x_pad")
        s_stats = sem("s_stats")
        s_std = sem("s_std")
        s_normed = sem("s_normed")
        s_turn = sem("s_turn")
        s_high = sem("s_high")
        s_turned = sem("s_turned")
        s_h = sem("s_h")
        s_h_taken = sem("s_h_taken")
        s_sides = sem("s_sides")
        s_half_free = sem("s_half_free")
        block = ctx.enter_context(nc.Block())

        @block.sync
        def _(sp):
            def load(t, p, m):
                sp.wait_ge(s_normed, t + 1)
                if isinstance(t, int) and (t + 1) * P > N:
                    sp.wait_ge(s_x_pad, 1)
                    sp.dma_start(x_t[0:N - t * P, p, :], x[t * P:N, :]).then_inc(s_x[p], 16)
                else:
                    sp.dma_start(x_t[:, p, :], x[ds(t * P, P), :]).then_inc(s_x[p], 16)
            load(0, 0, 0)
            load(1, 1, 0)
            split.load(sp, w_source)
            sp.dma_start(a_rows[:], a.broadcast_to([P, 2 * D])).then_inc(s_a, 16)
            with sp.Fori(1, T // 2 - 1) as i:
                for p in (0, 1):
                    load(2 * i + p, p, i)
            load(T - 2, 0, T // 2 - 1)
            load(T - 1, 1, T // 2 - 1)

        @block.vector
        def _(dve):
            dve.sem_inc(s_normed, 2)
            split.low(dve)

            def norm(t, p, m):
                if isinstance(t, int) and t == T - 1:
                    dve.wait_ge(s_normed, T)
                    dve.memset(x_t[:, p, :], 0.0).then_inc(s_x_pad, 1)
                dve.wait_ge(s_x[p], 16 * m + 16)
                link = chain(dve, s_stats, t, 3)
                layer_stats(dve, g, link, [x_t[:, p, a:a + HALF] for a in (0, HALF)], stats[:, p, :], mean_var[:, p, :])
                dve.wait_ge(s_std, 2 * t + 1)
                dve.reciprocal(rstd[:, p:p + 1], std[:, p:p + 1]).then_inc(s_std, 1)
                dve.wait_ge(s_std, 2 * t + 2)
                dve.tensor_scalar(normed[:, p, :], x_t[:, p, :], mean_var[:, p, 0:1],
                                  rstd[:, p:p + 1], ALU.subtract, ALU.mult).then_inc(s_normed, 1)

            def low(t, p, m):
                dve.wait_ge(s_high, t + 1)
                dve.tensor_tensor(normed_t[:, p, 1].rearrange("p k c -> p (k c)"), ps_turn[:],
                                  normed_t[:, p, 0].rearrange("p k c -> p (k c)").bitcast(F32), ALU.subtract).then_inc(s_turned, 1)

            def sides(t, p, m):
                dve.wait_ge(s_h_taken, t + 1)
                link = chain(dve, s_sides, t, 4)
                high = flat(nodes[:, ds(t, 1), 0, :])
                link(dve.tensor_tensor(flat(nodes[:, ds(t, 1), 1, :]), ps_h[:, p, :], high.bitcast(F32), ALU.subtract))
                for k in (0, 1):
                    link(dve.tensor_tensor_reduce(product[:], ps_h[:, p, :], a_rows[:, k * D:(k + 1) * D], 1.0, 0.0,
                                                  ALU.mult, ALU.add, side[:, p, k:k + 1]))
                dve.sem_inc(s_half_free, 1)
                link(dve.tensor_copy(flat(g.sides[:, ds(t, 1), :]), side[:, p, :]), g.always)
            dve.wait_ge(s_a, 16)
            pipeline(dve, T, [(low, 1), (norm, 0), (sides, 2)], last_apart=True)

        @block.scalar
        def _(act):
            split.high(act)

            def root(t, p, m):
                act.wait_ge(s_stats, t * 3 + 3)
                act.activation(std[:, p:p + 1], mean_var[:, p, 1:2], ACT.Sqrt, bias=g.eps[:, 0:1]).then_inc(s_std, 1)

            def take_turned(t, p, m):
                act.wait_ge(s_turn, t + 1)
                act.activation(normed_t[:, p, 0].rearrange("p k c -> p (k c)"), ps_turn[:], ACT.Copy).then_inc(s_high, 1)

            def take_h(t, p, m):
                act.wait_ge(s_h, t + 1)
                act.activation(flat(nodes[:, ds(t, 1), 0, :]), ps_h[:, p, :], ACT.Copy).then_inc(s_h_taken, 1)
            pipeline(act, T, [(take_turned, 1), (root, 0), (take_h, 2)])

        @block.tensor
        def _(pe):
            pe.sem_inc(s_turned, 1)
            pe.sem_inc(s_half_free, 2)
            def turn(t, p, m):
                pe.wait_ge(s_normed, t + 3)
                pe.wait_ge(s_turned, t + 1)
                for k in range(K):
                    last = pe.transpose(ps_turn[:, k * P:(k + 1) * P], normed[:, p, k * P:(k + 1) * P], g.ident[:])
                last.then_inc(s_turn, 1)

            def multiply(t, p, m):
                pe.wait_ge(s_turned, t + 2)
                pe.wait_ge(s_half_free, t + 1)
                for k in range(K):
                    if isinstance(t, int) and t == 0:
                        split.ready(pe, k)
                    last = products(pe, ps_h[:, p, :], lambda s, k: normed_t[:, p, s, k, :], lambda s, k: w[:, s, k, :], k, k == 0, k == K - 1)
                last.then_inc(s_h, 1)
            pipeline(pe, T, [(turn, 0), (multiply, 1)])


def attention_phase(nc, g, x, w_gate, b_gate, nodes):
    T, K, D, X, N = g.T, g.K, g.D, g.X, g.N
    with ExitStack() as ctx:
        sb, ps, sem = makers(ctx, nc, "attend")
        gate_w = sb("gate_w", [P, K, X])
        gate_b = sb("gate_b", [P, X])
        order = sb("order", [P, X])
        counts = sb("counts", [P, 2, T, P])
        diag = sb("diag", [P, 2, P])
        sums = sb("sums", [P, T, P])
        leaky = sb("leaky", [P, 2, T, P])
        weights = sb("weights", [P, 2, 2, T, P], F32R)
        x_t = sb("x_t", [P, 2, D])
        rowsum = sb("rowsum", [P, 2])
        inv = sb("inv", [P, 2])
        below = sb("below", [P, D])
        above = sb("above", [P, D])
        elu = sb("elu", [P, D])
        stats = sb("stats", [P, 12])
        mean_var = sb("mean_var", [P, 2])
        std = sb("std", [P, 1])
        rstd = sb("rstd", [P, 1])
        normed = sb("normed", [P, 2, D])
        normed_t = sb("normed_t", [P, K, P])
        logits = sb("logits", [P, X])
        neg_max = sb("neg_max", [P, 1])
        exps = sb("exps", [P, X])
        exp_sum = sb("exp_sum", [P, 1])
        exp_max = sb("exp_max", [P, 1])
        ranked = sb("ranked", [P, X])
        best = sb("best", [P, 1])
        ps_h = ps("ps_h", [P, 2, D])
        ps_turn = ps("ps_turn", [P, D])
        ps_left = ps("ps_left", [P, P])
        ps_rowsum = ps("ps_rowsum", [P, 2])

        s_gate = sem("s_gate")
        s_order = sem("s_order")
        s_counts = [sem("s_counts0"), sem("s_counts1")]
        s_x = [sem("s_x_0"), sem("s_x_1")]
        s_x_pad = sem("s_x_pad")
        s_x1_out = [sem("s_x1_out0"), sem("s_x1_out1")]
        s_product = sem("s_product")
        s_high = sem("s_high")
        s_diag = sem("s_diag")
        s_left = sem("s_left")
        s_sums = sem("s_sums")
        s_exp = sem("s_exp")
        s_weights = sem("s_weights")
        s_attended = sem("s_attended")
        s_inv = sem("s_inv")
        s_below = sem("s_below")
        s_elu_parts = sem("s_elu_parts")
        s_x1 = sem("s_x1")
        s_stats = sem("s_stats")
        s_std = sem("s_std")
        s_normed = sem("s_normed")
        s_stored = [sem("s_stored0"), sem("s_stored1")]
        s_turn = sem("s_turn")
        s_turned = sem("s_turned")
        s_logits = sem("s_logits")
        s_logits_read = sem("s_logits_read")
        s_exps = sem("s_exps")
        s_route = sem("s_route")
        block = ctx.enter_context(nc.Block())

        @block.sync
        def _(sp):
            sp.dma_start(gate_w[:], w_gate.rearrange("(k p) e -> p k e", p=P)).then_inc(s_gate, 16)
            sp.dma_start(gate_b[:], b_gate.rearrange("(a e) -> a e", a=1).broadcast_to([P, X])).then_inc(s_gate, 16)

            def load(t, p, m):
                sp.wait_ge(s_product, t + 1)
                sp.dma_start(counts[:, p], g.counts_dram.rearrange("j p n -> p j n")[:, :, ds(t * P, P)]).then_inc(s_counts[p], 16)

            def load_x(t, p, m):
                sp.wait_ge(s_x1_out[p], 16 * m + 16)
                if isinstance(t, int) and (t + 1) * P > N:
                    sp.wait_ge(s_x_pad, 1)
                    sp.dma_start(x_t[0:N - t * P, p, :], x[t * P:N, :]).then_inc(s_x[p], 16)
                else:
                    sp.dma_start(x_t[:, p, :], x[ds(t * P, P), :]).then_inc(s_x[p], 16)

            def store(t, p, m):
                sp.wait_ge(s_normed, t + 1)
                sp.dma_start(g.x1_dram[ds(t, 1)].rearrange("a p d -> (a p) d"), x_t[:, p, :]).then_inc(s_x1_out[p], 16)
                sp.dma_start(g.normed_dram[ds(t * P, P), :], normed[:, p, :]).then_inc(s_stored[p], 16)
            pipeline(sp, T, [(load, 0), (store, 4), (load_x, 2)])
            for p in (0, 1):
                sp.wait_ge(s_stored[p], 16 * (T // 2) + 16)
                sp.wait_ge(s_x1_out[p], 16 * (T // 2) + 16)

        @block.vector
        def _(dve):
            dve.sem_inc(s_product, 2)
            dve.sem_inc(s_inv, 2)
            dve.sem_inc(s_sums, 2)
            dve.sem_inc(s_logits_read, 2)
            dve.wait_ge(s_gate, 32)
            dve.tensor_scalar(order[:], g.col_id[:, 0:X], -1.0, float(X), ALU.mult, ALU.add).then_inc(s_order, 1)
            dve.wait_ge(s_order, 1)

            def low(t, p, m):
                if isinstance(t, int) and t == T - 1:
                    dve.wait_ge(s_x1_out[p], 16 * m + 16)
                    dve.memset(x_t[:, p, :], 0.0).then_inc(s_x_pad, 1)
                dve.wait_ge(s_high, t + 1)
                dve.tensor_tensor(weights[:, p, 1], leaky[:, p], weights[:, p, 0].bitcast(F32), ALU.subtract).then_inc(s_weights, 1)

            def add_sides(t, p, m):
                dve.wait_ge(s_left, t + 1)
                left = ps_left[:].unsqueeze(1).broadcast_to([P, T, P])
                right = g.sides[:, :, 1:2].broadcast_to([P, T, P])
                link = chain(dve, s_sums, t, 2, 2)
                link(dve.tensor_tensor(sums[:], left, right, ALU.add))
                link(dve.scalar_tensor_tensor(leaky[:, p], sums[:], NEG_SLOPE, sums[:], ALU.mult, ALU.max))

            def diagonal(t, p, m):
                dve.tensor_scalar(diag[:, p, :], g.ident[:], g.sides[:, ds(t, 1), 0:1].rearrange("p a b -> p (a b)"), None, ALU.mult).then_inc(s_diag, 1)

            def finish(t, p, m):
                dve.wait_ge(s_attended, t + 1)
                link = chain(dve, s_inv, t, 2, 2)
                link(dve.tensor_scalar(rowsum[:, p:p + 1], ps_rowsum[:, 0:1], GAT_EPS, None, ALU.add))
                link(dve.reciprocal(inv[:, p:p + 1], rowsum[:, p:p + 1]))
                dve.tensor_scalar(below[:], ps_h[:, p, :], inv[:, p:p + 1], 0.0, ALU.mult, ALU.min).then_inc(s_below, 1)
                dve.wait_ge(s_elu_parts, 2 * t + 2)
                link = chain(dve, s_x1, t, 2)
                x1 = x_t[:, p, :]
                dve.wait_ge(s_x[p], 16 * m + 16)
                link(dve.scalar_tensor_tensor(elu[:], below[:], -1.0, above[:], ALU.add, ALU.add))
                link(dve.tensor_tensor(x1, x1, elu[:], ALU.add), g.always)
                link = chain(dve, s_stats, t, 3)
                layer_stats(dve, g, link, [x_t[:, p, a:a + HALF] for a in (0, HALF)], stats[:], mean_var[:])
                dve.wait_ge(s_std, 2 * t + 1)
                dve.reciprocal(rstd[:], std[:]).then_inc(s_std, 1)
                dve.wait_ge(s_std, 2 * t + 2)
                dve.wait_ge(s_stored[p], m * 16 + 16)
                dve.wait_ge(s_turn, t + 1)
                dve.tensor_scalar(normed[:, p, :], x1, mean_var[:, 0:1], rstd[:, 0:1], ALU.subtract, ALU.mult).then_inc(s_normed, 1)

            def route(t, p, m):
                dve.wait_ge(s_logits, t + 1)
                link = chain(dve, s_logits_read, t, 2, 2)
                link(dve.tensor_tensor(logits[:], ps_turn[:, 0:X], gate_b[:], ALU.add))
                link(dve.tensor_reduce(neg_max[:], logits[:], AX, ALU.max, negate=True))
                dve.wait_ge(s_exps, t + 1)
                link = chain(dve, s_route, t, 5)
                link(dve.reciprocal(g.route_p[:, ds(t, 1)], exp_sum[:]))
                link(dve.tensor_reduce(exp_max[:], exps[:], AX, ALU.max))
                link(dve.scalar_tensor_tensor(ranked[:], exps[:], exp_max[:, 0:1], order[:], ALU.is_ge, ALU.mult))
                link(dve.tensor_reduce(best[:], ranked[:], AX, ALU.max))
                link(dve.tensor_scalar(flat(g.chosen[:, ds(t, 1), :]), ranked[:], best[:, 0:1], None, ALU.is_equal))
            pipeline(dve, T, [(low, 2), (add_sides, 1), (diagonal, 0), (route, 4), (finish, 3)])

        @block.gpsimd
        def _(pool):
            def weigh(t, p, m):
                pool.wait_ge(s_exp, t + 1)
                pool.wait_ge(s_counts[p], m * 16 + 16)
                pool.tensor_tensor(leaky[:, p], leaky[:, p], counts[:, p], ALU.mult).then_inc(s_product, 1)
            pipeline(pool, T, [(weigh, 0)])

        @block.scalar
        def _(act):
            for p in (0, 1):
                act.sem_inc(s_stored[p], 16)
                act.sem_inc(s_x1_out[p], 16)

            def high(t, p, m):
                act.wait_ge(s_product, t + 3)
                act.activation(weights[:, p, 0], leaky[:, p], ACT.Copy).then_inc(s_high, 1)

            def exponent(t, p, m):
                act.wait_ge(s_sums, 2 * t + 4)
                act.activation(leaky[:, p], leaky[:, p], ACT.Exp, scale=-1.0).then_inc(s_exp, 1)

            def elu_parts(t, p, m):
                act.wait_ge(s_below, t + 1)
                act.activation(above[:], ps_h[:, p, :], ACT.Relu, scale=inv[:, p:p + 1]).then_inc(s_elu_parts, 1)
                act.activation(below[:], below[:], ACT.Exp).then_inc(s_elu_parts, 1)

            def root(t, p, m):
                act.wait_ge(s_stats, 3 * t + 3)
                act.activation(std[:], mean_var[:, 1:2], ACT.Sqrt, bias=g.eps[:, 0:1]).then_inc(s_std, 1)

            def take_turned(t, p, m):
                act.wait_ge(s_turn, t + 3)
                act.activation(normed_t[:].rearrange("p k c -> p (k c)"), ps_turn[:], ACT.Copy).then_inc(s_turned, 1)

            def exps_of(t, p, m):
                act.wait_ge(s_logits_read, 2 * t + 4)
                act.activation(exps[:], logits[:], ACT.Exp, bias=neg_max[:, 0:1], accum_out=exp_sum[:]).then_inc(s_exps, 1)
            pipeline(act, T, [(high, 2), (exponent, 1), (exps_of, 4), (elu_parts, 3), (root, 3), (take_turned, 3)])

        @block.tensor
        def _(pe):
            pe.sem_inc(s_turn, 2)
            pe.wait_ge(s_gate, 32)

            def attend(t, p, m):
                pe.wait_ge(s_weights, t + 1)
                for j in range(T):
                    products(pe, ps_h[:, p, :], lambda s, j: weights[:, p, s, j, :], lambda s, j: nodes[:, j, s, :], j, j == 0, j == T - 1)
                pe.wait_ge(s_inv, 2 * t + 2)
                for j in range(T):
                    for s in (0, 1):
                        last = pe.matmul(ps_rowsum[:], weights[:, p, s, j, :], g.ones_r[:, 0:2], start=(j == 0 and s == 0), stop=(j == T - 1 and s == 1))
                last.then_inc(s_attended, 1)

            def left(t, p, m):
                pe.wait_ge(s_diag, t + 1)
                pe.wait_ge(s_sums, 2 * t + 2)
                pe.matmul(ps_left[:], g.ones[:], diag[:, p, :], start=True, stop=True).then_inc(s_left, 1)

            def turn(t, p, m):
                pe.wait_ge(s_normed, t + 1)
                pe.wait_ge(s_logits_read, 2 * t + 2)
                for k in range(K):
                    last = pe.transpose(ps_turn[:, k * P:(k + 1) * P], normed[:, p, k * P:(k + 1) * P], g.ident[:])
                last.then_inc(s_turn, 1)

            def gate(t, p, m):
                pe.wait_ge(s_turned, t + 1)
                for k in range(K):
                    last = pe.matmul(ps_turn[:, 0:X], normed_t[:, k, :], gate_w[:, k, :], start=(k == 0), stop=(k == K - 1))
                last.then_inc(s_logits, 1)
            pipeline(pe, T, [(gate, 4), (attend, 2), (left, 0), (turn, 3)])


def expert_phase(nc, g, w1, b1, w2, b2):
    T, K, D, X, NP, S = g.T, g.K, g.D, g.X, g.NP, g.slot_tiles
    M = w1.shape[2]
    KM = M // P
    with ExitStack() as ctx:
        sb, ps, sem = makers(ctx, nc, "expert")
        rank = sb("rank", [P, T, X])
        total = sb("total", [P, T, X])
        base = sb("base", [P, T + 1, X])
        tiles_i = sb("tiles_i", [P, X], I32)
        n_tiles = sb("n_tiles", [P, X])
        ends = sb("ends", [P, X])
        first_slot = sb("first_slot", [P, X])
        place = sb("place", [P, T, X])
        slot_f = sb("slot_f", [P, T])
        passed = sb("passed", [1, S, X])
        expert_f = sb("expert_f", [1, S])
        expert_i = sb("expert_i", [1, S], I32)
        pairs_i = sb("pairs_i", [1, 1], I32)
        unused = sb("unused", [P, D])
        no_token = sb("no_token", [S, P], I32)
        tokens = sb("tokens", [P, S], I32)
        token_col = sb("token_col", [P, 2], I32)
        w1_t = sb("w1_t", [P, 2, K, M])
        w2_t = sb("w2_t", [P, 2, KM, D])
        b1_t = sb("b1_t", [1, 2, M])
        b2_t = sb("b2_t", [1, 2, D])
        rows = sb("rows", [P, 2, D])
        rows_t = sb("rows_t", [P, 2, K, P])
        hidden = sb("hidden", [P, 2, M])
        hidden_t = sb("hidden_t", [P, KM, P])
        y = sb("y", [P, 2, D])
        ps_turn = ps("ps_turn", [P, D])
        ps_hidden = ps("ps_hidden", [P, M])
        ps_hidden_t = ps("ps_hidden_t", [P, M])
        ps_y = ps("ps_y", [P, 2, D])

        s_sums = sem("s_sums")
        s_place = sem("s_place")
        s_clear = sem("s_clear")
        s_cleared = sem("s_cleared")
        s_unused = [sem("s_unused0"), sem("s_unused1")]
        s_scatter = sem("s_scatter")
        s_tokens = sem("s_tokens")
        s_token_col = sem("s_token_col")
        s_rows = [sem("s_rows0"), sem("s_rows1")]
        s_w1 = [sem("s_w1_0"), sem("s_w1_1")]
        s_w2 = [sem("s_w2_0"), sem("s_w2_1")]
        s_turn = sem("s_turn")
        s_turned = sem("s_turned")
        s_hidden = sem("s_hidden")
        s_relu = sem("s_relu")
        s_hidden_t = sem("s_hidden_t")
        s_hidden_taken = sem("s_hidden_taken")
        s_y = sem("s_y")
        s_y_taken = sem("s_y_taken")
        s_y_out = [sem("s_y_out0"), sem("s_y_out1")]
        s_stored = sem("s_stored")
        block = ctx.enter_context(nc.Block())
        PLACE = 19 + T + X

        @block.sync
        def _(sp):
            sp.wait_ge(s_clear, 1)
            sp.dma_start(g.slot_token_dram.rearrange("(s p) a -> s (p a)", p=P), no_token[:]).then_inc(s_cleared, 16)
            sp.wait_ge(s_scatter, 16 * T)
            sp.dma_start(tokens[:], g.slot_token_dram.rearrange("(s p) a -> p (s a)", p=P), allow_slow_non_contiguous=True).then_inc(s_tokens, 16)
            sp.sem_inc(s_hidden, 2)
            sp.sem_inc(s_y, 2)

            def load(t, p, m):
                expert = sp.value_load(expert_i[0:1, ds(t, 1)], min_val=0, max_val=X - 1)
                sp.wait_ge(s_hidden, t + 1)
                sp.dma_start(w1_t[:, p], w1[ds(expert, 1)].rearrange("a (k p) m -> p (a k) m", p=P)).then_inc(s_w1[p], 16)
                sp.dma_start(b1_t[0:1, p, :], b1[ds(expert, 1), :]).then_inc(s_w1[p], 16)
                sp.wait_ge(s_y, t + 1)
                sp.dma_start(w2_t[:, p], w2[ds(expert, 1)].rearrange("a (k p) d -> p (a k) d", p=P)).then_inc(s_w2[p], 16)
                sp.dma_start(b2_t[0:1, p, :], b2[ds(expert, 1), :]).then_inc(s_w2[p], 16)
            pairs = sp.value_load(pairs_i[0:1, 0:1], min_val=0, max_val=(S - T) // 2) + T // 2
            pipeline(sp, S, [(load, 0)], pairs)
            sp.wait_ge(s_clear, 2)
            with sp.Fori(0, pairs) as _:
                for p in (0, 1):
                    sp.sem_inc(s_unused[p], 16)
            with sp.Fori(pairs, S // 2) as i:
                for p in (0, 1):
                    sp.dma_start(g.y_dram[ds((2 * i + p) * P, P), :], unused[:]).then_inc(s_unused[p], 16)
            for p in (0, 1):
                sp.wait_ge(s_unused[p], 16 * (S // 2))

        @block.gpsimd
        def _(pool):
            pool.memset(no_token[:], 0).then_inc(s_clear, 1)
            pool.memset(unused[:], 0.0).then_inc(s_clear, 1)
            pool.wait_ge(s_place, PLACE)
            pool.wait_ge(s_cleared, 16)
            for t in range(T):
                pool.indirect_dma_start(g.slot_token_dram, bass.IndirectOffsetOnAxis(g.slot[:, t:t + 1], 0),
                                        g.token_id[:, t:t + 1], None).then_inc(s_scatter, 16)
            pool.wait_ge(s_tokens, 16)

            def gather(t, p, m):
                pool.wait_ge(s_turn, t + 1)
                pool.tensor_copy(token_col[:, p:p + 1], tokens[:, ds(t, 1)]).then_inc(s_token_col, 1)
                wait_apart(pool, g.always, s_token_col, t + 1)
                pool.indirect_dma_start(rows[:, p, :], None, g.normed_dram, bass.IndirectOffsetOnAxis(token_col[:, p:p + 1], 0)).then_inc(s_rows[p], 16)
            pairs = pool.value_load(pairs_i[0:1, 0:1], min_val=0, max_val=(S - T) // 2) + T // 2
            pipeline(pool, S, [(gather, 0)], pairs)

        @block.vector
        def _(dve):
            dve.wait_ge(s_sums, 1)
            link = chain(dve, s_place, 0, PLACE)
            chosen = g.chosen[:].rearrange("p t e -> p (t e)")
            link(dve.tensor_copy(rank[:].rearrange("p t e -> p (t e)"), ps_turn[:, 0:T * X]))
            link(dve.tensor_copy(total[:].rearrange("p t e -> p (t e)"), ps_turn[:, HALF:HALF + T * X]))
            link(dve.memset(base[:, 0, :], 0.0))
            for t in range(T):
                link(dve.tensor_tensor(base[:, t + 1, :], base[:, t, :], total[:, t, :], ALU.add))
            link(dve.tensor_scalar(tiles_i[:], base[:, T, :], float(P - 1), None, ALU.add))
            link(dve.tensor_scalar(tiles_i[:], tiles_i[:], 7, None, ALU.arith_shift_right))
            link(dve.tensor_copy(n_tiles[:], tiles_i[:]))
            link(dve.tensor_copy(ends[:, 0:1], n_tiles[:, 0:1]))
            for e in range(1, X):
                link(dve.tensor_tensor(ends[:, e:e + 1], ends[:, e - 1:e], n_tiles[:, e:e + 1], ALU.add))
            link(dve.tensor_tensor(first_slot[:], ends[:], n_tiles[:], ALU.subtract))
            link(dve.tensor_scalar(first_slot[:], first_slot[:], float(P), None, ALU.mult))
            link(dve.tensor_tensor(place[:], rank[:], base[:, 0:T, :], ALU.add))
            link(dve.tensor_tensor(place[:], place[:], first_slot[:].unsqueeze(1).broadcast_to([P, T, X]), ALU.add))
            link(dve.tensor_tensor(place[:], place[:], g.chosen[:], ALU.mult))
            link(dve.tensor_reduce(slot_f[:], place[:], AX, ALU.add))
            link(dve.tensor_copy(g.slot[:], slot_f[:]))
            link(dve.tensor_tensor(passed[:], ends[0:1, :].unsqueeze(1).broadcast_to([1, S, X]),
                                   g.col_id[0:1, 0:S].unsqueeze(2).broadcast_to([1, S, X]), ALU.is_le))
            link(dve.tensor_reduce(expert_f[:], passed[:], AX, ALU.add))
            link(dve.tensor_scalar(expert_i[:], expert_f[:], float(X - 1), None, ALU.min))
            link(dve.tensor_scalar(pairs_i[:], ends[0:1, X - 1:X], 1.0, None, ALU.add))
            link(dve.tensor_scalar(pairs_i[:], pairs_i[:], 1, None, ALU.arith_shift_right))
            link(dve.tensor_scalar(pairs_i[:], pairs_i[:], T // 2, None, ALU.subtract))

            dve.wait_ge(s_place, PLACE)

            def take_hidden_t(t, p, m):
                dve.wait_ge(s_hidden_t, t + 1)
                dve.tensor_copy(hidden_t[:].rearrange("p k c -> p (k c)"), ps_hidden_t[:]).then_inc(s_hidden_taken, 1)

            def take_y(t, p, m):
                dve.wait_ge(s_y, t + 3)
                dve.wait_ge(s_y_out[p], m * 16 + 16)
                dve.tensor_copy(y[:, p, :], ps_y[:, p, :]).then_inc(s_y_taken, 1)
            pairs = dve.value_load(pairs_i[0:1, 0:1], min_val=0, max_val=(S - T) // 2) + T // 2
            pipeline(dve, S, [(take_hidden_t, 0), (take_y, 1)], pairs)

        @block.scalar
        def _(act):
            for p in (0, 1):
                act.sem_inc(s_y_out[p], 16)

            def take_turned(t, p, m):
                act.wait_ge(s_turn, t + 3)
                act.wait_ge(s_hidden, t + 1)
                act.activation(rows_t[:, p].rearrange("p k c -> p (k c)"), ps_turn[:], ACT.Copy).then_inc(s_turned, 1)

            def relu(t, p, m):
                act.wait_ge(s_hidden, t + 3)
                act.activation(hidden[:, p, :], ps_hidden[:], ACT.Relu).then_inc(s_relu, 1)

            def store(t, p, m):
                act.wait_ge(s_y_taken, t + 3)
                act.dma_start(g.y_dram[ds(t * P, P), :], y[:, p, :]).then_inc(s_y_out[p], 16)
            act.wait_ge(s_place, PLACE)
            pairs = act.value_load(pairs_i[0:1, 0:1], min_val=0, max_val=(S - T) // 2) + T // 2
            pipeline(act, S, [(take_turned, 0), (relu, 1), (store, 3)], pairs)
            for p in (0, 1):
                act.wait_ge(s_y_out[p], 16 * pairs + 16)
            act.sem_inc(s_stored, 1)

        @block.tensor
        def _(pe):
            chosen = g.chosen[:].rearrange("p t e -> p (t e)")
            pe.matmul(ps_turn[:, 0:T * X], g.before[:], chosen, start=True, stop=True)
            pe.matmul(ps_turn[:, HALF:HALF + T * X], g.ones[:], chosen, start=True, stop=True).then_inc(s_sums, 1)
            pe.wait_ge(s_place, 2)
            pe.sem_inc(s_turn, 2)
            pe.sem_inc(s_turned, 1)

            def turn(t, p, m):
                pe.wait_ge(s_rows[p], m * 16 + 16)
                pe.wait_ge(s_turned, t + 1)
                for k in range(K):
                    last = pe.transpose(ps_turn[:, k * P:(k + 1) * P], rows[:, p, k * P:(k + 1) * P], g.ident[:])
                last.then_inc(s_turn, 1)

            def first(t, p, m):
                pe.wait_ge(s_w1[p], m * 32 + 32)
                pe.wait_ge(s_turned, t + 2)
                pe.wait_ge(s_relu, t + 1)
                pe.matmul(ps_hidden[:], g.ones[0:1, :], b1_t[0:1, p, :], start=True, stop=False)
                for k in range(K):
                    last = pe.matmul(ps_hidden[:], rows_t[:, p, k, :], w1_t[:, p, k, :], start=False, stop=(k == K - 1))
                last.then_inc(s_hidden, 1)

            def turn_hidden(t, p, m):
                pe.wait_ge(s_relu, t + 2)
                pe.wait_ge(s_hidden_taken, t + 1)
                for k in range(KM):
                    last = pe.transpose(ps_hidden_t[:, k * P:(k + 1) * P], hidden[:, p, k * P:(k + 1) * P], g.ident[:])
                last.then_inc(s_hidden_t, 1)

            def second(t, p, m):
                pe.wait_ge(s_w2[p], m * 32 + 32)
                pe.wait_ge(s_hidden_taken, t + 2)
                pe.wait_ge(s_y_taken, t + 1)
                for a in range(0, D, HALF):
                    pe.matmul(ps_y[:, p, a:a + HALF], g.ones[0:1, :], b2_t[0:1, p, a:a + HALF], start=True, stop=False)
                    for k in range(KM):
                        last = pe.matmul(ps_y[:, p, a:a + HALF], hidden_t[:, k, :], w2_t[:, p, k, a:a + HALF], start=False, stop=(k == KM - 1))
                last.then_inc(s_y, 1)
            pe.sem_inc(s_relu, 1)
            pe.sem_inc(s_hidden_taken, 1)
            pe.sem_inc(s_y_taken, 2)
            pe.wait_ge(s_place, PLACE)
            pairs = pe.value_load(pairs_i[0:1, 0:1], min_val=0, max_val=(S - T) // 2) + T // 2
            pipeline(pe, S, [(turn_hidden, 2), (turn, 0), (first, 1), (second, 2)], pairs)


def neighbour_phase(nc, g, n, w_source, w, nodes, ffn_sources):
    T, K, D = g.T, g.K, g.D
    with ExitStack() as ctx:
        sb, ps, sem = makers(ctx, nc, f"neighbour{n}")
        raw = sb("raw", [P, 2, D])
        split = Split((sb, ps, sem), "w", raw, w)
        feat_t = sb("feat_t", [P, 2, 2, K, P], F32R)
        ps_turn = ps("ps_turn", [P, D])
        ps_out = ps("ps_out", [P, 2, D])
        s_out = sem("s_out")
        s_kept_high = sem("s_kept_high")
        s_kept = sem("s_kept")
        s_feat = [sem("s_feat0"), sem("s_feat1")]
        s_feat_t = sem("s_feat_t")
        if n == 1:
            rows = sb("rows", [P, g.w_tiles, D])
            w_scale = sb("w_scale", [P, D // W_BLOCK])
            w_inv = sb("w_inv", [P, D // W_BLOCK])
            s_rows = sem("s_rows")
            s_quant = sem("s_quant")
            s_rows_out = sem("s_rows_out")
        else:
            widest = sb("widest", [P, 1])
            s_widest_turn = sem("s_widest_turn")
            slot_col = sb("slot_col", [P, 2], I32)
            y = sb("y", [P, 2, D])
            x2 = sb("x2", [P, 2, D])
            stats = sb("stats", [P, 12])
            mean_var = sb("mean_var", [P, 2])
            std = sb("std", [P, 1])
            rstd = sb("rstd", [P, 1])
            normed = sb("normed", [P, 2, D])
            s_deg = sem("s_deg")
            s_col = sem("s_col")
            s_y = [sem("s_y0"), sem("s_y1")]
            s_x = [sem("s_x0"), sem("s_x1")]
            s_added = sem("s_added")
            s_stats = sem("s_stats")
            s_std = sem("s_std")
            s_normed = sem("s_normed")
            s_turn = sem("s_turn")
            s_high = sem("s_high")
            s_x2_out = [sem("s_x2_out0"), sem("s_x2_out1")]
        block = ctx.enter_context(nc.Block())

        @block.sync
        def _(sp):
            def load(t, p, m):
                sp.wait_ge(s_out, t + 1)
                sp.dma_start(feat_t[:, p].rearrange("p s k c -> p (s k c)").bitcast(F32), g.nodes_t_dram[1][ds(t, 1)].rearrange("a p n -> (a p) n")).then_inc(s_feat[p], 16)

            def load_x1(t, p, m):
                sp.wait_ge(s_x2_out[p], 16 * m + 16)
                sp.dma_start(x2[:, p, :], g.x1_dram[ds(t, 1)].rearrange("a p d -> (a p) d")).then_inc(s_x[p], 16)

            def store_x2(t, p, m):
                sp.wait_ge(s_normed, t + 1)
                sp.dma_start(g.x2_dram[ds(t, 1)].rearrange("a p d -> (a p) d"), x2[:, p, :]).then_inc(s_x2_out[p], 16)

            def store_features(t, p, m):
                sp.wait_ge(s_feat_t, t + 2)
                sp.dma_start(g.nodes_t_dram[0][ds(t, 1)].rearrange("a p n -> (a p) n"), feat_t[:, p].rearrange("p s k c -> p (s k c)").bitcast(F32)).then_inc(s_feat[p], 16)
            split.load(sp, w_source)
            if n:
                at = 0
                for source in ffn_sources:
                    rows_of = source.rearrange("(o p) i -> p o i", p=P)
                    width = rows_of.shape[1] * rows_of.shape[2]
                    sp.dma_start(flat(rows)[:, at:at + width].rearrange("p (o i) -> p o i", i=rows_of.shape[2]), rows_of).then_inc(s_rows, 16)
                    at += width
                pipeline(sp, T, [(load, 0)])
                sp.wait_ge(s_quant, 7 * g.w_tiles)
                sp.dma_start(g.w_rows_dram, rows[:]).then_inc(s_rows_out, 16)
                sp.wait_ge(s_rows_out, 16)
            else:
                pipeline(sp, T, [(load_x1, 0), (store_x2, 1), (store_features, 1)])
                for p in (0, 1):
                    sp.wait_ge(s_x2_out[p], 16 * (T // 2) + 16)
                    sp.wait_ge(s_feat[p], 16 * (T // 2) + 16)

        if n == 0:
            @block.gpsimd
            def _(pool):
                def gather(t, p, m):
                    pool.wait_ge(s_added, t + 1)
                    pool.tensor_copy(slot_col[:, p:p + 1], g.slot[:, ds(t, 1)]).then_inc(s_col, 1)
                    wait_apart(pool, g.always, s_col, t + 1)
                    pool.indirect_dma_start(y[:, p, :], None, g.y_dram, bass.IndirectOffsetOnAxis(slot_col[:, p:p + 1], 0)).then_inc(s_y[p], 16)
                pipeline(pool, T, [(gather, 0)])

        @block.vector
        def _(dve):
            if n == 0:
                dve.sem_inc(s_added, 2)
                link = chain(dve, s_deg, 0, 5)
                link(dve.tensor_reduce(widest[:], g.deg[:], AX, ALU.max))
                dve.wait_ge(s_widest_turn, 1)
                link(dve.tensor_reduce(widest[0:1, :], ps_turn[0:1, 0:P], AX, ALU.max))
                link(dve.tensor_scalar(g.many_i[:], widest[0:1, :], 4096.0, None, ALU.is_gt))
                link(dve.tensor_scalar(g.deg[:], g.deg[:], 1.0, None, ALU.max))
                link(dve.reciprocal(g.deg[:], g.deg[:]))
            split.low(dve)

            def add(t, p, m):
                x = x2[:, p, :]
                dve.wait_ge(s_x[p], m * 16 + 16)
                dve.wait_ge(s_y[p], m * 16 + 16)
                dve.scalar_tensor_tensor(x, y[:, p, :], g.route_p[:, ds(t, 1)], x, ALU.mult, ALU.add).then_inc(s_added, 1)
                wait_apart(dve, g.always, s_added, t + 3)
                link = chain(dve, s_stats, t, 3)
                layer_stats(dve, g, link, [x2[:, p, a:a + HALF] for a in (0, HALF)], stats[:], mean_var[:])
                dve.wait_ge(s_std, 2 * t + 1)
                dve.reciprocal(rstd[:], std[:]).then_inc(s_std, 1)
                dve.wait_ge(s_std, 2 * t + 2)
                dve.tensor_scalar(normed[:, p, :], x, mean_var[:, 0:1], rstd[:, 0:1], ALU.subtract, ALU.mult).then_inc(s_normed, 1)

            def low(t, p, m):
                dve.wait_ge(s_high, t + 1)
                dve.tensor_tensor(feat_t[:, p, 1].rearrange("p k c -> p (k c)"), ps_turn[:],
                                  feat_t[:, p, 0].rearrange("p k c -> p (k c)").bitcast(F32), ALU.subtract).then_inc(s_feat_t, 1)

            def keep(t, p, m):
                dve.wait_ge(s_kept_high, t + 1)
                dve.tensor_tensor(flat(nodes[:, ds(t, 1), 1, :]), ps_out[:, p, :], flat(nodes[:, ds(t, 1), 0, :]).bitcast(F32), ALU.subtract).then_inc(s_kept, 1)

            def quantise_weights(t, p, m):
                if isinstance(t, int) and t >= g.w_tiles:
                    return
                link = chain(dve, s_quant, t, 7)
                value = flat(rows[:, ds(t, 1), :]).rearrange("p (b c) -> p b c", c=W_BLOCK)
                wide = [P, D // W_BLOCK, W_BLOCK]
                scale = w_scale[:].unsqueeze(2).broadcast_to(wide)
                inv = w_inv[:].unsqueeze(2).broadcast_to(wide)
                link(dve.tensor_reduce(w_scale[:], value, AX, ALU.max, apply_absolute_value=True))
                link(dve.tensor_scalar(w_scale[:], w_scale[:], 1.0 / W_MAX, 1e-12, ALU.mult, ALU.max))
                link(dve.reciprocal(w_inv[:], w_scale[:]))
                link(dve.tensor_tensor(value, value, inv, ALU.mult))
                link(dve.tensor_scalar(value, value, ROUND, ROUND, ALU.add, ALU.subtract))
                link(dve.tensor_scalar(value, value, -W_MAX - 1.0, W_MAX, ALU.max, ALU.min))
                link(dve.tensor_tensor(value, value, scale, ALU.mult))
            if n == 0:
                pipeline(dve, T, [(low, 1), (add, 0), (keep, 2)])
            else:
                assert g.w_tiles <= T
                dve.wait_ge(s_rows, 16 * len(ffn_sources))
                pipeline(dve, T, [(keep, 2), (quantise_weights, 0)], last_apart=True)

        @block.scalar
        def _(act):
            split.high(act)

            def root(t, p, m):
                act.wait_ge(s_stats, 3 * t + 3)
                act.activation(std[:], mean_var[:, 1:2], ACT.Sqrt, bias=g.eps[:, 0:1]).then_inc(s_std, 1)

            def high(t, p, m):
                act.wait_ge(s_turn, t + 1)
                act.wait_ge(s_feat[p], 16 * m + 16)
                act.activation(feat_t[:, p, 0].rearrange("p k c -> p (k c)"), ps_turn[:], ACT.Copy).then_inc(s_high, 1)

            def keep_high(t, p, m):
                act.wait_ge(s_out, t + 3)
                act.activation(flat(nodes[:, ds(t, 1), 0, :]), ps_out[:, p, :], ACT.Copy).then_inc(s_kept_high, 1)
            if n == 0:
                for p in (0, 1):
                    act.sem_inc(s_feat[p], 16)
                    act.sem_inc(s_x2_out[p], 16)
            pipeline(act, T, [(keep_high, 2)] if n else [(high, 1), (root, 0), (keep_high, 2)])

        @block.tensor
        def _(pe):
            pe.sem_inc(s_kept, 2)
            pe.sem_inc(s_out, 2)
            if n == 0:
                pe.wait_ge(s_deg, 1)
                pe.transpose(ps_turn[0:1, 0:P], widest[:], g.ident[:]).then_inc(s_widest_turn, 1)
                pe.wait_ge(s_deg, 2)
                pe.sem_inc(s_feat_t, 1)

            def turn(t, p, m):
                pe.wait_ge(s_normed, t + 1)
                pe.wait_ge(s_feat_t, t + 1)
                for k in range(K):
                    last = pe.transpose(ps_turn[:, k * P:(k + 1) * P], normed[:, p, k * P:(k + 1) * P], g.ident[:])
                last.then_inc(s_turn, 1)

            def multiply(t, p, m):
                if n:
                    pe.wait_ge(s_feat[p], 16 * m + 16)
                else:
                    pe.wait_ge(s_feat_t, t + 2)
                pe.wait_ge(s_kept, t + 1)
                for k in range(K):
                    if isinstance(t, int) and t == 0:
                        split.ready(pe, k)
                    last = products(pe, ps_out[:, p, :], lambda s, k: feat_t[:, p, s, k, :], lambda s, k: w[:, s, k, :], k, k == 0, k == K - 1)
                last.then_inc(s_out, 1)
            pipeline(pe, T, [(multiply, 1)] if n else [(turn, 0), (multiply, 1)])


def aggregate_phase(nc, g, n, w_source, bias, w, nodes):
    T, K, D = g.T, g.K, g.D
    last = n == 1
    with ExitStack() as ctx:
        sb, ps, sem = makers(ctx, nc, f"aggregate{n}")
        work = sb("work", [P, 2, D])
        split = Split((sb, ps, sem), "w", work, w)
        bias_rows = sb("bias_rows", [P, D])
        counts_raw = sb("counts_raw", [P, T, P])
        counts = sb("counts", [P, 2, T, P], F32R)
        counts_rest = sb("counts_rest", [P, T, P], F32R)
        feat_t = sb("feat_t", [P, 2, 2, K, P], F32R)
        x3 = sb("x3", [P, 2, D]) if last else None
        out_t = None if last else sb("out_t", [P, 2, K, P], F32R)
        stats = sb("stats", [P, 12])
        std = sb("std", [P, 1])
        rstd = sb("rstd", [P, 1])
        ps_sum = ps("ps_sum", [P, D])
        ps_own = ps("ps_own", [P, D])
        ps_turn = ps("ps_turn", [P, D])

        s_bias = sem("s_bias")
        s_raw = sem("s_raw")
        s_counts_high = sem("s_counts_high")
        s_counts = sem("s_counts")
        s_feat = [sem("s_feat0"), sem("s_feat1")]
        s_summed = sem("s_summed")
        s_mean = sem("s_mean")
        s_own = sem("s_own")
        s_out = sem("s_out")
        s_relu = sem("s_relu")
        s_turn = sem("s_turn")
        s_high = sem("s_high")
        s_out_t = sem("s_out_t")
        s_x2 = [sem("s_x2_0"), sem("s_x2_1")]
        s_x3 = sem("s_x3")
        s_stored = [sem("s_stored0"), sem("s_stored1")]
        s_std = sem("s_std")
        s_largest = sem("s_largest")
        block = ctx.enter_context(nc.Block())

        @block.sync
        def _(sp):
            sp.sem_inc(s_own, 2)
            sp.sem_inc(s_counts, 1)

            def load(t, p, m):
                sp.wait_ge(s_counts, t + 1)
                sp.dma_start(counts_raw[:].rearrange("p j c -> p (j c)"), g.turned_dram[ds(t, 1)].rearrange("a p n -> (a p) n")).then_inc(s_raw, 16)
                sp.wait_ge(s_own, t + 1)
                sp.dma_start(feat_t[:, p].rearrange("p s k c -> p (s k c)").bitcast(F32), g.nodes_t_dram[n][ds(t, 1)].rearrange("a p n -> (a p) n")).then_inc(s_feat[p], 16)

            def load_x2(t, p, m):
                sp.wait_ge(s_stored[p], 16 * m + 16)
                sp.dma_start(x3[:, p, :], g.x2_dram[ds(t, 1)].rearrange("a p d -> (a p) d")).then_inc(s_x2[p], 16)

            def store_x3(t, p, m):
                sp.wait_ge(s_largest, 8 * t + 7)
                sp.dma_start(g.x3_dram[ds(t, 1)].rearrange("a p d -> (a p) d"), x3[:, p, :]).then_inc(s_stored[p], 16)

            def store_out(t, p, m):
                sp.wait_ge(s_out_t, t + 2)
                sp.dma_start(g.nodes_t_dram[1][ds(t, 1)].rearrange("a p n -> (a p) n"), out_t[:].rearrange("p s k c -> p (s k c)").bitcast(F32)).then_inc(s_stored[0], 16)
            split.load(sp, w_source)
            sp.dma_start(bias_rows[:], bias.rearrange("(a d) -> a d", a=1).broadcast_to([P, D])).then_inc(s_bias, 16)
            if last:
                pipeline(sp, T, [(load, 0), (load_x2, 1), (store_x3, 2)])
                for p in (0, 1):
                    sp.wait_ge(s_stored[p], 16 * (T // 2) + 16)
            else:
                pipeline(sp, T, [(load, 0), (store_out, 3)])
                sp.wait_ge(s_stored[0], 16 * T + 16)

        @block.scalar
        def _(act):
            for p in (0, 1):
                act.sem_inc(s_stored[p], 16)

            def counts_high(t, p, m):
                act.wait_ge(s_raw, 16 * t + 16)
                act.wait_ge(s_summed, t + 1)
                act.activation(counts[:, p], counts_raw[:], ACT.Copy).then_inc(s_counts_high, 1)

            def relu(t, p, m):
                act.wait_ge(s_out, t + 2)
                act.activation(work[:, 1, :], work[:, 0, :], ACT.Relu).then_inc(s_relu, 1)

            def out_high(t, p, m):
                act.wait_ge(s_turn, t + 1)
                act.wait_ge(s_stored[0], 16 * t + 16)
                act.activation(out_t[:, 0].rearrange("p k c -> p (k c)"), ps_turn[:], ACT.Copy).then_inc(s_high, 1)

            def root(t, p, m):
                act.wait_ge(s_largest, 8 * t + 3)
                act.activation(std[:], g.mean_var[:, 1:2], ACT.Sqrt, bias=g.eps[:, 0:1]).then_inc(s_std, 1)
            split.high(act)
            pipeline(act, T, [(counts_high, 0), (root, 1)] if last else [(counts_high, 0), (out_high, 2), (relu, 1)])

        @block.vector
        def _(dve):
            def counts_low(t, p, m):
                dve.wait_ge(s_counts_high, t + 1)
                dve.tensor_tensor(counts_rest[:], counts_raw[:], counts[:, p].bitcast(F32), ALU.subtract).then_inc(s_counts, 1)

            def mean(t, p, m):
                dve.wait_ge(s_summed, t + 3)
                if not last:
                    dve.wait_ge(s_relu, t + 1)
                dve.scalar_tensor_tensor(work[:, 0, :], ps_sum[:], g.deg[:, ds(t, 1)], bias_rows[:], ALU.mult, ALU.add).then_inc(s_mean, 1)

            def add(t, p, m):
                dve.wait_ge(s_own, t + 3)
                dve.wait_ge(s_mean, t + 2)
                dve.tensor_tensor(work[:, 0, :], work[:, 0, :], ps_own[:], ALU.add).then_inc(s_out, 1)

            def out_low(t, p, m):
                dve.wait_ge(s_high, t + 1)
                dve.tensor_tensor(out_t[:, 1].rearrange("p k c -> p (k c)"), ps_turn[:],
                                  out_t[:, 0].rearrange("p k c -> p (k c)").bitcast(F32), ALU.subtract).then_inc(s_out_t, 1)

            def finish(t, p, m):
                dve.wait_ge(s_out, t + 2)
                dve.wait_ge(s_x2[p], 16 * m + 16)
                dve.tensor_tensor(x3[:, p, :], x3[:, p, :], work[:, 0, :], ALU.add).then_inc(s_x3, 1)
                wait_apart(dve, g.always, s_x3, t + 1)
                link = chain(dve, s_largest, t, 8)
                layer_stats(dve, g, link, [x3[:, p, a:a + HALF] for a in (0, HALF)], stats[:], g.mean_var[:])
                dve.wait_ge(s_std, t + 1)
                link(dve.reciprocal(rstd[:], std[:]))
                link(dve.tensor_copy(g.means[:, ds(t, 1)], g.mean_var[:, 0:1]))
                link(dve.tensor_copy(g.rstds[:, ds(t, 1)], rstd[:]))
                link(dve.tensor_scalar(work[:, 1, :], x3[:, p, :], g.mean_var[:, 0:1], rstd[:, 0:1], ALU.subtract, ALU.mult))
                link(dve.tensor_reduce(g.largest[:, ds(t, 1)], work[:, 1, :], AX, ALU.max, apply_absolute_value=True))
            split.low(dve)
            dve.wait_ge(s_bias, 16)
            pipeline(dve, T, [(mean, 1), (counts_low, 0), (add, 1), (finish, 1)] if last else
                     [(mean, 1), (counts_low, 0), (out_low, 2), (add, 1)])

        @block.tensor
        def _(pe):
            pe.sem_inc(s_summed, 2)
            pe.sem_inc(s_mean, 1)
            pe.sem_inc(s_out, 1)
            pe.sem_inc(s_out_t, 1)
            pe.sem_inc(s_relu, 1)
            more = pe.value_load(g.many_i[0:1, 0:1], min_val=0, max_val=1)

            def add_up(t, p, m):
                pe.wait_ge(s_counts, t + 2)
                pe.wait_ge(s_mean, t + 1)

                def term(left, r, j, start, stop):
                    for a in range(0, D, HALF):
                        last_mm = pe.matmul(ps_sum[:, a:a + HALF], left[:, j, :], nodes[:, j, r, a:a + HALF], start=start, stop=stop)
                    return last_mm
                high = counts[:, p]
                for j in range(T):
                    term(high, 0, j, j == 0, False)
                    if j < T - 1:
                        term(high, 1, j, False, False)
                with pe.Fori(0, more) as _:
                    for j in range(T):
                        term(counts_rest, 0, j, False, False)
                term(high, 1, T - 1, False, True).then_inc(s_summed, 1)

            def turn(t, p, m):
                pe.wait_ge(s_relu, t + 2)
                pe.wait_ge(s_out_t, t + 1)
                for k in range(K):
                    last_mm = pe.transpose(ps_turn[:, k * P:(k + 1) * P], work[:, 1, k * P:(k + 1) * P], g.ident[:])
                last_mm.then_inc(s_turn, 1)

            def own(t, p, m):
                if isinstance(t, int) and t == 0:
                    split.ready(pe)
                pe.wait_ge(s_feat[p], 16 * m + 16)
                pe.wait_ge(s_out, t + 1)
                for k in range(K):
                    last_mm = products(pe, ps_own[:], lambda s, k: feat_t[:, p, s, k, :], lambda s, k: w[:, s, k, :], k, k == 0, k == K - 1)
                last_mm.then_inc(s_own, 1)
            pipeline(pe, T, [(add_up, 1), (own, 1)] if last else [(add_up, 1), (turn, 2), (own, 1)])


def quantised(dve, link, out, value, inv_scale, scale, low, high):
    link(dve.tensor_scalar(out, value, inv_scale, ROUND, ALU.mult, ALU.add))
    link(dve.tensor_scalar(out, out, ROUND, high, ALU.subtract, ALU.min))
    link(dve.tensor_scalar(out, out, low, scale, ALU.max, ALU.mult))


def feed_forward_phase(nc, g, out):
    T, K, D, N = g.T, g.K, g.D, g.N
    I = g.I
    KI = I // P
    BLOCKS = D // P
    with ExitStack() as ctx:
        sb, ps, sem = makers(ctx, nc, "ffn")
        rows = sb("rows", [P, 2, D])
        w_t = sb("w_t", [P, 2, g.w_tiles * BLOCKS, P], F32R)
        x3 = sb("x3", [P, T, D])
        gate_up = sb("gate_up", [P, 2, T, I])
        normed = sb("normed", [P, D])
        normed_t = sb("normed_t", [P, 2, 2, K, P], F32R)
        largest = sb("largest", [P, 3, T])
        widest = sb("widest", [P, 1])
        top = sb("top", [1, 1])
        scales = sb("scales", [P, 5, 2])
        sig = sb("sig", [P, T, I])
        o_t = sb("o_t", [P, 2, 2, KI, P], F32R)
        result = sb("result", [P, 2, D])
        ps_turn = ps("ps_turn", [P, 2, D])
        ps_gate_up = ps("ps_gate_up", [P, 2, HALF])
        ps_scale = ps("ps_scale", [P, HALF])
        ps_down = ps_gate_up

        s_rows = [sem("s_rows0"), sem("s_rows1")]
        s_x3 = sem("s_x3")
        s_w_turn = sem("s_w_turn")
        s_w_high = sem("s_w_high")
        s_w = sem("s_w")
        s_widest = sem("s_widest")
        s_level = sem("s_level")
        s_scaled = sem("s_scaled")
        s_quant = sem("s_quant")
        s_normed = sem("s_normed")
        s_turn = sem("s_turn")
        s_high = sem("s_high")
        s_turned = sem("s_turned")
        s_gate_up = sem("s_gate_up")
        s_gate_up_kept = sem("s_gate_up_kept")
        s_largest = sem("s_largest")
        s_all = sem("s_all")
        s_sig = sem("s_sig")
        s_o = sem("s_o")
        s_o_turn = sem("s_o_turn")
        s_o_high = sem("s_o_high")
        s_o_t = sem("s_o_t")
        s_down = sem("s_down")
        s_result = sem("s_result")
        s_out = [sem("s_out0"), sem("s_out1")]
        block = ctx.enter_context(nc.Block())

        def weight(s, side, k):
            blocks = w_t[:, s, side * KI * K:(side + 1) * KI * K, :]
            return blocks.rearrange("p (i k) c -> p k i c", k=K)[:, k]

        def down_weight(s, k):
            blocks = w_t[:, s, 2 * KI * K:, :]
            return blocks.rearrange("p (o k) c -> p k o c", k=KI)[:, k]

        @block.sync
        def _(sp):
            sp.sem_inc(s_w, 2)

            def load_rows(t, p, m):
                sp.wait_ge(s_w, t + 1)
                sp.dma_start(rows[:, p, :], g.w_rows_dram[:, ds(t, 1), :].rearrange("p a d -> p (a d)")).then_inc(s_rows[p], 16)
            load_rows(0, 0, 0)
            load_rows(1, 1, 0)
            sp.dma_start(x3[:], g.x3_dram.rearrange("t p d -> p t d")).then_inc(s_x3, 16)
            for t in range(2, g.w_tiles):
                load_rows(t, t % 2, t // 2)

            for p in (0, 1):
                sp.sem_inc(s_out[p], 16)

            def store(t, p, m):
                sp.wait_ge(s_result, t + 2)
                if isinstance(t, int) and (t + 1) * P > N:
                    sp.dma_start(out[t * P:N, :], result[0:N - t * P, p, :]).then_inc(s_out[p], 16)
                else:
                    sp.dma_start(out[ds(t * P, P), :], result[:, p, :]).then_inc(s_out[p], 16)
            with sp.Fori(0, T // 2 - 1) as i:
                for p in (0, 1):
                    store(2 * i + p, p, i)
            store(T - 2, 0, T // 2 - 1)
            store(T - 1, 1, T // 2 - 1)
            for p in (0, 1):
                sp.wait_ge(s_out[p], 16 * (T // 2) + 16)

        @block.vector
        def _(dve):
            def w_low(t, p, m):
                dve.wait_ge(s_w_high, t + 1)
                dve.tensor_tensor(w_t[:, 1, ds(t * BLOCKS, BLOCKS), :].rearrange("p b c -> p (b c)"), ps_turn[:, p, :],
                                  w_t[:, 0, ds(t * BLOCKS, BLOCKS), :].rearrange("p b c -> p (b c)").bitcast(F32), ALU.subtract).then_inc(s_w, 1)
            pipeline(dve, g.w_tiles, [(w_low, 0)])

            def scale_of(n, values):
                link = chain(dve, s_widest, n, 2)
                link(dve.tensor_tensor(values, values, g.exists[:], ALU.mult))
                link(dve.tensor_reduce(widest[:], values, AX, ALU.max))
                dve.wait_ge(s_level, 2 * n + 1)
                dve.tensor_reduce(top[:], ps_scale[0:1, 0:P], AX, ALU.max).then_inc(s_level, 1)
                dve.wait_ge(s_scaled, 3 * n + 1)
                dve.tensor_scalar(scales[:, n, 0:1], ps_scale[:, 0:1], 1.0 / A_MAX, 1e-12, ALU.mult, ALU.max).then_inc(s_scaled, 1)
                dve.wait_ge(s_scaled, 3 * n + 2)
                dve.reciprocal(scales[:, n, 1:2], scales[:, n, 0:1]).then_inc(s_scaled, 1)
                dve.wait_ge(s_scaled, 3 * n + 3)
                return scales[:, n, 0:1], scales[:, n, 1:2]

            scale, inv = scale_of(0, g.largest[:])

            dve.wait_ge(s_x3, 16)

            def low(t, p, m):
                dve.wait_ge(s_high, t + 1)
                dve.tensor_tensor(normed_t[:, p, 1].rearrange("p k c -> p (k c)"), ps_turn[:, p, :],
                                  normed_t[:, p, 0].rearrange("p k c -> p (k c)").bitcast(F32), ALU.subtract).then_inc(s_turned, 1)

            def norm(t, p, m):
                dve.wait_ge(s_turn, t + 1)
                link = chain(dve, s_normed, t, 4)
                link(dve.tensor_scalar(normed[:], flat(x3[:, ds(t, 1), :]), g.means[:, ds(t, 1)], g.rstds[:, ds(t, 1)], ALU.subtract, ALU.mult))
                quantised(dve, link, normed[:], normed[:], inv, scale, -A_MAX - 1.0, A_MAX)

            def measure(t, p, m):
                dve.wait_ge(s_gate_up_kept, t + 1)
                for side in (0, 1):
                    ins = dve.tensor_reduce(largest[:, side, ds(t, 1)], ps_gate_up[:, side, 0:I], AX, ALU.max, apply_absolute_value=True)
                    ins.then_inc(s_largest, 1)
            pipeline(dve, T, [(norm, 0), (low, 0), (measure, 1)])
            dve.wait_ge(s_largest, 2 * T + 2)
            gate, up = gate_up[:, 0], gate_up[:, 1]
            link = chain(dve, s_quant, 0, 14)
            scale, inv = scale_of(1, largest[:, 0, :])
            quantised(dve, link, gate, gate, inv, scale, -A_MAX - 1.0, A_MAX)
            scale, inv = scale_of(2, largest[:, 1, :])
            quantised(dve, link, up, up, inv, scale, -A_MAX - 1.0, A_MAX)
            dve.wait_ge(s_sig, 1)
            quantised(dve, link, sig[:], sig[:], 65536.0, 1.0 / 65536.0, 0.0, S_MAX)
            link(dve.tensor_tensor(gate, gate, sig[:], ALU.mult))
            link(dve.tensor_reduce(largest[:, 0, :], gate, AX, ALU.max, apply_absolute_value=True))
            scale, inv = scale_of(3, largest[:, 0, :])
            quantised(dve, link, gate, gate, inv, scale, -A_MAX - 1.0, A_MAX)
            link2 = chain(dve, s_all, 0, 2)
            link2(dve.tensor_tensor(gate, gate, up, ALU.mult))
            link2(dve.tensor_reduce(largest[:, 0, :], gate, AX, ALU.max, apply_absolute_value=True))
            scale, inv = scale_of(4, largest[:, 0, :])

            def quantise_o(t, p, m):
                dve.wait_ge(s_o_turn, t + 1)
                link = chain(dve, s_o, t, 3)
                value = flat(gate[:, ds(t, 1), :])
                quantised(dve, link, normed[:, p * I:(p + 1) * I], value, inv, scale, -A_MAX - 1.0, A_MAX)

            def o_low(t, p, m):
                dve.wait_ge(s_o_high, t + 1)
                dve.tensor_tensor(o_t[:, p, 1].rearrange("p k c -> p (k c)"), ps_turn[:, p, 0:KI * P],
                                  o_t[:, p, 0].rearrange("p k c -> p (k c)").bitcast(F32), ALU.subtract).then_inc(s_o_t, 1)

            def finish(t, p, m):
                dve.wait_ge(s_out[p], 16 * m + 16)
                dve.wait_ge(s_down, t + 3)
                dve.tensor_tensor(result[:, p, :], flat(ps_down), flat(x3[:, ds(t, 1), :]), ALU.add).then_inc(s_result, 1)
            pipeline(dve, T, [(quantise_o, 0), (o_low, 0), (finish, 1)])

        @block.scalar
        def _(act):
            def w_high(t, p, m):
                act.wait_ge(s_w_turn, t + 1)
                act.activation(w_t[:, 0, ds(t * BLOCKS, BLOCKS), :].rearrange("p b c -> p (b c)"), ps_turn[:, p, :], ACT.Copy).then_inc(s_w_high, 1)
            pipeline(act, g.w_tiles, [(w_high, 0)])

            def high(t, p, m):
                act.wait_ge(s_turn, t + 2)
                act.wait_ge(s_gate_up, t + 1)
                act.activation(normed_t[:, p, 0].rearrange("p k c -> p (k c)"), ps_turn[:, p, :], ACT.Copy).then_inc(s_high, 1)

            def keep(t, p, m):
                act.wait_ge(s_gate_up, t + 3)
                act.activation(gate_up[:, :, ds(t, 1), :].rearrange("p s a i -> p s (a i)"), ps_gate_up[:, :, 0:I], ACT.Copy).then_inc(s_gate_up_kept, 1)
            pipeline(act, T, [(high, 0), (keep, 1)])
            act.wait_ge(s_quant, 3)
            act.activation(sig[:], gate_up[:, 0], ACT.Sigmoid).then_inc(s_sig, 1)

            def take_o(t, p, m):
                act.wait_ge(s_o_turn, t + 3)
                act.wait_ge(s_down, t + 1)
                act.activation(o_t[:, p, 0].rearrange("p k c -> p (k c)"), ps_turn[:, p, 0:KI * P], ACT.Copy).then_inc(s_o_high, 1)
            pipeline(act, T, [(take_o, 0)])

        @block.tensor
        def _(pe):
            def w_turn(t, p, m):
                pe.wait_ge(s_rows[p], 16 * m + 16)
                pe.wait_ge(s_w, t + 1)
                for k in range(BLOCKS):
                    last = pe.transpose(ps_turn[:, p, k * P:(k + 1) * P], rows[:, p, k * P:(k + 1) * P], g.ident[:])
                last.then_inc(s_w_turn, 1)
            pipeline(pe, g.w_tiles, [(w_turn, 0)])

            def level(n):
                pe.wait_ge(s_widest, 2 * n + 2)
                pe.transpose(ps_scale[0:1, 0:P], widest[:, 0:1], g.ident[:]).then_inc(s_level, 1)
                pe.wait_ge(s_level, 2 * n + 2)
                pe.matmul(ps_scale[:, 0:1], g.ones[0:1, :], top[0:1, 0:1], start=True, stop=True).then_inc(s_scaled, 1)
            level(0)
            pe.sem_inc(s_turn, 1)
            pe.sem_inc(s_turned, 2)
            pe.sem_inc(s_gate_up, 2)
            pe.sem_inc(s_largest, 2)
            pe.wait_ge(s_w, g.w_tiles + 2)

            def turn(t, p, m):
                pe.wait_ge(s_normed, 4 * t + 4)
                pe.wait_ge(s_turned, t + 1)
                for k in range(K):
                    last = pe.transpose(ps_turn[:, p, k * P:(k + 1) * P], normed[:, k * P:(k + 1) * P], g.ident[:])
                last.then_inc(s_turn, 1)

            def multiply(t, p, m):
                pe.wait_ge(s_turned, t + 3)
                pe.wait_ge(s_largest, 2 * t + 2)
                for side in (0, 1):
                    for k in range(K):
                        for n, (l, r) in enumerate(TERMS):
                            last = pe.matmul(ps_gate_up[:, side, 0:I], normed_t[:, p, l, k, :], weight(r, side, k), start=(k == 0 and n == 0), stop=(k == K - 1 and n == 2))
                last.then_inc(s_gate_up, 1)
            pipeline(pe, T, [(turn, 0), (multiply, 1)])
            for n in range(1, 5):
                level(n)
            pe.sem_inc(s_o_t, 2)
            pe.sem_inc(s_result, 1)
            pe.sem_inc(s_o_turn, 2)
            pe.sem_inc(s_down, 2)

            def turn_o(t, p, m):
                pe.wait_ge(s_o, 3 * t + 3)
                pe.wait_ge(s_o_t, t + 1)
                for k in range(KI):
                    last = pe.transpose(ps_turn[:, p, k * P:(k + 1) * P], normed[:, p * I + k * P:p * I + (k + 1) * P], g.ident[:])
                last.then_inc(s_o_turn, 1)

            def down(t, p, m):
                pe.wait_ge(s_o_t, t + 3)
                pe.wait_ge(s_result, t + 1)
                for k in range(KI):
                    for n, (l, r) in enumerate(TERMS):
                        for a in (0, 1):
                            blocks = HALF // P
                            last = pe.matmul(ps_down[:, a, :], o_t[:, p, l, k, :], down_weight(r, k)[:, a * blocks:(a + 1) * blocks, :],
                                             start=(k == 0 and n == 0), stop=(k == KI - 1 and n == 2))
                last.then_inc(s_down, 1)
            pipeline(pe, T, [(turn_o, 0), (down, 1)])


def build(nc, ins, out, until=99):
    g = Shared()
    g.N, g.D = ins["x"].shape
    g.E = ins["src"].shape[0]
    g.T, g.K = tiles(g.N), g.D // P
    g.NP = g.T * P
    g.X = ins["L0_ffn_w_gate"].shape[1]
    g.slot_tiles = (g.NP + g.X * (P - 1)) // P
    g.slot_tiles += g.slot_tiles % 2
    T, K, NP, D, S = g.T, g.K, g.NP, g.D, g.slot_tiles
    ffn_sources = [ins["L1_ffn_w_gate"], ins["L1_ffn_w_up"], ins["L1_ffn_w_down"]]
    g.I = ins["L1_ffn_w_gate"].shape[0]
    g.w_tiles = 3 * g.I // P
    with ExitStack() as ctx:
        def sb(name, shape, dt=F32, where=ctx):
            return where.enter_context(nc.sbuf_tensor(name, shape, dt))

        def dram(name, shape, dt=F32):
            return nc.dram_tensor(name, shape, dt).ap()

        g.counts_dram = dram("counts_dram", (T, P, NP))
        g.turned_dram = dram("turned_dram", (T, P, NP))
        g.x1_dram = dram("x1_dram", (T, P, D))
        g.x2_dram = dram("x2_dram", (T, P, D))
        g.x3_dram = dram("x3_dram", (T, P, D))
        g.normed_dram = dram("normed_dram", (NP, D))
        g.slot_token_dram = dram("slot_token_dram", (S * P, 1), I32)
        g.y_dram = dram("y_dram", (S * P, D))
        g.nodes_t_dram = [dram(f"nodes_t_dram{n}", (T, P, 2 * D)) for n in (0, 1)]
        g.w_rows_dram = dram("w_rows_dram", (P, g.w_tiles, D))
        g.col_id = sb("col_id", [P, P])
        g.row_id = sb("row_id", [P, 1])
        g.node_id = sb("node_id", [P, T])
        g.token_id = sb("token_id", [P, T], I32)
        g.exists = sb("exists", [P, T])
        g.ident = sb("ident", [P, P])
        g.before = sb("before", [P, P])
        g.ones = sb("ones", [P, P])
        g.ones_r = sb("ones_r", [P, P], F32R)
        g.eps = sb("eps", [P, 1])
        g.deg = sb("deg", [P, T])
        g.many_i = sb("many_i", [1, 1], I32)
        g.sides = sb("sides", [P, T, 2])
        g.route_p = sb("route_p", [P, T])
        g.chosen = sb("chosen", [P, T, g.X])
        g.slot = sb("slot", [P, T], I32)
        g.mean_var = sb("mean_var", [P, 2])
        g.means = sb("means", [P, T])
        g.rstds = sb("rstds", [P, T])
        g.largest = sb("largest", [P, T])
        g.always = ctx.enter_context(nc.semaphore("always"))
        with nc.cleanup_on_exit(), ExitStack() as early:
            nodes = sb("hidden", [P, T, 2, D], F32R, early)
            with ExitStack() as first:
                w = sb("w_gnn", [P, 2, K, D], F32R, first)
                graph_phase(nc, g, ins["src"], ins["dst"])
                if until < 1:
                    return
                hidden_phase(nc, g, ins["x"], ins["L0_gnn_W"], ins["L0_gnn_a"], w, nodes)
            if until < 2:
                return
            attention_phase(nc, g, ins["x"], ins["L0_ffn_w_gate"], ins["L0_ffn_b_gate"], nodes)
        if until < 3:
            return
        with ExitStack() as late:
            w = sb("w_sage", [P, 2, K, D], F32R, late)
            expert_phase(nc, g, ins["L0_ffn_W1"], ins["L0_ffn_b1"], ins["L0_ffn_W2"], ins["L0_ffn_b2"])
            if until < 4:
                return
            nodes = sb("neighbours", [P, T, 2, D], F32R, late)
            for n in (0, 1):
                neighbour_phase(nc, g, n, ins[f"L1_gnn_W_neigh{n}"], w, nodes, ffn_sources)
                if until < 5 + 2 * n:
                    return
                aggregate_phase(nc, g, n, ins[f"L1_gnn_W_self{n}"], ins[f"L1_gnn_b{n}"], w, nodes)
                if until < 6 + 2 * n:
                    return
        feed_forward_phase(nc, g, out)


_INS = ["x", "src", "dst", "L0_gnn_W", "L0_gnn_a", "L0_ffn_w_gate", "L0_ffn_b_gate", "L0_ffn_W1", "L0_ffn_b1",
        "L0_ffn_W2", "L0_ffn_b2", "L1_gnn_W_self0", "L1_gnn_W_neigh0", "L1_gnn_b0", "L1_gnn_W_self1",
        "L1_gnn_W_neigh1", "L1_gnn_b1", "L1_ffn_w_gate", "L1_ffn_w_up", "L1_ffn_w_down"]


def kernel(**inputs):
    import numpy as np
    import concourse.bacc as bacc
    from concourse.bass_utils import run_bass_kernel_spmd

    nc = bacc.Bacc("TRN2", target_bir_lowering=False, num_devices=1)
    arrays, ins = {}, {}
    for name in _INS:
        a = np.ascontiguousarray(inputs[name])
        arrays[f"in_{name}"] = a
        ins[name] = nc.dram_tensor(f"in_{name}", a.shape, mybir.dt.from_np(a.dtype), kind="ExternalInput").ap()
    out = nc.dram_tensor("out", inputs["x"].shape, F32, kind="ExternalOutput").ap()
    build(nc, ins, out)
    r = run_bass_kernel_spmd(nc, [arrays], core_ids=[0])
    return r.results[0]["out"]
```

```python
from contextlib import ExitStack

import concourse.bass as bass
from concourse import mybir

ALU = mybir.AluOpType
ACT = mybir.ActivationFunctionType
AX = mybir.AxisListType.X
F32 = mybir.dt.float32
F32R = mybir.dt.float32r
F16 = mybir.dt.float16
I32 = mybir.dt.int32
ds = bass.ds

P = 128
HALF = 512
CHUNKS = 4
UNIT = CHUNKS * P
ROUND = 12582912.0
LN_EPS = 1e-5
GAT_EPS = 1e-5
NEG_SLOPE = 0.1
W_BLOCK = 32
W_MAX = 7.0
A_MAX = 32767.0
S_MAX = 65535.0


def flat(ap):
    return ap.rearrange("p a d -> p (a d)")


def tiles(n):
    return -(-n // P)


def makers(ctx, nc, phase):
    def sb(name, shape, dt=F32):
        return ctx.enter_context(nc.sbuf_tensor(f"{phase}_{name}", shape, dt))

    def ps(name, shape):
        return ctx.enter_context(nc.psum_tensor(f"{phase}_{name}", shape, F32))

    def sem(name):
        return nc.alloc_semaphore(f"{phase}_{name}")
    return sb, ps, sem


def layer_stats(dve, g, link, halves, stats, mean_var):
    link(dve.bn_stats(stats[:, 0:6], halves[0]), g.always)
    link(dve.bn_stats(stats[:, 6:12], halves[1]), g.always)
    link(dve.bn_aggr(mean_var, stats))


def wait_apart(eng, always, sem, value):
    if isinstance(value, int):
        eng.wait_ge(always, 1)
        eng.wait_ge(sem, value)
        return
    with eng.register() as reg:
        eng.reg_mov(reg, value)
        eng.wait_ge(always, 1)
        eng.wait_ge(sem, reg)


def chain(eng, sem, t, per, start=0):
    k = [0]

    def link(ins, always=None):
        k[0] += 1
        assert k[0] <= per
        ins.then_inc(sem, 1)
        if always is None:
            eng.wait_ge(sem, t * per + k[0] + start)
        else:
            wait_apart(eng, always, sem, t * per + k[0] + start)
    return link


def pipeline(eng, count, stages, pairs=None, last_apart=False):
    deepest = max(lag for _, lag in stages)
    first = deepest + deepest % 2
    end = count - count % 2 - (2 if last_apart else 0)

    def step(s):
        for stage, lag in stages:
            t = s - lag
            if 0 <= t and (pairs is not None or t < count):
                stage(t, t % 2, t // 2)

    if pairs is None and first >= end:
        for s in range(count + deepest):
            step(s)
        return
    for s in range(first):
        step(s)
    with eng.Fori(first // 2, end // 2 if pairs is None else pairs) as i:
        for r in (0, 1):
            for stage, lag in stages:
                stage(2 * i + (r - lag), (r - lag) % 2, i + (r - lag) // 2)
    if pairs is None:
        for s in range(end, count + deepest):
            step(s)
        return
    for r in range(deepest):
        for stage, lag in stages:
            if lag > r:
                stage(2 * pairs + (r - lag), (r - lag) % 2, pairs + (r - lag) // 2)


class Split:

    def __init__(self, makers, raw, both):
        _, _, sem = makers
        self.raw, self.both, self.K, self.slots = raw, both, both.shape[2], min(raw.shape[1], both.shape[2])
        self.s_raw = [sem(f"s_w_raw{slot}") for slot in range(self.slots)]
        self.s_high = sem("s_w_high")
        self.s_low = sem("s_w_low")

    def load(self, sp, source):
        for k in range(self.K):
            if k >= self.slots:
                sp.wait_ge(self.s_low, k - self.slots + 1)
            slot = k % self.slots
            sp.dma_start(self.raw[:, slot, :], source[k * P:(k + 1) * P, :]).then_inc(self.s_raw[slot], 16)

    def high(self, act):
        for k in range(self.K):
            act.wait_ge(self.s_raw[k % self.slots], 16 * (k // self.slots + 1))
            act.activation(self.both[:, 0, k, :], self.raw[:, k % self.slots, :], ACT.Copy).then_inc(self.s_high, 1)

    def low(self, dve):
        for k in range(self.K):
            dve.wait_ge(self.s_high, k + 1)
            dve.tensor_tensor(self.both[:, 1, k, :], self.raw[:, k % self.slots, :],
                              self.both[:, 0, k, :].bitcast(F32), ALU.subtract).then_inc(self.s_low, 1)

    def ready(self, eng, k=None):
        eng.wait_ge(self.s_low, self.K if k is None else k + 1)


TERMS = ((0, 0), (0, 1), (1, 0))


def products(pe, out, left, right, k, start, stop):
    for n, (l, r) in enumerate(TERMS):
        for a in range(0, out.shape[1], HALF):
            b = min(a + HALF, out.shape[1])
            last = pe.matmul(out[:, a:b], left(l, k), right(r, k)[:, a:b], start=start and n == 0, stop=stop and n == 2)
    return last


class Shared:
    pass


def graph_phase(nc, g, src, dst, w_source, w):
    T, N, NP, E = g.T, g.N, g.NP, g.E
    full, rest = E // UNIT, E % UNIT
    units = full + (rest > 0)
    with ExitStack() as ctx:
        sb, ps, sem = makers(ctx, nc, "graph")

        split = Split((sb, ps, sem), sb("w_raw", [P, 2, g.D]), w)
        src_i = sb("src_i", [P, UNIT], I32)
        dst_i = sb("dst_i", [P, UNIT], I32)
        src_f = sb("src_f", [P, UNIT], F32)
        dst_f = sb("dst_f", [P, UNIT], F32)
        least = sb("least", [P, 1])
        most = sb("most", [P, 1])
        starts = sb("starts", [P, T])
        ends = sb("ends", [P, T])
        present = sb("present", [P, T], F32)
        from_start = sb("from_start", [T, units], F32)
        from_end = sb("from_end", [T, units], F32)
        edge_of = sb("edge_of", [T, 2], F32)
        bounds = sb("bounds", [T, 2], F32)
        bounds_i = sb("bounds_i", [1, 2 * T], I32)
        col_i = sb("col_i", [P, NP], I32)
        row_i = sb("row_i", [P, 1], I32)
        node_i = sb("node_i", [P, T], I32)
        src_t = sb("src_t", [P, CHUNKS, units], F32)
        dst_t = sb("dst_t", [P, CHUNKS, units], F16)
        zeros16 = sb("zeros16", [P, P], F16)
        iota16 = sb("iota16", [P, NP], F16)
        dst_hot = sb("dst_hot", [P, CHUNKS, P], F16)
        src_hot = sb("src_hot", [P, CHUNKS, N], F16)
        counts = sb("counts", [P, 2, NP], F32)
        turned = sb("turned", [P, 2, T, P], F32)
        deg_t = sb("deg_t", [P, 2], F32)
        acc = ps("acc", [P, 2, 3 * HALF])
        ps_turn = ps("ps_turn", [P, 2, HALF])

        s_iota = sem("s_iota")
        s_fill = sem("s_fill")
        s_src = sem("s_src")
        s_dst = sem("s_dst")
        s_rest = sem("s_rest")
        s_const = sem("s_const")
        s_prep = sem("s_prep")
        s_present_t = sem("s_present_t")
        s_edges_t = sem("s_edges_t")
        s_edges_kept = sem("s_edges_kept")
        s_bounds = sem("s_bounds")
        s_bounds_t = sem("s_bounds_t")
        s_ready = sem("s_ready")
        s_hot = sem("s_hot")
        s_hot_free = sem("s_hot_free")
        s_acc = sem("s_acc")
        s_counts = sem("s_counts")
        s_turn = sem("s_turn")
        s_turn_free = sem("s_turn_free")
        s_counts_out = [sem("s_counts_out0"), sem("s_counts_out1")]
        s_turned_out = [sem("s_turned_out0"), sem("s_turned_out1")]
        block = ctx.enter_context(nc.Block())

        @block.gpsimd
        def _(pool):
            pool.iota(col_i[:], [[1, NP]], base=0, channel_multiplier=0).then_inc(s_iota, 1)
            pool.iota(row_i[:], [[1, 1]], base=0, channel_multiplier=1).then_inc(s_iota, 1)
            pool.iota(node_i[:], [[P, T]], base=0, channel_multiplier=1).then_inc(s_iota, 1)
            pool.iota(g.token_id[:], [[P, T]], base=0, channel_multiplier=1).then_inc(s_iota, 1)
            split.low(pool)

        @block.sync
        def _(sp):
            sp.wait_ge(s_fill, 2)
            sp.dma_start(dst_i[0:full, :], dst[0:full * UNIT].rearrange("(a b) -> a b", b=UNIT)).then_inc(s_dst, 16)
            sp.dma_start(src_i[0:full, :], src[0:full * UNIT].rearrange("(a b) -> a b", b=UNIT)).then_inc(s_src, 16)
            if rest:
                sp.dma_start(dst_i[full:full + 1, 0:rest], dst[full * UNIT:E].rearrange("(a b) -> a b", a=1)).then_inc(s_rest, 16)
                sp.dma_start(src_i[full:full + 1, 0:rest], src[full * UNIT:E].rearrange("(a b) -> a b", a=1)).then_inc(s_rest, 16)
            split.load(sp, w_source)

            def store(t, p, m):
                sp.wait_ge(s_counts, t + 3)
                sp.dma_start(g.counts_dram[ds(t, 1)].rearrange("a p n -> (a p) n"), counts[:, p, :]).then_inc(s_counts_out[p], 16)
                sp.wait_ge(s_turn_free, 3 * t + 5)
                sp.dma_start(g.turned_dram[ds(t, 1)].rearrange("a p n -> (a p) n"),
                             turned[:, p].rearrange("p j c -> p (j c)")).then_inc(s_turned_out[p], 16)
            pipeline(sp, T, [(store, 0)])
            for p in (0, 1):
                sp.wait_ge(s_counts_out[p], 16 * (T // 2) + 16)
                sp.wait_ge(s_turned_out[p], 16 * (T // 2) + 16)

        @block.vector
        def _(dve):
            dve.sem_inc(g.always, 1)
            dve.memset(src_i[:], -1).then_inc(s_fill, 1)
            dve.memset(dst_i[:], N - 1).then_inc(s_fill, 1)
            dve.memset(zeros16[:], 0.0).then_inc(s_const, 1)
            dve.memset(g.ones[:], 1.0).then_inc(s_const, 1)
            dve.memset(g.eps[:], LN_EPS).then_inc(s_const, 1)
            dve.memset(counts[:, :, N:NP], 0.0).then_inc(s_const, 1)
            dve.wait_ge(s_iota, 4)
            dve.tensor_copy(g.col_id[:], col_i[:, 0:P]).then_inc(s_const, 1)
            dve.tensor_copy(iota16[:], col_i[:]).then_inc(s_const, 1)
            dve.tensor_copy(g.row_id[:], row_i[:]).then_inc(s_const, 1)
            dve.tensor_copy(g.node_id[:], node_i[:]).then_inc(s_const, 1)
            dve.wait_ge(s_const, 8)
            dve.tensor_scalar(g.ident[:], g.col_id[:], g.row_id[:, 0:1], None, ALU.is_equal).then_inc(s_const, 1)
            dve.tensor_scalar(g.before[:], g.col_id[:], g.row_id[:, 0:1], None, ALU.is_gt).then_inc(s_const, 1)
            dve.tensor_copy(g.ones_r[:], g.ones[:]).then_inc(s_const, 1)
            dve.tensor_scalar(g.exists[:], g.node_id[:], float(N), None, ALU.is_lt).then_inc(s_const, 1)
            dve.wait_ge(s_dst, 16)
            dve.wait_ge(s_src, 16)
            if rest:
                dve.wait_ge(s_rest, 32)
            link = chain(dve, s_prep, 0, 8)
            link(dve.tensor_copy(src_f[:], src_i[:]))
            link(dve.tensor_copy(dst_f[:], dst_i[:]))
            link(dve.tensor_reduce(least[:], dst_f[:], AX, ALU.min))
            link(dve.tensor_reduce(most[:], dst_f[:], AX, ALU.max))
            link(dve.tensor_scalar(starts[:], g.col_id[:, 0:T], float(P), None, ALU.mult))
            link(dve.tensor_scalar(ends[:], starts[:], float(P), None, ALU.add))
            link(dve.tensor_scalar(ends[:], ends[:], least[:, 0:1], None, ALU.is_gt))
            link(dve.scalar_tensor_tensor(present[:], starts[:], most[:, 0:1], ends[:], ALU.is_le, ALU.mult))
            dve.wait_ge(s_edges_t, 2)
            dve.tensor_copy(src_t[:], acc[:, 0, 0:CHUNKS * P].rearrange("p (c u) -> p c u", c=CHUNKS)[:, :, 0:units]).then_inc(s_edges_kept, 1)
            dve.tensor_copy(dst_t[:], acc[:, 0, HALF:HALF + CHUNKS * P].rearrange("p (c u) -> p c u", c=CHUNKS)[:, :, 0:units]).then_inc(s_edges_kept, 1)
            dve.wait_ge(s_present_t, 1)
            link = chain(dve, s_bounds, 0, 9)
            here = ps_turn[0:T, 0, 0:units]
            link(dve.tensor_scalar(from_start[:], g.col_id[0:T, 0:units], 1.0, None, ALU.add))
            link(dve.tensor_scalar(from_end[:], g.col_id[0:T, 0:units], -1.0, float(units), ALU.mult, ALU.add))
            link(dve.tensor_tensor(from_start[:], from_start[:], here, ALU.mult))
            link(dve.tensor_tensor(from_end[:], from_end[:], here, ALU.mult))
            link(dve.tensor_reduce(edge_of[:, 0:1], from_end[:], AX, ALU.max))
            link(dve.tensor_reduce(edge_of[:, 1:2], from_start[:], AX, ALU.max))
            link(dve.tensor_scalar(bounds[:, 0:1], edge_of[:, 0:1], -1.0, float(units), ALU.mult, ALU.add))
            link(dve.tensor_scalar(bounds[:, 0:1], bounds[:, 0:1], float(units - 1), None, ALU.min))
            link(dve.tensor_scalar(bounds[:, 1:2], edge_of[:, 1:2], -1.0, bounds[:, 0:1], ALU.add, ALU.max))
            dve.wait_ge(s_bounds_t, 1)
            dve.tensor_copy(bounds_i[0:1, 0:T], ps_turn[0:1, 1, 0:T]).then_inc(s_ready, 1)
            dve.tensor_scalar(bounds_i[0:1, T:2 * T], ps_turn[0:1, 1, T:2 * T], 1.0, None, ALU.add).then_inc(s_ready, 1)
            dve.wait_ge(s_ready, 2)
            dve.wait_ge(s_edges_kept, 2)
            made = dve.alloc_register("hot_made")
            dve.reg_mov(made, 0)

            def hot(t, p, m):
                lo = dve.value_load(bounds_i[0:1, ds(t, 1)], min_val=0, max_val=units - 1)
                hi = dve.value_load(bounds_i[0:1, ds(t + T, 1)], min_val=1, max_val=units)
                with dve.Fori(lo, hi) as u:
                    for c in range(0, CHUNKS, 2):
                        dve.reg_add(made, made, 1)
                        dve.wait_ge(s_hot_free, made)
                        here = [P, 2, P]
                        dve.tensor_tensor(dst_hot[:, c:c + 2, :], iota16[:, ds(t * P, P)].unsqueeze(1).broadcast_to(here),
                                          dst_t[:, c:c + 2, ds(u, 1)].broadcast_to(here), ALU.is_equal)
                        for d in (c, c + 1):
                            dve.tensor_scalar(src_hot[:, d, :], iota16[:, 0:N], src_t[:, d, ds(u, 1)], None, ALU.is_equal).then_inc(s_hot, 1)
            pipeline(dve, T, [(hot, 0)])
            dve.free_register(made)

        @block.tensor
        def _(pe):
            pe.sem_inc(s_hot_free, CHUNKS // 2)
            pe.wait_ge(s_const, 12)
            pe.wait_ge(s_prep, 8)
            for c in range(CHUNKS):
                last = pe.transpose(acc[:, 0, c * P:(c + 1) * P], src_f[:, c * P:(c + 1) * P], g.ident[:])
            last.then_inc(s_edges_t, 1)
            for c in range(CHUNKS):
                last = pe.transpose(acc[:, 0, HALF + c * P:HALF + (c + 1) * P], dst_f[:, c * P:(c + 1) * P], g.ident[:])
            last.then_inc(s_edges_t, 1)
            pe.transpose(ps_turn[0:T, 0, 0:P], present[:], g.ident[:]).then_inc(s_present_t, 1)
            pe.wait_ge(s_bounds, 9)
            pe.transpose(ps_turn[0:1, 1, 0:T], bounds[:, 0:1], g.ident[0:T, 0:T])
            pe.transpose(ps_turn[0:1, 1, T:2 * T], bounds[:, 1:2], g.ident[0:T, 0:T]).then_inc(s_bounds_t, 1)
            pe.wait_ge(s_ready, 2)
            pe.wait_ge(s_edges_kept, 2)
            done = pe.alloc_register("hot_done")
            pe.reg_mov(done, 0)
            spans = [(a, min(a + HALF, N)) for a in range(0, N, HALF)]

            def count(t, p, m):
                lo = pe.value_load(bounds_i[0:1, ds(t, 1)], min_val=0, max_val=units - 1)
                hi = pe.value_load(bounds_i[0:1, ds(t + T, 1)], min_val=1, max_val=units)
                pe.wait_ge(s_counts, t + 1)
                for a, b in spans:
                    pe.matmul(acc[:, p, a:b], zeros16[:], iota16[:, 0:b - a], start=True, stop=False, skip_group_check=True)
                with pe.Fori(lo, hi) as u:
                    for c in range(CHUNKS):
                        pe.reg_add(done, done, 1)
                        pe.wait_ge(s_hot, done)
                        for a, b in spans:
                            last = pe.matmul(acc[:, p, a:b], dst_hot[:, c, :], src_hot[:, c, a:b], start=False, stop=False, skip_group_check=True)
                        if c % 2:
                            last.then_inc(s_hot_free, 1)
                for a, b in spans:
                    last = pe.matmul(acc[:, p, a:a + 2], zeros16[:], iota16[:, 0:2], start=False, stop=True, skip_group_check=True)
                last.then_inc(s_acc, 1)

            def turn(t, p, m):
                pe.wait_ge(s_counts, t + 3)
                for r in range(3):
                    pe.wait_ge(s_turn_free, t * 3 + r + 1)
                    for j in range(4 * r, min(4 * r + 4, T)):
                        last = pe.transpose(ps_turn[:, (p + r) % 2, (j % 4) * P:(j % 4 + 1) * P], counts[:, p, j * P:(j + 1) * P], g.ident[:])
                    last.then_inc(s_turn, 1)
            pipeline(pe, T, [(count, 0), (turn, 1)])
            pe.free_register(done)

        @block.scalar
        def _(act):
            act.sem_inc(s_counts, 2)
            act.sem_inc(s_turn_free, 2)
            for p in (0, 1):
                act.sem_inc(s_counts_out[p], 16)
                act.sem_inc(s_turned_out[p], 16)
            split.high(act)
            act.wait_ge(s_const, 12)
            def take(t, p, m):
                act.wait_ge(s_acc, t + 1)
                act.wait_ge(s_counts_out[p], m * 16 + 16)
                act.activation(counts[:, p, 0:N], acc[:, p, 0:N], ACT.Copy, accum_out=deg_t[:, p:p + 1]).then_inc(s_counts, 1)
                act.wait_ge(s_counts, t + 3)
                act.activation(g.deg[:, ds(t, 1)], deg_t[:, p:p + 1], ACT.Copy)

            def take_turned(t, p, m):
                act.wait_ge(s_turned_out[p], m * 16 + 16)
                for r in range(3):
                    act.wait_ge(s_turn, t * 3 + r + 1)
                    n = min(4, T - 4 * r)
                    ins = act.activation(turned[:, p, 4 * r:4 * r + n, :], ps_turn[:, (p + r) % 2, 0:n * P].rearrange("p (j c) -> p j c", c=P), ACT.Copy)
                    ins.then_inc(s_turn_free, 1)
            pipeline(act, T, [(take, 0), (take_turned, 1)])


def hidden_phase(nc, g, x, a, w, nodes):
    T, K, D, N = g.T, g.K, g.D, g.N
    with ExitStack() as ctx:
        sb, ps, sem = makers(ctx, nc, "hidden")

        a_rows = sb("a_rows", [P, 2 * D])
        x_t = sb("x_t", [P, 2, D])
        stats = sb("stats", [P, 2, 12])
        mean_var = sb("mean_var", [P, 2, 2])
        std = sb("std", [P, 2])
        rstd = sb("rstd", [P, 2])
        normed = sb("normed", [P, 2, D])
        normed_t = sb("normed_t", [P, 2, 2, K, P], F32R)
        product = sb("product", [P, D])
        side = sb("side", [P, 2, 2])
        ps_turn = ps("ps_turn", [P, D])
        ps_h = ps("ps_h", [P, 2, D])

        s_a = sem("s_a")
        s_x = [sem("s_x0"), sem("s_x1")]
        s_x_pad = sem("s_x_pad")
        s_stats = sem("s_stats")
        s_std = sem("s_std")
        s_normed = sem("s_normed")
        s_turn = sem("s_turn")
        s_high = sem("s_high")
        s_turned = sem("s_turned")
        s_h = sem("s_h")
        s_h_taken = sem("s_h_taken")
        s_sides = sem("s_sides")
        s_half_free = sem("s_half_free")
        block = ctx.enter_context(nc.Block())

        @block.sync
        def _(sp):
            def load(t, p, m):
                sp.wait_ge(s_normed, t + 1)
                if isinstance(t, int) and (t + 1) * P > N:
                    sp.wait_ge(s_x_pad, 1)
                    sp.dma_start(x_t[0:N - t * P, p, :], x[t * P:N, :]).then_inc(s_x[p], 16)
                else:
                    sp.dma_start(x_t[:, p, :], x[ds(t * P, P), :]).then_inc(s_x[p], 16)
            load(0, 0, 0)
            load(1, 1, 0)
            sp.dma_start(a_rows[:], a.broadcast_to([P, 2 * D])).then_inc(s_a, 16)
            with sp.Fori(1, T // 2 - 1) as i:
                for p in (0, 1):
                    load(2 * i + p, p, i)
            load(T - 2, 0, T // 2 - 1)
            load(T - 1, 1, T // 2 - 1)

        @block.vector
        def _(dve):
            dve.sem_inc(s_normed, 2)
            def norm(t, p, m):
                if isinstance(t, int) and t == T - 1:
                    dve.wait_ge(s_normed, T)
                    dve.memset(x_t[:, p, :], 0.0).then_inc(s_x_pad, 1)
                dve.wait_ge(s_x[p], 16 * m + 16)
                link = chain(dve, s_stats, t, 3)
                layer_stats(dve, g, link, [x_t[:, p, a:a + HALF] for a in (0, HALF)], stats[:, p, :], mean_var[:, p, :])
                dve.wait_ge(s_std, 2 * t + 1)
                dve.reciprocal(rstd[:, p:p + 1], std[:, p:p + 1]).then_inc(s_std, 1)
                dve.wait_ge(s_std, 2 * t + 2)
                dve.tensor_scalar(normed[:, p, :], x_t[:, p, :], mean_var[:, p, 0:1],
                                  rstd[:, p:p + 1], ALU.subtract, ALU.mult).then_inc(s_normed, 1)

            def low(t, p, m):
                dve.wait_ge(s_high, t + 1)
                dve.tensor_tensor(normed_t[:, p, 1].rearrange("p k c -> p (k c)"), ps_turn[:],
                                  normed_t[:, p, 0].rearrange("p k c -> p (k c)").bitcast(F32), ALU.subtract).then_inc(s_turned, 1)

            def sides(t, p, m):
                dve.wait_ge(s_h_taken, t + 1)
                link = chain(dve, s_sides, t, 4)
                high = flat(nodes[:, ds(t, 1), 0, :])
                link(dve.tensor_tensor(flat(nodes[:, ds(t, 1), 1, :]), ps_h[:, p, :], high.bitcast(F32), ALU.subtract))
                for k in (0, 1):
                    link(dve.tensor_tensor_reduce(product[:], ps_h[:, p, :], a_rows[:, k * D:(k + 1) * D], 1.0, 0.0,
                                                  ALU.mult, ALU.add, side[:, p, k:k + 1]))
                dve.sem_inc(s_half_free, 1)
                link(dve.tensor_copy(flat(g.sides[:, ds(t, 1), :]), side[:, p, :]), g.always)
            dve.wait_ge(s_a, 16)
            pipeline(dve, T, [(low, 1), (norm, 0), (sides, 2)], last_apart=True)

        @block.scalar
        def _(act):
            def root(t, p, m):
                act.wait_ge(s_stats, t * 3 + 3)
                act.activation(std[:, p:p + 1], mean_var[:, p, 1:2], ACT.Sqrt, bias=g.eps[:, 0:1]).then_inc(s_std, 1)

            def take_turned(t, p, m):
                act.wait_ge(s_turn, t + 1)
                act.activation(normed_t[:, p, 0].rearrange("p k c -> p (k c)"), ps_turn[:], ACT.Copy).then_inc(s_high, 1)

            def take_h(t, p, m):
                act.wait_ge(s_h, t + 1)
                act.activation(flat(nodes[:, ds(t, 1), 0, :]), ps_h[:, p, :], ACT.Copy).then_inc(s_h_taken, 1)
            pipeline(act, T, [(take_turned, 1), (root, 0), (take_h, 2)])

        @block.tensor
        def _(pe):
            pe.sem_inc(s_turned, 1)
            pe.sem_inc(s_half_free, 2)
            def turn(t, p, m):
                pe.wait_ge(s_normed, t + 3)
                pe.wait_ge(s_turned, t + 1)
                for k in range(K):
                    last = pe.transpose(ps_turn[:, k * P:(k + 1) * P], normed[:, p, k * P:(k + 1) * P], g.ident[:])
                last.then_inc(s_turn, 1)

            def multiply(t, p, m):
                pe.wait_ge(s_turned, t + 2)
                pe.wait_ge(s_half_free, t + 1)
                for k in range(K):
                    last = products(pe, ps_h[:, p, :], lambda s, k: normed_t[:, p, s, k, :], lambda s, k: w[:, s, k, :], k, k == 0, k == K - 1)
                last.then_inc(s_h, 1)
            pipeline(pe, T, [(turn, 0), (multiply, 1)])


def attention_phase(nc, g, x, w_gate, b_gate, nodes):
    T, K, D, X, N = g.T, g.K, g.D, g.X, g.N
    with ExitStack() as ctx:
        sb, ps, sem = makers(ctx, nc, "attend")
        gate_w = sb("gate_w", [P, K, X])
        gate_b = sb("gate_b", [P, X])
        order = sb("order", [P, X])
        counts = sb("counts", [P, 2, T, P])
        diag = sb("diag", [P, 2, P])
        sums = sb("sums", [P, T, P])
        leaky = sb("leaky", [P, 2, T, P])
        weights = sb("weights", [P, 2, 2, T, P], F32R)
        x_t = sb("x_t", [P, 2, D])
        total = sb("total", [P, 2, P])
        rowsum = sb("rowsum", [P, 2])
        inv = sb("inv", [P, 2])
        below = sb("below", [P, D])
        above = sb("above", [P, D])
        elu = sb("elu", [P, D])
        stats = sb("stats", [P, 12])
        mean_var = sb("mean_var", [P, 2])
        std = sb("std", [P, 1])
        rstd = sb("rstd", [P, 1])
        normed = sb("normed", [P, 2, D])
        normed_t = sb("normed_t", [P, K, P])
        logits = sb("logits", [P, X])
        neg_max = sb("neg_max", [P, 1])
        exps = sb("exps", [P, X])
        exp_sum = sb("exp_sum", [P, 1])
        exp_max = sb("exp_max", [P, 1])
        ranked = sb("ranked", [P, X])
        best = sb("best", [P, 1])
        ps_h = ps("ps_h", [P, 2, D])
        ps_turn = ps("ps_turn", [P, D])
        ps_left = ps("ps_left", [P, P])
        ps_small = ps("ps_small", [P, HALF])
        ps_rowsum, ps_logits = ps_small[:, 0:1], ps_small[:, X:2 * X]

        s_gate = sem("s_gate")
        s_order = sem("s_order")
        s_counts = [sem("s_counts0"), sem("s_counts1")]
        s_x = [sem("s_x_0"), sem("s_x_1")]
        s_x_pad = sem("s_x_pad")
        s_x1_out = [sem("s_x1_out0"), sem("s_x1_out1")]
        s_product = sem("s_product")
        s_high = sem("s_high")
        s_total = sem("s_total")
        s_diag = sem("s_diag")
        s_left = sem("s_left")
        s_sums = sem("s_sums")
        s_exp = sem("s_exp")
        s_weights = sem("s_weights")
        s_attended = sem("s_attended")
        s_inv = sem("s_inv")
        s_below = sem("s_below")
        s_elu_parts = sem("s_elu_parts")
        s_x1 = sem("s_x1")
        s_stats = sem("s_stats")
        s_std = sem("s_std")
        s_normed = sem("s_normed")
        s_stored = [sem("s_stored0"), sem("s_stored1")]
        s_turn = sem("s_turn")
        s_turned = sem("s_turned")
        s_logits = sem("s_logits")
        s_logits_read = sem("s_logits_read")
        s_exps = sem("s_exps")
        s_route = sem("s_route")
        block = ctx.enter_context(nc.Block())

        @block.sync
        def _(sp):
            sp.dma_start(gate_w[:], w_gate.rearrange("(k p) e -> p k e", p=P)).then_inc(s_gate, 16)
            sp.dma_start(gate_b[:], b_gate.rearrange("(a e) -> a e", a=1).broadcast_to([P, X])).then_inc(s_gate, 16)

            def load(t, p, m):
                sp.wait_ge(s_product, t + 1)
                sp.dma_start(counts[:, p], g.counts_dram.rearrange("j p n -> p j n")[:, :, ds(t * P, P)]).then_inc(s_counts[p], 16)

            def load_x(t, p, m):
                sp.wait_ge(s_x1_out[p], 16 * m + 16)
                if isinstance(t, int) and (t + 1) * P > N:
                    sp.wait_ge(s_x_pad, 1)
                    sp.dma_start(x_t[0:N - t * P, p, :], x[t * P:N, :]).then_inc(s_x[p], 16)
                else:
                    sp.dma_start(x_t[:, p, :], x[ds(t * P, P), :]).then_inc(s_x[p], 16)

            def store(t, p, m):
                sp.wait_ge(s_normed, t + 1)
                sp.dma_start(g.x1_dram[ds(t, 1)].rearrange("a p d -> (a p) d"), x_t[:, p, :]).then_inc(s_x1_out[p], 16)
                sp.dma_start(g.normed_dram[ds(t * P, P), :], normed[:, p, :]).then_inc(s_stored[p], 16)
            pipeline(sp, T, [(load, 0), (store, 5), (load_x, 3)])
            for p in (0, 1):
                sp.wait_ge(s_stored[p], 16 * (T // 2) + 16)
                sp.wait_ge(s_x1_out[p], 16 * (T // 2) + 16)

        @block.vector
        def _(dve):
            dve.sem_inc(s_product, 2)
            dve.sem_inc(s_inv, 2)
            dve.sem_inc(s_sums, 2)
            dve.sem_inc(s_logits_read, 2)
            dve.wait_ge(s_gate, 32)
            dve.tensor_scalar(order[:], g.col_id[:, 0:X], -1.0, float(X), ALU.mult, ALU.add).then_inc(s_order, 1)
            dve.wait_ge(s_order, 1)

            def low(t, p, m):
                if isinstance(t, int) and t == T - 1:
                    dve.wait_ge(s_x1_out[p], 16 * m + 16)
                    dve.memset(x_t[:, p, :], 0.0).then_inc(s_x_pad, 1)
                dve.wait_ge(s_product, t + 3)
                dve.tensor_reduce(total[:, p, :], leaky[:, p].rearrange("p j c -> p c j"), AX, ALU.add).then_inc(s_total, 1)
                dve.wait_ge(s_high, t + 1)
                dve.tensor_tensor(weights[:, p, 1], leaky[:, p], weights[:, p, 0].bitcast(F32), ALU.subtract).then_inc(s_weights, 1)

            def add_sides(t, p, m):
                dve.wait_ge(s_left, t + 1)
                left = ps_left[:].unsqueeze(1).broadcast_to([P, T, P])
                right = g.sides[:, :, 1:2].broadcast_to([P, T, P])
                link = chain(dve, s_sums, t, 2, 2)
                link(dve.tensor_tensor(sums[:], left, right, ALU.add))
                link(dve.scalar_tensor_tensor(leaky[:, p], sums[:], NEG_SLOPE, sums[:], ALU.mult, ALU.max))

            def diagonal(t, p, m):
                dve.tensor_scalar(diag[:, p, :], g.ident[:], g.sides[:, ds(t, 1), 0:1].rearrange("p a b -> p (a b)"), None, ALU.mult).then_inc(s_diag, 1)

            def finish(t, p, m):
                dve.wait_ge(s_attended, t + 1)
                link = chain(dve, s_inv, t, 2, 2)
                link(dve.tensor_scalar(rowsum[:, p:p + 1], ps_rowsum, GAT_EPS, None, ALU.add))
                link(dve.reciprocal(inv[:, p:p + 1], rowsum[:, p:p + 1]))
                dve.tensor_scalar(below[:], ps_h[:, p, :], inv[:, p:p + 1], 0.0, ALU.mult, ALU.min).then_inc(s_below, 1)
                dve.wait_ge(s_elu_parts, 2 * t + 2)
                link = chain(dve, s_x1, t, 2)
                x1 = x_t[:, p, :]
                dve.wait_ge(s_x[p], 16 * m + 16)
                link(dve.scalar_tensor_tensor(elu[:], below[:], -1.0, above[:], ALU.add, ALU.add))
                link(dve.tensor_tensor(x1, x1, elu[:], ALU.add), g.always)
                link = chain(dve, s_stats, t, 3)
                layer_stats(dve, g, link, [x_t[:, p, a:a + HALF] for a in (0, HALF)], stats[:], mean_var[:])
                dve.wait_ge(s_std, 2 * t + 1)
                dve.reciprocal(rstd[:], std[:]).then_inc(s_std, 1)
                dve.wait_ge(s_std, 2 * t + 2)
                dve.wait_ge(s_stored[p], m * 16 + 16)
                dve.wait_ge(s_turn, t + 1)
                dve.tensor_scalar(normed[:, p, :], x1, mean_var[:, 0:1], rstd[:, 0:1], ALU.subtract, ALU.mult).then_inc(s_normed, 1)

            def route(t, p, m):
                dve.wait_ge(s_logits, t + 1)
                link = chain(dve, s_logits_read, t, 2, 2)
                link(dve.tensor_tensor(logits[:], ps_logits, gate_b[:], ALU.add))
                link(dve.tensor_reduce(neg_max[:], logits[:], AX, ALU.max, negate=True))
                dve.wait_ge(s_exps, t + 1)
                link = chain(dve, s_route, t, 5)
                link(dve.reciprocal(g.route_p[:, ds(t, 1)], exp_sum[:]))
                link(dve.tensor_reduce(exp_max[:], exps[:], AX, ALU.max))
                link(dve.scalar_tensor_tensor(ranked[:], exps[:], exp_max[:, 0:1], order[:], ALU.is_ge, ALU.mult))
                link(dve.tensor_reduce(best[:], ranked[:], AX, ALU.max))
                link(dve.tensor_scalar(flat(g.chosen[:, ds(t, 1), :]), ranked[:], best[:, 0:1], None, ALU.is_equal))
            pipeline(dve, T, [(diagonal, 0), (finish, 4), (low, 2), (add_sides, 1), (route, 5)])

        @block.gpsimd
        def _(pool):
            def weigh(t, p, m):
                pool.wait_ge(s_exp, t + 1)
                pool.wait_ge(s_counts[p], m * 16 + 16)
                pool.tensor_tensor(leaky[:, p], leaky[:, p], counts[:, p], ALU.mult).then_inc(s_product, 1)
            pipeline(pool, T, [(weigh, 0)])

        @block.scalar
        def _(act):
            for p in (0, 1):
                act.sem_inc(s_stored[p], 16)
                act.sem_inc(s_x1_out[p], 16)

            def high(t, p, m):
                act.wait_ge(s_product, t + 3)
                act.activation(weights[:, p, 0], leaky[:, p], ACT.Copy).then_inc(s_high, 1)

            def exponent(t, p, m):
                act.wait_ge(s_sums, 2 * t + 4)
                act.activation(leaky[:, p], leaky[:, p], ACT.Exp, scale=-1.0).then_inc(s_exp, 1)

            def elu_parts(t, p, m):
                act.wait_ge(s_below, t + 1)
                act.activation(above[:], ps_h[:, p, :], ACT.Relu, scale=inv[:, p:p + 1]).then_inc(s_elu_parts, 1)
                act.activation(below[:], below[:], ACT.Exp).then_inc(s_elu_parts, 1)

            def root(t, p, m):
                act.wait_ge(s_stats, 3 * t + 3)
                act.activation(std[:], mean_var[:, 1:2], ACT.Sqrt, bias=g.eps[:, 0:1]).then_inc(s_std, 1)

            def take_turned(t, p, m):
                act.wait_ge(s_turn, t + 3)
                act.activation(normed_t[:].rearrange("p k c -> p (k c)"), ps_turn[:], ACT.Copy).then_inc(s_turned, 1)

            def exps_of(t, p, m):
                act.wait_ge(s_logits_read, 2 * t + 4)
                act.activation(exps[:], logits[:], ACT.Exp, bias=neg_max[:, 0:1], accum_out=exp_sum[:]).then_inc(s_exps, 1)
            pipeline(act, T, [(elu_parts, 4), (root, 4), (high, 2), (exponent, 1), (exps_of, 5), (take_turned, 4)])

        @block.tensor
        def _(pe):
            pe.sem_inc(s_turn, 2)
            pe.wait_ge(s_gate, 32)

            def attend(t, p, m):
                pe.wait_ge(s_weights, t + 1)
                for j in range(T):
                    products(pe, ps_h[:, p, :], lambda s, j: weights[:, p, s, j, :], lambda s, j: nodes[:, j, s, :], j, j == 0, j == T - 1)
                pe.wait_ge(s_inv, 2 * t + 2)
                pe.wait_ge(s_total, t + 1)
                pe.matmul(ps_rowsum, total[:, p, :], g.ones[:, 0:1], start=True, stop=True).then_inc(s_attended, 1)

            def left(t, p, m):
                pe.wait_ge(s_diag, t + 1)
                pe.wait_ge(s_sums, 2 * t + 2)
                pe.matmul(ps_left[:], g.ones[:], diag[:, p, :], start=True, stop=True).then_inc(s_left, 1)

            def turn(t, p, m):
                pe.wait_ge(s_normed, t + 1)
                for k in range(K):
                    last = pe.transpose(ps_turn[:, k * P:(k + 1) * P], normed[:, p, k * P:(k + 1) * P], g.ident[:])
                last.then_inc(s_turn, 1)

            def gate(t, p, m):
                pe.wait_ge(s_inv, 2 * t + (5 if not isinstance(t, int) or t < T - 1 else 4))
                pe.wait_ge(s_turned, t + 1)
                for k in range(K):
                    last = pe.matmul(ps_logits, normed_t[:, k, :], gate_w[:, k, :], start=(k == 0), stop=(k == K - 1))
                last.then_inc(s_logits, 1)
            pipeline(pe, T, [(attend, 3), (gate, 5), (turn, 4), (left, 0)])


def expert_phase(nc, g, w1, b1, w2, b2):
    T, K, D, X, NP, S = g.T, g.K, g.D, g.X, g.NP, g.slot_tiles
    M = w1.shape[2]
    KM = M // P
    full = T - T % 2
    with ExitStack() as ctx:
        sb, ps, sem = makers(ctx, nc, "expert")
        rank = sb("rank", [P, T, X])
        total = sb("total", [P, T, X])
        base = sb("base", [P, T + 1, X])
        tiles_i = sb("tiles_i", [P, X], I32)
        n_tiles = sb("n_tiles", [P, X])
        ends = sb("ends", [P, X])
        first_slot = sb("first_slot", [P, X])
        place = sb("place", [P, T, X])
        slot_f = sb("slot_f", [P, T])
        beyond = sb("beyond", [P, T])
        beyond_row = sb("beyond_row", [P, 1])
        slot_written = sb("slot_written", [P, T], I32)
        passed = sb("passed", [1, S, X])
        expert_f = sb("expert_f", [1, S])
        expert_i = sb("expert_i", [1, S], I32)
        fresh_f = sb("fresh_f", [1, S])
        count_f = sb("count_f", [1, S])
        used = sb("used", [1, X])
        last_tile = sb("last_tile", [1, 1])
        tile_id = sb("tile_id", [1, S])
        fresh_i = sb("fresh_i", [1, S], I32)
        half_i = sb("half_i", [1, S], I32)
        pairs_i = sb("pairs_i", [1, 1], I32)
        unused = sb("unused", [P, D])
        no_token = sb("no_token", [S, P], I32)
        tokens = sb("tokens", [P, S], I32)
        token_col = sb("token_col", [P, 2], I32)
        w1_t = sb("w1_t", [P, 2, K, M])
        w2_t = sb("w2_t", [P, 2, KM, D])
        b1_raw = sb("b1_raw", [1, M])
        b2_raw = sb("b2_raw", [1, D])
        b1_t = sb("b1_t", [1, 2, 2, M], F32R)
        b2_t = sb("b2_t", [1, 2, 2, D], F32R)
        rows = sb("rows", [P, 2, D])
        rows_t = sb("rows_t", [P, 2, K, P])
        hidden = sb("hidden", [P, 2, M])
        hidden_t = sb("hidden_t", [P, KM, P])
        y = sb("y", [P, 2, D])
        ps_turn = ps("ps_turn", [P, D])
        ps_hidden = ps("ps_hidden", [P, M])
        ps_hidden_t = ps("ps_hidden_t", [P, M])
        ps_y = ps("ps_y", [P, 2, D])

        s_real = sem("s_real")
        s_sums = sem("s_sums")
        s_place = sem("s_place")
        s_clear = sem("s_clear")
        s_cleared = sem("s_cleared")
        s_unused = [sem("s_unused0"), sem("s_unused1")]
        s_scatter = sem("s_scatter")
        s_tokens = sem("s_tokens")
        s_token_col = sem("s_token_col")
        s_rows = [sem("s_rows0"), sem("s_rows1")]
        s_w1 = [sem("s_w1_0"), sem("s_w1_1")]
        s_w2 = [sem("s_w2_0"), sem("s_w2_1")]
        s_turn = sem("s_turn")
        s_turned = sem("s_turned")
        s_hidden = sem("s_hidden")
        s_relu = sem("s_relu")
        s_hidden_t = sem("s_hidden_t")
        s_hidden_taken = sem("s_hidden_taken")
        s_y = sem("s_y")
        s_loading = sem("s_loading")
        s_b1_raw = sem("s_b1_raw")
        s_b1_high = sem("s_b1_high")
        s_b1 = sem("s_b1")
        s_b2_raw = sem("s_b2_raw")
        s_b2_high = sem("s_b2_high")
        s_b2 = sem("s_b2")
        s_y_taken = sem("s_y_taken")
        s_y_out = [sem("s_y_out0"), sem("s_y_out1")]
        s_stored = sem("s_stored")
        block = ctx.enter_context(nc.Block())
        PLACE = 33 + T + X

        @block.sync
        def _(sp):
            def load(t, p, m):
                fresh = sp.value_load(fresh_i[0:1, ds(t, 1)], min_val=0, max_val=1)
                expert = sp.value_load(expert_i[0:1, ds(t, 1)], min_val=0, max_val=X - 1)
                half = sp.value_load(half_i[0:1, ds(t, 1)], min_val=0, max_val=1)
                sp.wait_ge(s_hidden, t + 1)
                sp.sem_inc(s_loading, 1)
                with sp.If(fresh > 0):
                    sp.dma_start(w1_t[:, ds(half, 1)].rearrange("p a k m -> p (a k) m"), w1[ds(expert, 1)].rearrange("a (k p) m -> p (a k) m", p=P)).then_inc(s_w1[p], 16)
                with sp.If(fresh < 1):
                    sp.sem_inc(s_w1[p], 16)
                sp.wait_ge(s_y, t + 1)
                sp.sem_inc(s_loading, 1)
                with sp.If(fresh > 0):
                    sp.dma_start(w2_t[:, ds(half, 1)].rearrange("p a k d -> p (a k) d"), w2[ds(expert, 1)].rearrange("a (k p) d -> p (a k) d", p=P)).then_inc(s_w2[p], 16)
                with sp.If(fresh < 1):
                    sp.sem_inc(s_w2[p], 16)

            sp.wait_ge(s_clear, 1)
            sp.dma_start(g.slot_token_dram[0:S * P].rearrange("(s p) a -> s (p a)", p=P), no_token[:]).then_inc(s_cleared, 16)
            sp.wait_ge(s_place, PLACE)
            sp.sem_inc(s_hidden, 2)
            sp.sem_inc(s_y, 2)
            load(0, 0, 0)
            sp.wait_ge(s_scatter, 16 * T)
            sp.dma_start(tokens[:], g.slot_token_dram[0:S * P].rearrange("(s p) a -> p (s a)", p=P), allow_slow_non_contiguous=True).then_inc(s_tokens, 16)
            pairs = sp.value_load(pairs_i[0:1, 0:1], min_val=0, max_val=(S - full) // 2) + full // 2
            load(1, 1, 0)
            with sp.Fori(1, pairs) as i:
                for p in (0, 1):
                    load(2 * i + p, p, i)
            sp.wait_ge(s_clear, 2)
            with sp.Fori(0, pairs) as _:
                for p in (0, 1):
                    sp.sem_inc(s_unused[p], 16)
            with sp.Fori(pairs, S // 2 + 1) as i:
                for p in (0, 1):
                    sp.dma_start(g.y_dram[ds((2 * i + p) * P, P), :], unused[:]).then_inc(s_unused[p], 16)
            for p in (0, 1):
                sp.wait_ge(s_unused[p], 16 * (S // 2 + 1))

        @block.gpsimd
        def _(pool):
            pool.memset(no_token[:], 0).then_inc(s_clear, 1)
            pool.memset(unused[:], 0.0).then_inc(s_clear, 1)
            pool.wait_ge(s_place, PLACE)
            pool.wait_ge(s_cleared, 16)
            for t in range(T):
                pool.indirect_dma_start(g.slot_token_dram, bass.IndirectOffsetOnAxis(slot_written[:, t:t + 1], 0),
                                        g.token_id[:, t:t + 1], None).then_inc(s_scatter, 16)
            pool.wait_ge(s_tokens, 16)

            def gather(t, p, m):
                pool.wait_ge(s_turn, t + 1)
                pool.tensor_copy(token_col[:, p:p + 1], tokens[:, ds(t, 1)]).then_inc(s_token_col, 1)
                wait_apart(pool, g.always, s_token_col, t + 1)
                pool.indirect_dma_start(rows[:, p, :], None, g.normed_dram, bass.IndirectOffsetOnAxis(token_col[:, p:p + 1], 0)).then_inc(s_rows[p], 16)
            pairs = pool.value_load(pairs_i[0:1, 0:1], min_val=0, max_val=(S - full) // 2) + full // 2
            pipeline(pool, S, [(gather, 0)], pairs)

        @block.vector
        def _(dve):
            dve.tensor_tensor(g.chosen[:], g.chosen[:], g.exists[:].unsqueeze(2).broadcast_to([P, T, X]), ALU.mult).then_inc(s_real, 1)
            dve.wait_ge(s_sums, 1)
            link = chain(dve, s_place, 0, PLACE)
            link(dve.tensor_copy(rank[:].rearrange("p t e -> p (t e)"), ps_turn[:, 0:T * X]))
            link(dve.tensor_copy(total[:].rearrange("p t e -> p (t e)"), ps_turn[:, HALF:HALF + T * X]))
            link(dve.memset(base[:, 0, :], 0.0))
            for t in range(T):
                link(dve.tensor_tensor(base[:, t + 1, :], base[:, t, :], total[:, t, :], ALU.add))
            link(dve.tensor_scalar(tiles_i[:], base[:, T, :], float(P - 1), None, ALU.add))
            link(dve.tensor_scalar(tiles_i[:], tiles_i[:], 7, None, ALU.arith_shift_right))
            link(dve.tensor_copy(n_tiles[:], tiles_i[:]))
            link(dve.tensor_copy(ends[:, 0:1], n_tiles[:, 0:1]))
            for e in range(1, X):
                link(dve.tensor_tensor(ends[:, e:e + 1], ends[:, e - 1:e], n_tiles[:, e:e + 1], ALU.add))
            link(dve.tensor_tensor(first_slot[:], ends[:], n_tiles[:], ALU.subtract))
            link(dve.tensor_scalar(first_slot[:], first_slot[:], float(P), None, ALU.mult))
            link(dve.tensor_tensor(place[:], rank[:], base[:, 0:T, :], ALU.add))
            link(dve.tensor_tensor(place[:], place[:], first_slot[:].unsqueeze(1).broadcast_to([P, T, X]), ALU.add))
            link(dve.tensor_tensor(place[:], place[:], g.chosen[:], ALU.mult))
            link(dve.tensor_reduce(slot_f[:], place[:], AX, ALU.add))
            link(dve.tensor_copy(g.slot[:], slot_f[:]))
            link(dve.tensor_scalar(beyond[:], g.exists[:], -1.0, -1.0, ALU.add, ALU.mult))
            link(dve.tensor_scalar(beyond_row[:], g.row_id[:], float(S * P), None, ALU.add))
            link(dve.tensor_scalar(beyond[:], beyond[:], beyond_row[:, 0:1], None, ALU.mult))
            link(dve.tensor_tensor(slot_written[:], slot_f[:], beyond[:], ALU.add))
            link(dve.tensor_scalar(last_tile[:], ends[0:1, X - 1:X], 1.0, None, ALU.subtract))
            link(dve.tensor_scalar(tile_id[:], g.col_id[0:1, 0:S], last_tile[:, 0:1], None, ALU.min))
            link(dve.tensor_tensor(passed[:], ends[0:1, :].unsqueeze(1).broadcast_to([1, S, X]),
                                   tile_id[:].unsqueeze(2).broadcast_to([1, S, X]), ALU.is_le))
            link(dve.tensor_reduce(expert_f[:], passed[:], AX, ALU.add))
            link(dve.tensor_copy(expert_i[:], expert_f[:]))
            link(dve.memset(fresh_f[:, 0:1], 1.0))
            link(dve.tensor_tensor(fresh_f[:, 1:S], expert_f[:, 1:S], expert_f[:, 0:S - 1], ALU.is_gt))
            link(dve.tensor_copy(fresh_i[:], fresh_f[:]))
            link(dve.tensor_scalar(used[:], n_tiles[0:1, :], 1.0, None, ALU.min))
            link(dve.tensor_tensor(passed[:], passed[:], used[:].unsqueeze(1).broadcast_to([1, S, X]), ALU.mult))
            link(dve.tensor_reduce(count_f[:], passed[:], AX, ALU.add))
            link(dve.tensor_copy(half_i[:], count_f[:]))
            link(dve.tensor_scalar(half_i[:], half_i[:], 1, None, ALU.bitwise_and))
            link(dve.tensor_scalar(pairs_i[:], ends[0:1, X - 1:X], 1.0, None, ALU.add))
            link(dve.tensor_scalar(pairs_i[:], pairs_i[:], 1, None, ALU.arith_shift_right))
            link(dve.tensor_scalar(pairs_i[:], pairs_i[:], full // 2, None, ALU.subtract))

            dve.wait_ge(s_place, PLACE)

            def take_hidden_t(t, p, m):
                dve.wait_ge(s_hidden_t, t + 1)
                dve.tensor_copy(hidden_t[:].rearrange("p k c -> p (k c)"), ps_hidden_t[:]).then_inc(s_hidden_taken, 1)

            def b1_low(t, p, m):
                dve.wait_ge(s_b1_high, t + 1)
                dve.tensor_tensor(b1_t[:, p, 1, :], b1_raw[:], b1_t[:, p, 0, :].bitcast(F32), ALU.subtract).then_inc(s_b1, 1)

            def b2_low(t, p, m):
                dve.wait_ge(s_b2_high, t + 1)
                dve.tensor_tensor(b2_t[:, p, 1, :], b2_raw[:], b2_t[:, p, 0, :].bitcast(F32), ALU.subtract).then_inc(s_b2, 1)

            def take_y(t, p, m):
                dve.wait_ge(s_y, t + 3)
                dve.wait_ge(s_y_out[p], m * 16 + 16)
                dve.tensor_copy(y[:, p, :], ps_y[:, p, :]).then_inc(s_y_taken, 1)
            pairs = dve.value_load(pairs_i[0:1, 0:1], min_val=0, max_val=(S - full) // 2) + full // 2
            pipeline(dve, S, [(take_hidden_t, 2), (b1_low, 0), (b2_low, 1), (take_y, 2)], pairs)

        @block.scalar
        def _(act):
            for p in (0, 1):
                act.sem_inc(s_y_out[p], 16)

            def take_turned(t, p, m):
                act.wait_ge(s_turn, t + 3)
                act.wait_ge(s_hidden, t + 1)
                act.activation(rows_t[:, p].rearrange("p k c -> p (k c)"), ps_turn[:], ACT.Copy).then_inc(s_turned, 1)

            def load_b1(t, p, m):
                expert = act.value_load(expert_i[0:1, ds(t, 1)], min_val=0, max_val=X - 1)
                act.wait_ge(s_b1, t + 1)
                act.dma_start(b1_raw[:], b1[ds(expert, 1), :]).then_inc(s_b1_raw, 16)

            def load_b2(t, p, m):
                expert = act.value_load(expert_i[0:1, ds(t, 1)], min_val=0, max_val=X - 1)
                act.wait_ge(s_b2, t + 1)
                act.dma_start(b2_raw[:], b2[ds(expert, 1), :]).then_inc(s_b2_raw, 16)

            def b1_high(t, p, m):
                act.wait_ge(s_b1_raw, 16 * t + 16)
                act.wait_ge(s_hidden, t + 1)
                act.activation(b1_t[:, p, 0, :], b1_raw[:], ACT.Copy).then_inc(s_b1_high, 1)

            def b2_high(t, p, m):
                act.wait_ge(s_b2_raw, 16 * t + 16)
                act.wait_ge(s_y, t + 1)
                act.activation(b2_t[:, p, 0, :], b2_raw[:], ACT.Copy).then_inc(s_b2_high, 1)

            def relu(t, p, m):
                act.wait_ge(s_hidden, t + 3)
                act.activation(hidden[:, p, :], ps_hidden[:], ACT.Relu).then_inc(s_relu, 1)

            def store(t, p, m):
                act.wait_ge(s_y_taken, t + 3)
                act.dma_start(g.y_dram[ds(t * P, P), :], y[:, p, :]).then_inc(s_y_out[p], 16)
            act.wait_ge(s_place, PLACE)
            pairs = act.value_load(pairs_i[0:1, 0:1], min_val=0, max_val=(S - full) // 2) + full // 2
            pipeline(act, S, [(load_b1, 0), (load_b2, 1), (take_turned, 0), (relu, 1), (store, 3), (b1_high, 0), (b2_high, 1)], pairs)
            for p in (0, 1):
                act.wait_ge(s_y_out[p], 16 * pairs + 16)
            act.sem_inc(s_stored, 1)

        @block.tensor
        def _(pe):
            chosen = g.chosen[:].rearrange("p t e -> p (t e)")
            pe.wait_ge(s_real, 1)
            pe.matmul(ps_turn[:, 0:T * X], g.before[:], chosen, start=True, stop=True)
            pe.matmul(ps_turn[:, HALF:HALF + T * X], g.ones[:], chosen, start=True, stop=True).then_inc(s_sums, 1)
            pe.wait_ge(s_place, 2)
            pe.sem_inc(s_turn, 2)
            pe.sem_inc(s_turned, 1)

            def turn(t, p, m):
                pe.wait_ge(s_rows[p], m * 16 + 16)
                pe.wait_ge(s_turned, t + 1)
                for k in range(K):
                    last = pe.transpose(ps_turn[:, k * P:(k + 1) * P], rows[:, p, k * P:(k + 1) * P], g.ident[:])
                last.then_inc(s_turn, 1)

            def half_of(t):
                return pe.value_load(half_i[0:1, ds(t, 1)], min_val=0, max_val=1)

            def first(t, p, m):
                w = w1_t[:, ds(half_of(t), 1)]
                pe.wait_ge(s_w1[p], m * 16 + 16)
                pe.wait_ge(s_turned, t + 2)
                pe.wait_ge(s_relu, t + 1)
                pe.wait_ge(s_b1, t + 2)
                for side in (0, 1):
                    pe.matmul(ps_hidden[:], g.ones_r[0:1, :], b1_t[0:1, p, side, :], start=(side == 0), stop=False)
                for k in range(K):
                    last = pe.matmul(ps_hidden[:], rows_t[:, p, k, :], w[:, 0, k, :], start=False, stop=(k == K - 1))
                last.then_inc(s_hidden, 1)

            def turn_hidden(t, p, m):
                pe.wait_ge(s_relu, t + 2)
                pe.wait_ge(s_hidden_taken, t + 1)
                for k in range(KM):
                    last = pe.transpose(ps_hidden_t[:, k * P:(k + 1) * P], hidden[:, p, k * P:(k + 1) * P], g.ident[:])
                last.then_inc(s_hidden_t, 1)

            def second(t, p, m):
                w = w2_t[:, ds(half_of(t), 1)]
                pe.wait_ge(s_w2[p], m * 16 + 16)
                pe.wait_ge(s_hidden_taken, t + 2)
                pe.wait_ge(s_y_taken, t + 1)
                pe.wait_ge(s_b2, t + 2)
                for a in range(0, D, HALF):
                    for side in (0, 1):
                        pe.matmul(ps_y[:, p, a:a + HALF], g.ones_r[0:1, :], b2_t[0:1, p, side, a:a + HALF], start=(side == 0), stop=False)
                    for k in range(KM):
                        last = pe.matmul(ps_y[:, p, a:a + HALF], hidden_t[:, k, :], w[:, 0, k, a:a + HALF], start=False, stop=(k == KM - 1))
                last.then_inc(s_y, 1)
            pe.sem_inc(s_relu, 1)
            pe.sem_inc(s_b1, 1)
            pe.sem_inc(s_b2, 1)
            pe.sem_inc(s_hidden_taken, 1)
            pe.sem_inc(s_y_taken, 2)
            pe.wait_ge(s_place, PLACE)
            pairs = pe.value_load(pairs_i[0:1, 0:1], min_val=0, max_val=(S - full) // 2) + full // 2
            pipeline(pe, S, [(turn_hidden, 2), (turn, 0), (first, 1), (second, 2)], pairs)


def neighbour_phase(nc, g, n, w_source, w, nodes, ffn_sources):
    T, K, D = g.T, g.K, g.D
    with ExitStack() as ctx:
        sb, ps, sem = makers(ctx, nc, f"neighbour{n}")
        feat_t = sb("feat_t", [P, 2, 2, K, P], F32R)
        ps_turn = ps("ps_turn", [P, D])
        ps_out = ps("ps_out", [P, 2, D])
        s_out = sem("s_out")
        s_kept_high = sem("s_kept_high")
        s_kept = sem("s_kept")
        s_feat = [sem("s_feat0"), sem("s_feat1")]
        s_feat_t = sem("s_feat_t")
        if n == 1:
            rows = sb("rows", [P, g.w_tiles, D])
            split = Split((sb, ps, sem), rows, w)
            w_scale = sb("w_scale", [P, D // W_BLOCK])
            w_inv = sb("w_inv", [P, D // W_BLOCK])
            s_rows = sem("s_rows")
            s_quant = sem("s_quant")
            s_rows_out = sem("s_rows_out")
        else:
            split = Split((sb, ps, sem), sb("w_raw", [P, 4, D]), w)
            widest = sb("widest", [P, 1])
            s_widest_turn = sem("s_widest_turn")
            slot_col = sb("slot_col", [P, 2], I32)
            y = sb("y", [P, 2, D])
            x2 = sb("x2", [P, 2, D])
            stats = sb("stats", [P, 12])
            mean_var = sb("mean_var", [P, 2])
            std = sb("std", [P, 1])
            rstd = sb("rstd", [P, 1])
            normed = sb("normed", [P, 2, D])
            s_deg = sem("s_deg")
            s_col = sem("s_col")
            s_y = [sem("s_y0"), sem("s_y1")]
            s_x = [sem("s_x0"), sem("s_x1")]
            s_added = sem("s_added")
            s_stats = sem("s_stats")
            s_std = sem("s_std")
            s_normed = sem("s_normed")
            s_turn = sem("s_turn")
            s_high = sem("s_high")
            s_x2_out = [sem("s_x2_out0"), sem("s_x2_out1")]
        block = ctx.enter_context(nc.Block())

        @block.sync
        def _(sp):
            def load(t, p, m):
                sp.wait_ge(s_out, t + 1)
                sp.dma_start(feat_t[:, p].rearrange("p s k c -> p (s k c)").bitcast(F32), g.nodes_t_dram[1][ds(t, 1)].rearrange("a p n -> (a p) n")).then_inc(s_feat[p], 16)

            def load_x1(t, p, m):
                sp.wait_ge(s_x2_out[p], 16 * m + 16)
                sp.dma_start(x2[:, p, :], g.x1_dram[ds(t, 1)].rearrange("a p d -> (a p) d")).then_inc(s_x[p], 16)

            def store_x2(t, p, m):
                sp.wait_ge(s_normed, t + 1)
                sp.dma_start(g.x2_dram[ds(t, 1)].rearrange("a p d -> (a p) d"), x2[:, p, :]).then_inc(s_x2_out[p], 16)

            def store_features(t, p, m):
                sp.wait_ge(s_feat_t, t + 2)
                sp.dma_start(g.nodes_t_dram[0][ds(t, 1)].rearrange("a p n -> (a p) n"), feat_t[:, p].rearrange("p s k c -> p (s k c)").bitcast(F32)).then_inc(s_feat[p], 16)
            if n:
                load(0, 0, 0)
            else:
                load_x1(0, 0, 0)
                load_x1(1, 1, 0)
            split.load(sp, w_source)
            if n:
                load(1, 1, 0)
                load(2, 0, 1)
                load(3, 1, 1)
                split.ready(sp)
                at = 0
                for source in ffn_sources:
                    rows_of = source.rearrange("(o p) i -> p o i", p=P)
                    width = rows_of.shape[1] * rows_of.shape[2]
                    sp.dma_start(flat(rows)[:, at:at + width].rearrange("p (o i) -> p o i", i=rows_of.shape[2]), rows_of).then_inc(s_rows, 16)
                    at += width
                with sp.Fori(2, T // 2) as i:
                    for p in (0, 1):
                        load(2 * i + p, p, i)
                third = g.w_tiles // 3
                for c in range(3):
                    here = slice(c * third, (c + 1) * third)
                    sp.wait_ge(s_quant, 7 * third * (c + 1))
                    sp.dma_start(g.w_rows_dram[:, here, :], rows[:, here, :]).then_inc(s_rows_out, 16)
                sp.wait_ge(s_rows_out, 48)
            else:
                def load_next(t, p, m):
                    if not (isinstance(t, int) and t < 2):
                        load_x1(t, p, m)
                pipeline(sp, T, [(load_next, 0), (store_x2, 1), (store_features, 1)])
                for p in (0, 1):
                    sp.wait_ge(s_x2_out[p], 16 * (T // 2) + 16)
                    sp.wait_ge(s_feat[p], 16 * (T // 2) + 16)

        if n == 0:
            @block.gpsimd
            def _(pool):
                def gather(t, p, m):
                    pool.wait_ge(s_added, t + 1)
                    pool.tensor_copy(slot_col[:, p:p + 1], g.slot[:, ds(t, 1)]).then_inc(s_col, 1)
                    wait_apart(pool, g.always, s_col, t + 1)
                    pool.indirect_dma_start(y[:, p, :], None, g.y_dram, bass.IndirectOffsetOnAxis(slot_col[:, p:p + 1], 0)).then_inc(s_y[p], 16)
                pipeline(pool, T, [(gather, 0)])

        @block.vector
        def _(dve):
            if n == 0:
                dve.sem_inc(s_added, 2)
                link = chain(dve, s_deg, 0, 5)
                link(dve.tensor_reduce(widest[:], g.deg[:], AX, ALU.max))
                dve.wait_ge(s_widest_turn, 1)
                link(dve.tensor_reduce(widest[0:1, :], ps_turn[0:1, 0:P], AX, ALU.max))
                link(dve.tensor_scalar(g.many_i[:], widest[0:1, :], 4096.0, None, ALU.is_gt))
                link(dve.tensor_scalar(g.deg[:], g.deg[:], 1.0, None, ALU.max))
                link(dve.reciprocal(g.deg[:], g.deg[:]))

            def weights(t, p, m):
                if isinstance(t, int) and t == 0:
                    split.low(dve)

            def add(t, p, m):
                x = x2[:, p, :]
                dve.wait_ge(s_x[p], m * 16 + 16)
                dve.wait_ge(s_y[p], m * 16 + 16)
                dve.scalar_tensor_tensor(x, y[:, p, :], g.route_p[:, ds(t, 1)], x, ALU.mult, ALU.add).then_inc(s_added, 1)
                wait_apart(dve, g.always, s_added, t + 3)
                link = chain(dve, s_stats, t, 3)
                layer_stats(dve, g, link, [x2[:, p, a:a + HALF] for a in (0, HALF)], stats[:], mean_var[:])
                dve.wait_ge(s_std, 2 * t + 1)
                dve.reciprocal(rstd[:], std[:]).then_inc(s_std, 1)
                dve.wait_ge(s_std, 2 * t + 2)
                dve.tensor_scalar(normed[:, p, :], x, mean_var[:, 0:1], rstd[:, 0:1], ALU.subtract, ALU.mult).then_inc(s_normed, 1)

            def low(t, p, m):
                dve.wait_ge(s_high, t + 1)
                dve.tensor_tensor(feat_t[:, p, 1].rearrange("p k c -> p (k c)"), ps_turn[:],
                                  feat_t[:, p, 0].rearrange("p k c -> p (k c)").bitcast(F32), ALU.subtract).then_inc(s_feat_t, 1)

            def keep(t, p, m):
                dve.wait_ge(s_kept_high, t + 1)
                dve.tensor_tensor(flat(nodes[:, ds(t, 1), 1, :]), ps_out[:, p, :], flat(nodes[:, ds(t, 1), 0, :]).bitcast(F32), ALU.subtract).then_inc(s_kept, 1)

            def quantise_weights(t, p, m):
                if isinstance(t, int) and t >= g.w_tiles:
                    return
                if isinstance(t, int) and t == 0:
                    dve.wait_ge(s_rows, 16 * len(ffn_sources))
                link = chain(dve, s_quant, t, 7)
                value = flat(rows[:, ds(t, 1), :]).rearrange("p (b c) -> p b c", c=W_BLOCK)
                wide = [P, D // W_BLOCK, W_BLOCK]
                scale = w_scale[:].unsqueeze(2).broadcast_to(wide)
                inv = w_inv[:].unsqueeze(2).broadcast_to(wide)
                link(dve.tensor_reduce(w_scale[:], value, AX, ALU.max, apply_absolute_value=True))
                link(dve.tensor_scalar(w_scale[:], w_scale[:], 1.0 / W_MAX, 1e-12, ALU.mult, ALU.max))
                link(dve.reciprocal(w_inv[:], w_scale[:]))
                link(dve.tensor_tensor(value, value, inv, ALU.mult))
                link(dve.tensor_scalar(value, value, ROUND, ROUND, ALU.add, ALU.subtract))
                link(dve.tensor_scalar(value, value, -W_MAX - 1.0, W_MAX, ALU.max, ALU.min))
                link(dve.tensor_tensor(value, value, scale, ALU.mult))
            if n == 0:
                pipeline(dve, T, [(low, 1), (add, 0), (weights, 1), (keep, 2)])
            else:
                split.low(dve)
                assert g.w_tiles <= T
                pipeline(dve, T, [(keep, 2), (quantise_weights, 3)], last_apart=True)

        @block.scalar
        def _(act):
            def weights(t, p, m):
                if isinstance(t, int) and t == 0:
                    split.high(act)

            def root(t, p, m):
                act.wait_ge(s_stats, 3 * t + 3)
                act.activation(std[:], mean_var[:, 1:2], ACT.Sqrt, bias=g.eps[:, 0:1]).then_inc(s_std, 1)

            def high(t, p, m):
                act.wait_ge(s_turn, t + 1)
                act.wait_ge(s_feat[p], 16 * m + 16)
                act.activation(feat_t[:, p, 0].rearrange("p k c -> p (k c)"), ps_turn[:], ACT.Copy).then_inc(s_high, 1)

            def keep_high(t, p, m):
                act.wait_ge(s_out, t + 3)
                act.activation(flat(nodes[:, ds(t, 1), 0, :]), ps_out[:, p, :], ACT.Copy).then_inc(s_kept_high, 1)
            if n == 0:
                for p in (0, 1):
                    act.sem_inc(s_feat[p], 16)
                    act.sem_inc(s_x2_out[p], 16)
            pipeline(act, T, [(weights, 0), (keep_high, 2)] if n else [(high, 1), (root, 0), (weights, 1), (keep_high, 2)])

        @block.tensor
        def _(pe):
            pe.sem_inc(s_kept, 2)
            pe.sem_inc(s_out, 2)
            if n == 0:
                pe.wait_ge(s_deg, 1)
                pe.transpose(ps_turn[0:1, 0:P], widest[:], g.ident[:]).then_inc(s_widest_turn, 1)
                pe.wait_ge(s_deg, 2)
                pe.sem_inc(s_feat_t, 1)

            def turn(t, p, m):
                pe.wait_ge(s_normed, t + 1)
                pe.wait_ge(s_feat_t, t + 1)
                for k in range(K):
                    last = pe.transpose(ps_turn[:, k * P:(k + 1) * P], normed[:, p, k * P:(k + 1) * P], g.ident[:])
                last.then_inc(s_turn, 1)

            def multiply(t, p, m):
                if n:
                    pe.wait_ge(s_feat[p], 16 * m + 16)
                else:
                    pe.wait_ge(s_feat_t, t + 2)
                pe.wait_ge(s_kept, t + 1)
                for k in range(K):
                    if isinstance(t, int) and t == 0:
                        split.ready(pe, k)
                    last = products(pe, ps_out[:, p, :], lambda s, k: feat_t[:, p, s, k, :], lambda s, k: w[:, s, k, :], k, k == 0, k == K - 1)
                last.then_inc(s_out, 1)
            pipeline(pe, T, [(multiply, 1)] if n else [(turn, 0), (multiply, 1)])


def aggregate_phase(nc, g, n, w_source, bias, w, nodes):
    T, K, D = g.T, g.K, g.D
    last = n == 1
    with ExitStack() as ctx:
        sb, ps, sem = makers(ctx, nc, f"aggregate{n}")
        work = sb("work", [P, 3, D])
        split = Split((sb, ps, sem), work, w)
        bias_rows = sb("bias_rows", [P, D])
        counts_raw = sb("counts_raw", [P, T, P])
        counts = sb("counts", [P, 2, T, P], F32R)
        counts_rest = sb("counts_rest", [P, T, P], F32R)
        feat_t = sb("feat_t", [P, 2, 2, K, P], F32R)
        x3 = sb("x3", [P, 2, D]) if last else None
        out_t = None if last else sb("out_t", [P, 2, K, P], F32R)
        stats = sb("stats", [P, 12])
        std = sb("std", [P, 1])
        rstd = sb("rstd", [P, 1])
        ps_sum = ps("ps_sum", [P, D])
        ps_own = ps("ps_own", [P, D])
        ps_turn = ps("ps_turn", [P, D])

        s_bias = sem("s_bias")
        s_raw = sem("s_raw")
        s_counts_high = sem("s_counts_high")
        s_counts = sem("s_counts")
        s_feat = [sem("s_feat0"), sem("s_feat1")]
        s_summed = sem("s_summed")
        s_mean = sem("s_mean")
        s_own = sem("s_own")
        s_out = sem("s_out")
        s_relu = sem("s_relu")
        s_turn = sem("s_turn")
        s_high = sem("s_high")
        s_out_t = sem("s_out_t")
        s_x2 = [sem("s_x2_0"), sem("s_x2_1")]
        s_x3 = sem("s_x3")
        s_stored = [sem("s_stored0"), sem("s_stored1")]
        s_std = sem("s_std")
        s_largest = sem("s_largest")
        block = ctx.enter_context(nc.Block())

        @block.sync
        def _(sp):
            sp.sem_inc(s_own, 2)
            sp.sem_inc(s_counts, 1)

            def load(t, p, m):
                sp.wait_ge(s_counts, t + 1)
                sp.dma_start(counts_raw[:].rearrange("p j c -> p (j c)"), g.turned_dram[ds(t, 1)].rearrange("a p n -> (a p) n")).then_inc(s_raw, 16)
                sp.wait_ge(s_own, t + 1)
                sp.dma_start(feat_t[:, p].rearrange("p s k c -> p (s k c)").bitcast(F32), g.nodes_t_dram[n][ds(t, 1)].rearrange("a p n -> (a p) n")).then_inc(s_feat[p], 16)

            def load_next(t, p, m):
                if isinstance(t, int) and t == 0:
                    return
                load(t, p, m)

            def load_x2(t, p, m):
                sp.wait_ge(s_stored[p], 16 * m + 16)
                sp.dma_start(x3[:, p, :], g.x2_dram[ds(t, 1)].rearrange("a p d -> (a p) d")).then_inc(s_x2[p], 16)

            def store_x3(t, p, m):
                sp.wait_ge(s_largest, 8 * t + 7)
                sp.dma_start(g.x3_dram[ds(t, 1)].rearrange("a p d -> (a p) d"), x3[:, p, :]).then_inc(s_stored[p], 16)

            def store_out(t, p, m):
                sp.wait_ge(s_out_t, t + 2)
                sp.dma_start(g.nodes_t_dram[1][ds(t, 1)].rearrange("a p n -> (a p) n"), out_t[:].rearrange("p s k c -> p (s k c)").bitcast(F32)).then_inc(s_stored[0], 16)
            load(0, 0, 0)
            sp.dma_start(bias_rows[:], bias.rearrange("(a d) -> a d", a=1).broadcast_to([P, D])).then_inc(s_bias, 16)
            split.load(sp, w_source)
            if last:
                pipeline(sp, T, [(load_next, 0), (load_x2, 1), (store_x3, 2)])
                for p in (0, 1):
                    sp.wait_ge(s_stored[p], 16 * (T // 2) + 16)
            else:
                pipeline(sp, T, [(load_next, 0), (store_out, 3)])
                sp.wait_ge(s_stored[0], 16 * T + 16)

        @block.scalar
        def _(act):
            for p in (0, 1):
                act.sem_inc(s_stored[p], 16)

            def counts_high(t, p, m):
                act.wait_ge(s_raw, 16 * t + 16)
                act.wait_ge(s_summed, t + 1)
                act.activation(counts[:, p], counts_raw[:], ACT.Copy).then_inc(s_counts_high, 1)

            def relu(t, p, m):
                act.wait_ge(s_out, t + 2)
                act.activation(work[:, 1, :], work[:, 0, :], ACT.Relu).then_inc(s_relu, 1)

            def out_high(t, p, m):
                act.wait_ge(s_turn, t + 1)
                act.wait_ge(s_stored[0], 16 * t + 16)
                act.activation(out_t[:, 0].rearrange("p k c -> p (k c)"), ps_turn[:], ACT.Copy).then_inc(s_high, 1)

            def root(t, p, m):
                act.wait_ge(s_largest, 8 * t + 3)
                act.activation(std[:], g.mean_var[:, 1:2], ACT.Sqrt, bias=g.eps[:, 0:1]).then_inc(s_std, 1)

            def weights(t, p, m):
                if isinstance(t, int) and t == 0:
                    split.high(act)
            pipeline(act, T, [(counts_high, 0), (weights, 0), (root, 1)] if last else
                     [(counts_high, 0), (weights, 0), (out_high, 2), (relu, 1)])

        @block.vector
        def _(dve):
            def counts_low(t, p, m):
                dve.wait_ge(s_counts_high, t + 1)
                dve.tensor_tensor(counts_rest[:], counts_raw[:], counts[:, p].bitcast(F32), ALU.subtract).then_inc(s_counts, 1)

            def mean(t, p, m):
                dve.wait_ge(s_summed, t + 3)
                if not last:
                    dve.wait_ge(s_relu, t + 1)
                dve.scalar_tensor_tensor(work[:, 0, :], ps_sum[:], g.deg[:, ds(t, 1)], bias_rows[:], ALU.mult, ALU.add).then_inc(s_mean, 1)

            def add(t, p, m):
                dve.wait_ge(s_own, t + 3)
                dve.wait_ge(s_mean, t + 2)
                dve.tensor_tensor(work[:, 0, :], work[:, 0, :], ps_own[:], ALU.add).then_inc(s_out, 1)

            def out_low(t, p, m):
                dve.wait_ge(s_high, t + 1)
                dve.tensor_tensor(out_t[:, 1].rearrange("p k c -> p (k c)"), ps_turn[:],
                                  out_t[:, 0].rearrange("p k c -> p (k c)").bitcast(F32), ALU.subtract).then_inc(s_out_t, 1)

            def finish(t, p, m):
                dve.wait_ge(s_out, t + 2)
                dve.wait_ge(s_x2[p], 16 * m + 16)
                dve.tensor_tensor(x3[:, p, :], x3[:, p, :], work[:, 0, :], ALU.add).then_inc(s_x3, 1)
                wait_apart(dve, g.always, s_x3, t + 1)
                link = chain(dve, s_largest, t, 8)
                layer_stats(dve, g, link, [x3[:, p, a:a + HALF] for a in (0, HALF)], stats[:], g.mean_var[:])
                dve.wait_ge(s_std, t + 1)
                link(dve.reciprocal(rstd[:], std[:]))
                link(dve.tensor_copy(g.means[:, ds(t, 1)], g.mean_var[:, 0:1]))
                link(dve.tensor_copy(g.rstds[:, ds(t, 1)], rstd[:]))
                link(dve.tensor_scalar(work[:, 1, :], x3[:, p, :], g.mean_var[:, 0:1], rstd[:, 0:1], ALU.subtract, ALU.mult))
                link(dve.tensor_reduce(g.largest[:, ds(t, 1)], work[:, 1, :], AX, ALU.max, apply_absolute_value=True))

            def weights(t, p, m):
                if isinstance(t, int) and t == 0:
                    split.low(dve)
                    split.ready(dve)
            dve.wait_ge(s_bias, 16)
            pipeline(dve, T, [(mean, 1), (counts_low, 0), (weights, 0), (add, 1), (finish, 1)] if last else
                     [(mean, 1), (counts_low, 0), (weights, 0), (out_low, 2), (add, 1)])

        @block.tensor
        def _(pe):
            pe.sem_inc(s_summed, 2)
            pe.sem_inc(s_mean, 1)
            pe.sem_inc(s_out, 1)
            pe.sem_inc(s_out_t, 1)
            pe.sem_inc(s_relu, 1)
            more = pe.value_load(g.many_i[0:1, 0:1], min_val=0, max_val=1)

            def add_up(t, p, m):
                pe.wait_ge(s_counts, t + 2)
                pe.wait_ge(s_mean, t + 1)

                def term(left, r, j, start, stop):
                    for a in range(0, D, HALF):
                        last_mm = pe.matmul(ps_sum[:, a:a + HALF], left[:, j, :], nodes[:, j, r, a:a + HALF], start=start, stop=stop)
                    return last_mm
                high = counts[:, p]
                for j in range(T):
                    term(high, 0, j, j == 0, False)
                    if j < T - 1:
                        term(high, 1, j, False, False)
                with pe.If(more > 0):
                    for j in range(T):
                        term(counts_rest, 0, j, False, False)
                term(high, 1, T - 1, False, True).then_inc(s_summed, 1)

            def turn(t, p, m):
                pe.wait_ge(s_relu, t + 2)
                pe.wait_ge(s_out_t, t + 1)
                for k in range(K):
                    last_mm = pe.transpose(ps_turn[:, k * P:(k + 1) * P], work[:, 1, k * P:(k + 1) * P], g.ident[:])
                last_mm.then_inc(s_turn, 1)

            def own(t, p, m):
                pe.wait_ge(s_feat[p], 16 * m + 16)
                pe.wait_ge(s_out, t + 1)
                for k in range(K):
                    if isinstance(t, int) and t == 0:
                        split.ready(pe, k)
                    last_mm = products(pe, ps_own[:], lambda s, k: feat_t[:, p, s, k, :], lambda s, k: w[:, s, k, :], k, k == 0, k == K - 1)
                last_mm.then_inc(s_own, 1)
            pipeline(pe, T, [(add_up, 1), (own, 1)] if last else [(add_up, 1), (turn, 2), (own, 1)])


def quantised(dve, link, out, value, inv_scale, scale, low, high):
    link(dve.tensor_scalar(out, value, inv_scale, ROUND, ALU.mult, ALU.add))
    link(dve.tensor_scalar(out, out, ROUND, high, ALU.subtract, ALU.min))
    link(dve.tensor_scalar(out, out, low, scale, ALU.max, ALU.mult))


def feed_forward_phase(nc, g, out):
    T, K, D, N = g.T, g.K, g.D, g.N
    I = g.I
    KI = I // P
    BLOCKS = D // P
    with ExitStack() as ctx:
        sb, ps, sem = makers(ctx, nc, "ffn")
        rows = sb("rows", [P, g.w_tiles, D])
        w_t = sb("w_t", [P, 2, g.w_tiles * BLOCKS, P], F32R)
        x3 = sb("x3", [P, T, D])
        gate_up = flat(rows)[:, 0:2 * T * I].rearrange("p (s t i) -> p s t i", s=2, t=T)
        normed = sb("normed", [P, 2, D])
        normed_t = sb("normed_t", [P, 2, 2, K, P], F32R)
        largest = sb("largest", [P, 3, T])
        widest = sb("widest", [P, 1])
        top = sb("top", [1, 1])
        scales = sb("scales", [P, 5, 2])
        sig = sb("sig", [P, T, I])
        o_t = sb("o_t", [P, 2, 2, KI, P], F32R)
        result = sb("result", [P, 2, D])
        ps_turn = ps("ps_turn", [P, D])
        ps_gate_up = ps("ps_gate_up", [P, 2, 2, HALF])
        ps_scale = ps("ps_scale", [P, HALF])
        ps_down = ps_gate_up

        s_rows = [sem(f"s_rows{c}") for c in range(3)]
        s_x3_first = sem("s_x3_first")
        s_x3 = sem("s_x3")
        s_w_turn = sem("s_w_turn")
        s_w_high = sem("s_w_high")
        s_w = sem("s_w")
        s_widest = sem("s_widest")
        s_level = sem("s_level")
        s_scaled = sem("s_scaled")
        s_quant = sem("s_quant")
        s_normed = sem("s_normed")
        s_turn = sem("s_turn")
        s_high = sem("s_high")
        s_turned = sem("s_turned")
        s_gate_up = sem("s_gate_up")
        s_gate_up_kept = sem("s_gate_up_kept")
        s_largest = sem("s_largest")
        s_all = sem("s_all")
        s_sig = sem("s_sig")
        s_o = sem("s_o")
        s_o_turn = sem("s_o_turn")
        s_o_high = sem("s_o_high")
        s_o_t = sem("s_o_t")
        s_down = sem("s_down")
        s_result = sem("s_result")
        s_out = [sem("s_out0"), sem("s_out1")]
        block = ctx.enter_context(nc.Block())

        def weight(s, side, k):
            blocks = w_t[:, s, side * KI * K:(side + 1) * KI * K, :]
            return blocks.rearrange("p (i k) c -> p k i c", k=K)[:, k]

        def down_weight(s, k):
            blocks = w_t[:, s, 2 * KI * K:, :]
            return blocks.rearrange("p (o k) c -> p k o c", k=KI)[:, k]

        @block.sync
        def _(sp):
            third = g.w_tiles // 3
            for c in range(3):
                here = slice(c * third, (c + 1) * third)
                sp.dma_start(rows[:, here, :], g.w_rows_dram[:, here, :]).then_inc(s_rows[c], 16)
                if c == 0:
                    sp.dma_start(x3[:, 0:2, :], g.x3_dram[0:2].rearrange("t p d -> p t d")).then_inc(s_x3_first, 16)
            sp.dma_start(x3[:, 2:T, :], g.x3_dram[2:T].rearrange("t p d -> p t d")).then_inc(s_x3, 16)

            for p in (0, 1):
                sp.sem_inc(s_out[p], 16)

            def store(t, p, m):
                sp.wait_ge(s_result, t + 3)
                if isinstance(t, int) and (t + 1) * P > N:
                    sp.dma_start(out[t * P:N, :], result[0:N - t * P, p, :]).then_inc(s_out[p], 16)
                else:
                    sp.dma_start(out[ds(t * P, P), :], result[:, p, :]).then_inc(s_out[p], 16)
            with sp.Fori(0, T // 2 - 1) as i:
                for p in (0, 1):
                    store(2 * i + p, p, i)
            store(T - 2, 0, T // 2 - 1)
            store(T - 1, 1, T // 2 - 1)
            for p in (0, 1):
                sp.wait_ge(s_out[p], 16 * (T // 2) + 16)

        @block.vector
        def _(dve):
            def scale_of(n, values):
                link = chain(dve, s_widest, n, 2)
                link(dve.tensor_tensor(values, values, g.exists[:], ALU.mult))
                link(dve.tensor_reduce(widest[:], values, AX, ALU.max))
                dve.wait_ge(s_level, 2 * n + 1)
                dve.tensor_reduce(top[:], ps_scale[0:1, 0:P], AX, ALU.max).then_inc(s_level, 1)
                dve.wait_ge(s_scaled, 3 * n + 1)
                dve.tensor_scalar(scales[:, n, 0:1], ps_scale[:, 0:1], 1.0 / A_MAX, 1e-12, ALU.mult, ALU.max).then_inc(s_scaled, 1)
                dve.wait_ge(s_scaled, 3 * n + 2)
                dve.reciprocal(scales[:, n, 1:2], scales[:, n, 0:1]).then_inc(s_scaled, 1)
                dve.wait_ge(s_scaled, 3 * n + 3)
                return scales[:, n, 0:1], scales[:, n, 1:2]

            scale, inv = scale_of(0, g.largest[:])

            def w_low(t, p, m):
                dve.wait_ge(s_w_high, t + 1)
                dve.tensor_tensor(w_t[:, 1, ds(t * BLOCKS, BLOCKS), :].rearrange("p b c -> p (b c)"), flat(ps_gate_up[:, p]),
                                  w_t[:, 0, ds(t * BLOCKS, BLOCKS), :].rearrange("p b c -> p (b c)").bitcast(F32), ALU.subtract).then_inc(s_w, 1)
            pipeline(dve, g.w_tiles, [(w_low, 0)])

            def low(t, p, m):
                dve.wait_ge(s_high, t + 1)
                dve.tensor_tensor(normed_t[:, p, 1].rearrange("p k c -> p (k c)"), ps_turn[:],
                                  normed_t[:, p, 0].rearrange("p k c -> p (k c)").bitcast(F32), ALU.subtract).then_inc(s_turned, 1)

            def norm(t, p, m):
                dve.wait_ge(s_x3_first if isinstance(t, int) and t < 2 else s_x3, 16)
                link = chain(dve, s_normed, t, 4)
                link(dve.tensor_scalar(normed[:, p, :], flat(x3[:, ds(t, 1), :]), g.means[:, ds(t, 1)], g.rstds[:, ds(t, 1)], ALU.subtract, ALU.mult))
                quantised(dve, link, normed[:, p, :], normed[:, p, :], inv, scale, -A_MAX - 1.0, A_MAX)

            def measure(t, p, m):
                dve.wait_ge(s_gate_up_kept, t + 1)
                for side in (0, 1):
                    ins = dve.tensor_reduce(largest[:, side, ds(t, 1)], ps_gate_up[:, p, side, 0:I], AX, ALU.max, apply_absolute_value=True)
                    ins.then_inc(s_largest, 1)
            pipeline(dve, T, [(low, 1), (norm, 0), (measure, 2)])
            dve.wait_ge(s_largest, 2 * T + 4)
            gate, up = gate_up[:, 0], gate_up[:, 1]
            link = chain(dve, s_quant, 0, 14)
            scale, inv = scale_of(1, largest[:, 0, :])
            quantised(dve, link, gate, gate, inv, scale, -A_MAX - 1.0, A_MAX)
            scale, inv = scale_of(2, largest[:, 1, :])
            quantised(dve, link, up, up, inv, scale, -A_MAX - 1.0, A_MAX)
            dve.wait_ge(s_sig, 1)
            quantised(dve, link, sig[:], sig[:], 65536.0, 1.0 / 65536.0, 0.0, S_MAX)
            link(dve.tensor_tensor(gate, gate, sig[:], ALU.mult))
            link(dve.tensor_reduce(largest[:, 0, :], gate, AX, ALU.max, apply_absolute_value=True))
            scale, inv = scale_of(3, largest[:, 0, :])
            quantised(dve, link, gate, gate, inv, scale, -A_MAX - 1.0, A_MAX)
            link2 = chain(dve, s_all, 0, 2)
            link2(dve.tensor_tensor(gate, gate, up, ALU.mult))
            link2(dve.tensor_reduce(largest[:, 0, :], gate, AX, ALU.max, apply_absolute_value=True))
            scale, inv = scale_of(4, largest[:, 0, :])

            def quantise_o(t, p, m):
                link = chain(dve, s_o, t, 3)
                value = flat(gate[:, ds(t, 1), :])
                quantised(dve, link, normed[:, p, 0:I], value, inv, scale, -A_MAX - 1.0, A_MAX)

            def o_low(t, p, m):
                dve.wait_ge(s_o_high, t + 1)
                dve.tensor_tensor(o_t[:, p, 1].rearrange("p k c -> p (k c)"), ps_turn[:, 0:KI * P],
                                  o_t[:, p, 0].rearrange("p k c -> p (k c)").bitcast(F32), ALU.subtract).then_inc(s_o_t, 1)

            def finish(t, p, m):
                dve.wait_ge(s_out[p], 16 * m + 16)
                dve.wait_ge(s_down, t + 3)
                dve.tensor_tensor(result[:, p, :], flat(ps_down[:, p]), flat(x3[:, ds(t, 1), :]), ALU.add).then_inc(s_result, 1)
            pipeline(dve, T, [(o_low, 1), (quantise_o, 0), (finish, 2)])

        @block.scalar
        def _(act):
            def w_high(t, p, m):
                act.wait_ge(s_w_turn, t + 1)
                act.activation(w_t[:, 0, ds(t * BLOCKS, BLOCKS), :].rearrange("p b c -> p (b c)"), flat(ps_gate_up[:, p]), ACT.Copy).then_inc(s_w_high, 1)
            pipeline(act, g.w_tiles, [(w_high, 0)])

            def high(t, p, m):
                act.wait_ge(s_turn, t + 1)
                act.wait_ge(s_gate_up, t + 1)
                act.activation(normed_t[:, p, 0].rearrange("p k c -> p (k c)"), ps_turn[:], ACT.Copy).then_inc(s_high, 1)

            def keep(t, p, m):
                act.wait_ge(s_gate_up, t + 3)
                act.activation(gate_up[:, :, ds(t, 1), :].rearrange("p s a i -> p s (a i)"), ps_gate_up[:, p, :, 0:I], ACT.Copy).then_inc(s_gate_up_kept, 1)
            pipeline(act, T, [(high, 1), (keep, 2)])
            act.wait_ge(s_quant, 3)
            act.activation(sig[:], gate_up[:, 0], ACT.Sigmoid).then_inc(s_sig, 1)

            def take_o(t, p, m):
                act.wait_ge(s_o_turn, t + 3)
                act.wait_ge(s_down, t + 1)
                act.activation(o_t[:, p, 0].rearrange("p k c -> p (k c)"), ps_turn[:, 0:KI * P], ACT.Copy).then_inc(s_o_high, 1)
            pipeline(act, T, [(take_o, 1)])

        @block.tensor
        def _(pe):
            def level(n):
                pe.wait_ge(s_widest, 2 * n + 2)
                pe.transpose(ps_scale[0:1, 0:P], widest[:, 0:1], g.ident[:]).then_inc(s_level, 1)
                pe.wait_ge(s_level, 2 * n + 2)
                pe.matmul(ps_scale[:, 0:1], g.ones[0:1, :], top[0:1, 0:1], start=True, stop=True).then_inc(s_scaled, 1)
            level(0)

            pe.sem_inc(s_w, 2)
            for t in range(g.w_tiles):
                p = t % 2
                pe.wait_ge(s_rows[t // (g.w_tiles // 3)], 16)
                pe.wait_ge(s_w, t + 1)
                for k in range(BLOCKS):
                    last = pe.transpose(flat(ps_gate_up[:, p])[:, k * P:(k + 1) * P], rows[:, t, k * P:(k + 1) * P], g.ident[:])
                last.then_inc(s_w_turn, 1)

            pe.sem_inc(s_turned, 1)
            pe.sem_inc(s_gate_up, 2)
            pe.sem_inc(s_largest, 4)
            pe.wait_ge(s_w, g.w_tiles + 2)

            def turn(t, p, m):
                pe.wait_ge(s_normed, 4 * t + 4)
                pe.wait_ge(s_turned, t + 1)
                for k in range(K):
                    last = pe.transpose(ps_turn[:, k * P:(k + 1) * P], normed[:, p, k * P:(k + 1) * P], g.ident[:])
                last.then_inc(s_turn, 1)

            def multiply(t, p, m):
                pe.wait_ge(s_turned, t + 2)
                pe.wait_ge(s_largest, 2 * t + 2)
                for side in (0, 1):
                    for k in range(K):
                        for n, (l, r) in enumerate(TERMS):
                            last = pe.matmul(ps_gate_up[:, p, side, 0:I], normed_t[:, p, l, k, :], weight(r, side, k), start=(k == 0 and n == 0), stop=(k == K - 1 and n == 2))
                last.then_inc(s_gate_up, 1)
            pipeline(pe, T, [(turn, 1), (multiply, 2)])
            for n in range(1, 5):
                level(n)
            pe.sem_inc(s_o_t, 1)
            pe.sem_inc(s_result, 2)
            pe.sem_inc(s_o_turn, 2)
            pe.sem_inc(s_down, 2)

            def turn_o(t, p, m):
                pe.wait_ge(s_o, 3 * t + 3)
                pe.wait_ge(s_o_t, t + 1)
                for k in range(KI):
                    last = pe.transpose(ps_turn[:, k * P:(k + 1) * P], normed[:, p, k * P:(k + 1) * P], g.ident[:])
                last.then_inc(s_o_turn, 1)

            def down(t, p, m):
                pe.wait_ge(s_o_t, t + 2)
                pe.wait_ge(s_result, t + 1)
                for k in range(KI):
                    for n, (l, r) in enumerate(TERMS):
                        for a in (0, 1):
                            blocks = HALF // P
                            last = pe.matmul(ps_down[:, p, a, :], o_t[:, p, l, k, :], down_weight(r, k)[:, a * blocks:(a + 1) * blocks, :],
                                             start=(k == 0 and n == 0), stop=(k == KI - 1 and n == 2))
                last.then_inc(s_down, 1)
            pipeline(pe, T, [(turn_o, 1), (down, 2)])


def build(nc, ins, out):
    g = Shared()
    g.N, g.D = ins["x"].shape
    g.E = ins["src"].shape[0]
    g.T, g.K = tiles(g.N), g.D // P
    g.NP = g.T * P
    g.X = ins["L0_ffn_w_gate"].shape[1]
    g.slot_tiles = (g.NP + g.X * (P - 1)) // P
    g.slot_tiles += g.slot_tiles % 2
    T, K, NP, D, S = g.T, g.K, g.NP, g.D, g.slot_tiles
    ffn_sources = [ins["L1_ffn_w_gate"], ins["L1_ffn_w_up"], ins["L1_ffn_w_down"]]
    g.I = ins["L1_ffn_w_gate"].shape[0]
    g.w_tiles = 3 * g.I // P
    with ExitStack() as ctx:
        def sb(name, shape, dt=F32, where=ctx):
            return where.enter_context(nc.sbuf_tensor(name, shape, dt))

        def dram(name, shape, dt=F32):
            return nc.dram_tensor(name, shape, dt).ap()

        g.counts_dram = dram("counts_dram", (T, P, NP))
        g.turned_dram = dram("turned_dram", (T, P, NP))
        g.x1_dram = dram("x1_dram", (T, P, D))
        g.x2_dram = dram("x2_dram", (T, P, D))
        g.x3_dram = dram("x3_dram", (T, P, D))
        g.normed_dram = dram("normed_dram", (NP, D))
        g.slot_token_dram = dram("slot_token_dram", ((S + 1) * P, 1), I32)
        g.y_dram = dram("y_dram", ((S + 2) * P, D))
        g.nodes_t_dram = [dram(f"nodes_t_dram{n}", (T, P, 2 * D)) for n in (0, 1)]
        g.w_rows_dram = dram("w_rows_dram", (P, g.w_tiles, D))
        g.col_id = sb("col_id", [P, P])
        g.row_id = sb("row_id", [P, 1])
        g.node_id = sb("node_id", [P, T])
        g.token_id = sb("token_id", [P, T], I32)
        g.exists = sb("exists", [P, T])
        g.ident = sb("ident", [P, P])
        g.before = sb("before", [P, P])
        g.ones = sb("ones", [P, P])
        g.ones_r = sb("ones_r", [P, P], F32R)
        g.eps = sb("eps", [P, 1])
        g.deg = sb("deg", [P, T])
        g.many_i = sb("many_i", [1, 1], I32)
        g.sides = sb("sides", [P, T, 2])
        g.route_p = sb("route_p", [P, T])
        g.chosen = sb("chosen", [P, T, g.X])
        g.slot = sb("slot", [P, T], I32)
        g.mean_var = sb("mean_var", [P, 2])
        g.means = sb("means", [P, T])
        g.rstds = sb("rstds", [P, T])
        g.largest = sb("largest", [P, T])
        g.always = ctx.enter_context(nc.semaphore("always"))
        with nc.cleanup_on_exit(), ExitStack() as early:
            nodes = sb("hidden", [P, T, 2, D], F32R, early)
            with ExitStack() as first:
                w = sb("w_gnn", [P, 2, K, D], F32R, first)
                graph_phase(nc, g, ins["src"], ins["dst"], ins["L0_gnn_W"], w)
                hidden_phase(nc, g, ins["x"], ins["L0_gnn_a"], w, nodes)
            attention_phase(nc, g, ins["x"], ins["L0_ffn_w_gate"], ins["L0_ffn_b_gate"], nodes)
        with ExitStack() as late:
            with nc.cleanup_on_exit():
                expert_phase(nc, g, ins["L0_ffn_W1"], ins["L0_ffn_b1"], ins["L0_ffn_W2"], ins["L0_ffn_b2"])
            w = sb("w_sage", [P, 2, K, D], F32R, late)
            nodes = sb("neighbours", [P, T, 2, D], F32R, late)
            for n in (0, 1):
                neighbour_phase(nc, g, n, ins[f"L1_gnn_W_neigh{n}"], w, nodes, ffn_sources)
                aggregate_phase(nc, g, n, ins[f"L1_gnn_W_self{n}"], ins[f"L1_gnn_b{n}"], w, nodes)
        feed_forward_phase(nc, g, out)


_INS = ["x", "src", "dst", "L0_gnn_W", "L0_gnn_a", "L0_ffn_w_gate", "L0_ffn_b_gate", "L0_ffn_W1", "L0_ffn_b1",
        "L0_ffn_W2", "L0_ffn_b2", "L1_gnn_W_self0", "L1_gnn_W_neigh0", "L1_gnn_b0", "L1_gnn_W_self1",
        "L1_gnn_W_neigh1", "L1_gnn_b1", "L1_ffn_w_gate", "L1_ffn_w_up", "L1_ffn_w_down"]


def kernel(**inputs):
    import numpy as np
    import concourse.bacc as bacc
    from concourse.bass_utils import run_bass_kernel_spmd

    nc = bacc.Bacc("TRN2", target_bir_lowering=False, num_devices=1)
    arrays, ins = {}, {}
    for name in _INS:
        a = np.ascontiguousarray(inputs[name])
        arrays[f"in_{name}"] = a
        ins[name] = nc.dram_tensor(f"in_{name}", a.shape, mybir.dt.from_np(a.dtype), kind="ExternalInput").ap()
    out = nc.dram_tensor("out", inputs["x"].shape, F32, kind="ExternalOutput").ap()
    build(nc, ins, out)
    r = run_bass_kernel_spmd(nc, [arrays], core_ids=[0])
    return r.results[0]["out"]
```
